# Optimizing a Trainium2 kernel written in Bass

```python
import numpy as np
import jax
import jax.numpy as jnp

def _softmax(x, axis=-1):
    return jax.nn.softmax(x, axis=axis)

def _gelu(x):
    return jax.nn.gelu(x, approximate=True)

def _silu(x):
    return jax.nn.silu(x)

def _sigmoid(x):
    return jax.nn.sigmoid(x)

def _layernorm(x, axis=-1, eps=1e-05):
    m = jnp.mean(x, axis=axis, keepdims=True)
    v = jnp.var(x, axis=axis, keepdims=True)
    return (x - m) / jnp.sqrt(v + eps)

def _scatter_add(tgt, idx, src, axis=0):
    return tgt.at[idx].add(src)

def _segment_sum(src, seg, n):
    return jax.ops.segment_sum(src, seg, n)
kernel_name = 'mk_hybrid_d1_jaxref_r8_981449'

def setup_inputs(seed: int=0):
    np.random.seed(seed)
    _w = jnp.asarray

    def _L0_attn_a_setup():
        import jax, jax.numpy as jnp
        import numpy as np
        D_MODEL = 128
        N_HEAD = 16
        HEAD_SIZE = D_MODEL // N_HEAD
        LAYER_ID = 12
        N_LAYER = 24
        HEAD_SIZE_DIVISOR = 8
        TM_DIM = 32
        TD_DIM = 64
        B, T = (4, 128)
        EPS = 1e-05 * HEAD_SIZE_DIVISOR ** 2

        def _wkv6(r, k, v, w, u):
            Bc, Tc, H, K = r.shape
            wdec = jnp.exp(-jnp.exp(w))

            def step(S, inp):
                r_t, k_t, v_t, wd_t = inp
                kv = k_t[:, :, :, None] * v_t[:, :, None, :]
                y = jnp.einsum('bhk,bhkj->bhj', r_t, S + u[None, :, :, None] * kv)
                S = S * wd_t[:, :, :, None] + kv
                return (S, y)
            S0 = jnp.zeros((Bc, H, K, K), r.dtype)
            xs = (jnp.swapaxes(r, 0, 1), jnp.swapaxes(k, 0, 1), jnp.swapaxes(v, 0, 1), jnp.swapaxes(wdec, 0, 1))
            _, ys = jax.lax.scan(step, S0, xs)
            return jnp.swapaxes(ys, 0, 1).reshape(Bc, Tc, H * K)
        key = jax.random.key(seed)
        ks = jax.random.split(key, 12)
        C = D_MODEL
        r0 = LAYER_ID / (N_LAYER - 1)
        r1 = 1.0 - LAYER_ID / N_LAYER
        ddd = np.arange(C, dtype=np.float64) / C
        time_maa_x = (1.0 - ddd ** r1).astype(np.float32)
        time_maa_w = (1.0 - ddd ** r1).astype(np.float32)
        time_maa_k = (1.0 - ddd ** r1).astype(np.float32)
        time_maa_v = (1.0 - (ddd ** r1 + 0.3 * r0)).astype(np.float32)
        time_maa_r = (1.0 - ddd ** (0.5 * r1)).astype(np.float32)
        time_maa_g = (1.0 - ddd ** (0.5 * r1)).astype(np.float32)
        n = np.arange(C, dtype=np.float64)
        time_decay = (-6.0 + 5.0 * (n / (C - 1)) ** (0.7 + 1.3 * r0)).astype(np.float32)
        zig = ((n + 1) % 3 - 1) * 0.1
        time_faaaa = (r0 * (1 - n / (C - 1)) + zig).astype(np.float32).reshape(N_HEAD, HEAD_SIZE)
        s = 1.0 / np.sqrt(C)
        inp = {'x': jax.random.normal(ks[0], (B, T, C), jnp.float32), 'time_maa_x': jnp.asarray(time_maa_x), 'time_maa_w': jnp.asarray(time_maa_w), 'time_maa_k': jnp.asarray(time_maa_k), 'time_maa_v': jnp.asarray(time_maa_v), 'time_maa_r': jnp.asarray(time_maa_r), 'time_maa_g': jnp.asarray(time_maa_g), 'time_maa_w1': jax.random.uniform(ks[1], (C, TM_DIM * 5), jnp.float32, -0.01, 0.01), 'time_maa_w2': jax.random.uniform(ks[2], (5, TM_DIM, C), jnp.float32, -0.01, 0.01), 'time_decay': jnp.asarray(time_decay), 'time_decay_w1': jax.random.uniform(ks[3], (C, TD_DIM), jnp.float32, -0.01, 0.01), 'time_decay_w2': jax.random.uniform(ks[4], (TD_DIM, C), jnp.float32, -0.01, 0.01), 'time_faaaa': jnp.asarray(time_faaaa), 'W_r': jax.random.normal(ks[5], (C, C), jnp.float32) * s, 'W_k': jax.random.normal(ks[6], (C, C), jnp.float32) * s, 'W_v': jax.random.normal(ks[7], (C, C), jnp.float32) * s, 'W_g': jax.random.normal(ks[8], (C, C), jnp.float32) * s, 'W_o': jax.random.normal(ks[9], (C, C), jnp.float32) * s, 'ln_gamma': jnp.ones((C,), jnp.float32), 'ln_beta': jnp.zeros((C,), jnp.float32)}
        return inp
    _L0_attn_a_in = _L0_attn_a_setup()

    def _L0_attn_b_setup():
        import math
        import jax, jax.numpy as jnp
        import numpy as np
        B, S, D, H = (2, 256, 128, 16)
        HD = D // H
        LAMBDA_MAX = 0.5
        AMP_EPS = 1e-06

        def _amp_norm(t):
            a = jax.nn.softplus(t)
            return a / jnp.sqrt(jnp.mean(a * a, axis=-1, keepdims=True) + AMP_EPS)
        key = jax.random.key(seed)
        ks = jax.random.split(key, 8)
        x = jax.random.normal(ks[0], (B, S, D), jnp.float32)
        w = lambda k, std: std * jax.random.normal(k, (D, D), jnp.float32)
        return {'x': x, 'Wq': w(ks[1], 0.02), 'Wk': w(ks[2], 0.02), 'Wv': w(ks[3], 0.02), 'Wo': w(ks[4], 0.02), 'Wqp': w(ks[5], 0.005), 'Wkp': w(ks[6], 0.005), 'lambda_raw': jnp.full((H,), float(np.arctanh(0.5)), jnp.float32)}
    _L0_attn_b_in = _L0_attn_b_setup()

    def _L0_ffn_setup():
        import jax, jax.numpy as jnp
        import numpy as np
        B, S, H, E, K = (4, 256, 128, 8, 2)
        key = jax.random.key(seed)
        k0, k1, k2, k3 = jax.random.split(key, 4)
        x = jax.random.normal(k0, (B, S, H), dtype=jnp.float32)
        router_w = jax.random.normal(k1, (E, H), dtype=jnp.float32) * np.float32(1.0 / np.sqrt(H))
        xav1 = np.float32(np.sqrt(2.0 / (2 * H + H)))
        w1 = jax.random.normal(k2, (E, 2 * H, H), dtype=jnp.float32) * xav1
        w2 = jax.random.normal(k3, (E, H, 2 * H), dtype=jnp.float32) * xav1
        return {'x': x, 'router_w': router_w, 'w1': w1, 'w2': w2}
    _L0_ffn_in = _L0_ffn_setup()
    _d = {'L0_attn_a_x': _L0_attn_a_in['x'], 'L0_attn_a_time_maa_x': _L0_attn_a_in['time_maa_x'], 'L0_attn_a_time_maa_w': _L0_attn_a_in['time_maa_w'], 'L0_attn_a_time_maa_k': _L0_attn_a_in['time_maa_k'], 'L0_attn_a_time_maa_v': _L0_attn_a_in['time_maa_v'], 'L0_attn_a_time_maa_r': _L0_attn_a_in['time_maa_r'], 'L0_attn_a_time_maa_g': _L0_attn_a_in['time_maa_g'], 'L0_attn_a_time_maa_w1': _L0_attn_a_in['time_maa_w1'], 'L0_attn_a_time_maa_w2': _L0_attn_a_in['time_maa_w2'], 'L0_attn_a_time_decay': _L0_attn_a_in['time_decay'], 'L0_attn_a_time_decay_w1': _L0_attn_a_in['time_decay_w1'], 'L0_attn_a_time_decay_w2': _L0_attn_a_in['time_decay_w2'], 'L0_attn_a_time_faaaa': _L0_attn_a_in['time_faaaa'], 'L0_attn_a_W_r': _L0_attn_a_in['W_r'], 'L0_attn_a_W_k': _L0_attn_a_in['W_k'], 'L0_attn_a_W_v': _L0_attn_a_in['W_v'], 'L0_attn_a_W_g': _L0_attn_a_in['W_g'], 'L0_attn_a_W_o': _L0_attn_a_in['W_o'], 'L0_attn_a_ln_gamma': _L0_attn_a_in['ln_gamma'], 'L0_attn_a_ln_beta': _L0_attn_a_in['ln_beta'], 'L0_attn_b_Wq': _L0_attn_b_in['Wq'], 'L0_attn_b_Wk': _L0_attn_b_in['Wk'], 'L0_attn_b_Wv': _L0_attn_b_in['Wv'], 'L0_attn_b_Wo': _L0_attn_b_in['Wo'], 'L0_attn_b_Wqp': _L0_attn_b_in['Wqp'], 'L0_attn_b_Wkp': _L0_attn_b_in['Wkp'], 'L0_attn_b_lambda_raw': _L0_attn_b_in['lambda_raw'], 'L0_ffn_router_w': _L0_ffn_in['router_w'], 'L0_ffn_w1': _L0_ffn_in['w1'], 'L0_ffn_w2': _L0_ffn_in['w2']}
    _x0 = _d['L0_attn_a_x']
    _d['L0_attn_a_x'] = jax.random.normal(jax.random.fold_in(jax.random.key(seed), 1), (8, 512, 128), dtype=_x0.dtype)
    del _x0
    return _d

def reference(L0_attn_a_x, L0_attn_a_time_maa_x, L0_attn_a_time_maa_w, L0_attn_a_time_maa_k, L0_attn_a_time_maa_v, L0_attn_a_time_maa_r, L0_attn_a_time_maa_g, L0_attn_a_time_maa_w1, L0_attn_a_time_maa_w2, L0_attn_a_time_decay, L0_attn_a_time_decay_w1, L0_attn_a_time_decay_w2, L0_attn_a_time_faaaa, L0_attn_a_W_r, L0_attn_a_W_k, L0_attn_a_W_v, L0_attn_a_W_g, L0_attn_a_W_o, L0_attn_a_ln_gamma, L0_attn_a_ln_beta, L0_attn_b_Wq, L0_attn_b_Wk, L0_attn_b_Wv, L0_attn_b_Wo, L0_attn_b_Wqp, L0_attn_b_Wkp, L0_attn_b_lambda_raw, L0_ffn_router_w, L0_ffn_w1, L0_ffn_w2):

    def _L0_attn_a_ref(x, time_maa_x, time_maa_w, time_maa_k, time_maa_v, time_maa_r, time_maa_g, time_maa_w1, time_maa_w2, time_decay, time_decay_w1, time_decay_w2, time_faaaa, W_r, W_k, W_v, W_g, W_o, ln_gamma, ln_beta):
        import jax, jax.numpy as jnp
        import numpy as np
        D_MODEL = 128
        N_HEAD = 16
        HEAD_SIZE = D_MODEL // N_HEAD
        LAYER_ID = 12
        N_LAYER = 24
        HEAD_SIZE_DIVISOR = 8
        TM_DIM = 32
        TD_DIM = 64
        B, T = (4, 128)
        EPS = 1e-05 * HEAD_SIZE_DIVISOR ** 2

        def _wkv6(r, k, v, w, u):
            Bc, Tc, H, K = r.shape
            wdec = jnp.exp(-jnp.exp(w))

            def step(S, inp):
                r_t, k_t, v_t, wd_t = inp
                kv = k_t[:, :, :, None] * v_t[:, :, None, :]
                y = jnp.einsum('bhk,bhkj->bhj', r_t, S + u[None, :, :, None] * kv)
                S = S * wd_t[:, :, :, None] + kv
                return (S, y)
            S0 = jnp.zeros((Bc, H, K, K), r.dtype)
            xs = (jnp.swapaxes(r, 0, 1), jnp.swapaxes(k, 0, 1), jnp.swapaxes(v, 0, 1), jnp.swapaxes(wdec, 0, 1))
            _, ys = jax.lax.scan(step, S0, xs)
            return jnp.swapaxes(ys, 0, 1).reshape(Bc, Tc, H * K)
        Bc, Tc, C = x.shape
        H, K = (N_HEAD, HEAD_SIZE)
        xs = jnp.pad(x, ((0, 0), (1, 0), (0, 0)))[:, :-1]
        xx = xs - x
        xxx = x + xx * time_maa_x
        m = jnp.tanh(xxx @ time_maa_w1).reshape(Bc, Tc, 5, TM_DIM)
        m = jnp.einsum('btfe,fec->fbtc', m, time_maa_w2)
        mw, mk, mv, mr, mg = (m[0], m[1], m[2], m[3], m[4])
        xw = x + xx * (time_maa_w + mw)
        xk = x + xx * (time_maa_k + mk)
        xv = x + xx * (time_maa_v + mv)
        xr = x + xx * (time_maa_r + mr)
        xg = x + xx * (time_maa_g + mg)
        r = xr @ W_r
        k = xk @ W_k
        v = xv @ W_v
        g = jax.nn.silu(xg @ W_g)
        w = time_decay + jnp.tanh(xw @ time_decay_w1) @ time_decay_w2
        y = _wkv6(r.reshape(Bc, Tc, H, K), k.reshape(Bc, Tc, H, K), v.reshape(Bc, Tc, H, K), w.reshape(Bc, Tc, H, K), time_faaaa)
        yg = y.reshape(Bc, Tc, H, K)
        mu = jnp.mean(yg, axis=-1, keepdims=True)
        var = jnp.mean((yg - mu) ** 2, axis=-1, keepdims=True)
        yn = ((yg - mu) / jnp.sqrt(var + EPS)).reshape(Bc, Tc, C)
        yn = yn * ln_gamma + ln_beta
        return yn * g @ W_o

    def _L0_attn_b_ref(x, Wq, Wk, Wv, Wo, Wqp, Wkp, lambda_raw):
        import math
        import jax, jax.numpy as jnp
        import numpy as np
        B, S, D, H = (2, 256, 128, 16)
        HD = D // H
        LAMBDA_MAX = 0.5
        AMP_EPS = 1e-06

        def _amp_norm(t):
            a = jax.nn.softplus(t)
            return a / jnp.sqrt(jnp.mean(a * a, axis=-1, keepdims=True) + AMP_EPS)
        b, s, d = x.shape
        split = lambda t: t.reshape(b, s, H, HD)
        q = split(x @ Wq)
        k = split(x @ Wk)
        v = split(x @ Wv)
        scale = 1.0 / math.sqrt(HD)
        scores_dot = jnp.einsum('bihd,bjhd->bhij', q, k) * scale
        q_amp = _amp_norm(q)
        k_amp = _amp_norm(k)
        q_phi = math.pi * jnp.tanh(split(x @ Wqp))
        k_phi = math.pi * jnp.tanh(split(x @ Wkp))
        q_cos = q_amp * jnp.cos(q_phi)
        q_sin = q_amp * jnp.sin(q_phi)
        k_cos = k_amp * jnp.cos(k_phi)
        k_sin = k_amp * jnp.sin(k_phi)
        scores_phase = (jnp.einsum('bihd,bjhd->bhij', q_cos, k_cos) + jnp.einsum('bihd,bjhd->bhij', q_sin, k_sin)) * scale
        lam = (LAMBDA_MAX * jnp.tanh(lambda_raw))[None, :, None, None]
        scores = scores_dot + lam * scores_phase
        causal = jnp.tril(jnp.ones((s, s), bool))
        scores = jnp.where(causal[None, None], scores, -jnp.inf)
        attn = jax.nn.softmax(scores, axis=-1)
        out = jnp.einsum('bhij,bjhd->bihd', attn, v).reshape(b, s, d)
        return out @ Wo

    def _L0_ffn_ref(x, router_w, w1, w2):
        import jax, jax.numpy as jnp
        import numpy as np
        B, S, H, E, K = (4, 256, 128, 8, 2)
        bsz, seq, hidden = x.shape
        n_experts = w1.shape[0]
        tokens = x.reshape(-1, hidden)
        T = tokens.shape[0]
        logits = tokens @ router_w.T
        topv, topi = jax.lax.top_k(logits, K)
        w = jax.nn.softmax(topv, axis=-1).astype(tokens.dtype)
        gate = jnp.zeros((T, n_experts), tokens.dtype).at[jnp.arange(T)[:, None], topi].add(w)
        out = jnp.zeros_like(tokens)
        for e in range(n_experts):
            h = jax.nn.gelu(tokens @ w1[e].T, approximate=False)
            y = h @ w2[e].T
            out = out + gate[:, e:e + 1] * y
        return out.reshape(bsz, seq, hidden)
    x = L0_attn_a_x
    x = x + _L0_attn_a_ref(_layernorm(x, axis=-1), L0_attn_a_time_maa_x, L0_attn_a_time_maa_w, L0_attn_a_time_maa_k, L0_attn_a_time_maa_v, L0_attn_a_time_maa_r, L0_attn_a_time_maa_g, L0_attn_a_time_maa_w1, L0_attn_a_time_maa_w2, L0_attn_a_time_decay, L0_attn_a_time_decay_w1, L0_attn_a_time_decay_w2, L0_attn_a_time_faaaa, L0_attn_a_W_r, L0_attn_a_W_k, L0_attn_a_W_v, L0_attn_a_W_g, L0_attn_a_W_o, L0_attn_a_ln_gamma, L0_attn_a_ln_beta)
    x = x + _L0_ffn_ref(_layernorm(x, axis=-1), L0_ffn_router_w, L0_ffn_w1, L0_ffn_w2)
    x = x + _L0_attn_b_ref(_layernorm(x, axis=-1), L0_attn_b_Wq, L0_attn_b_Wk, L0_attn_b_Wv, L0_attn_b_Wo, L0_attn_b_Wqp, L0_attn_b_Wkp, L0_attn_b_lambda_raw)
    x = x + _L0_ffn_ref(_layernorm(x, axis=-1), L0_ffn_router_w, L0_ffn_w1, L0_ffn_w2)
    return x

_drawn_inputs = setup_inputs


def setup_inputs(seed=0):
    import zlib

    import numpy as np

    out = dict(_drawn_inputs(seed))
    spreads = {'L0_attn_a_ln_gamma': (1.0, 0.2),
     'L0_attn_a_ln_beta': (0.0, 0.1),
     'L0_attn_b_lambda_raw': (0.5493061542510986, 0.6)}
    factors = {'L0_attn_a_time_maa_x': 5.281,
     'L0_attn_a_time_maa_w': 8.0,
     'L0_attn_a_time_maa_w1': 3.332,
     'L0_attn_a_time_maa_w2': 2.963,
     'L0_attn_a_time_decay_w1': 8.0,
     'L0_attn_a_time_decay_w2': 8.0,
     'L0_attn_b_Wq': 8.0,
     'L0_attn_b_Wk': 8.0,
     'L0_attn_b_Wv': 3.003,
     'L0_attn_b_Wo': 3.333,
     'L0_attn_b_Wqp': 8.0,
     'L0_attn_b_Wkp': 8.0}
    for name, (base, spread) in spreads.items():
        noise = np.random.default_rng([zlib.crc32(name.encode()), seed]).standard_normal(out[name].shape)
        drawn = base * np.exp(spread * noise) if base else spread * noise
        out[name] = jnp.asarray(drawn.astype(out[name].dtype))
    for name, factor in factors.items():
        out[name] = (out[name] * factor).astype(out[name].dtype)
    return out
```

```python
from contextlib import ExitStack

import numpy as np
import concourse.bass as bass
from concourse import mybir

ALU = mybir.AluOpType
ACT = mybir.ActivationFunctionType
F32 = mybir.dt.float32
F32R = mybir.dt.float32r
BF16 = mybir.dt.bfloat16
AX_X = mybir.AxisListType.X

P = 128
NB = 8
T = 512
TC = T // P
NT = NB * TC
C = 128
H = 16
HD = C // H
NE = 8
PI = float(np.nextafter(np.float32(np.pi), np.float32(0)))
LAMBDA_MAX = 0.5
AMP_EPS = 1e-6
MIX_TERMS = (0, 1, 2, 3, 4)
HC = 2
LN_EPS = 1e-5
GN_EPS = 1e-5 * 8 ** 2
LOWEST = -3e38


def constants():
    rows = np.arange(P)
    head_of_channel, head_of_column = rows // HD, rows % H
    sel = np.zeros((P, 64 + 8 * P), np.float32)
    for half in range(2):
        sel[rows, 32 * half + 16 * half + head_of_channel] = 1.0
    sel[:, 64:64 + P] = head_of_channel[:, None] == head_of_column[None, :]
    sel[:, 64 + P:64 + 2 * P] = (head_of_column[:, None] == head_of_column[None, :]) / HD
    sel[:, 64 + 2 * P:64 + 3 * P] = (head_of_channel[:, None] == head_of_channel[None, :]) / HD
    for j in range(4):
        takes = (rows[:, None] % 64 // H == j) & (head_of_column[:, None] == head_of_channel[None, :])
        sel[:, 64 + (3 + j) * P:64 + (4 + j) * P] = takes
    sel[:, 64 + 7 * P:] = np.where(rows[None, :] > rows[:, None], LOWEST / 300, 0.0)
    return {
        "selections": sel,
        "ident": np.eye(P, dtype=np.float32),
        "codes": np.tile(np.arange(NE, 0, -1, dtype=np.float32), (P, TC)),
    }


def layout(inputs):
    a = {n.removeprefix("L0_attn_a_"): np.asarray(v) for n, v in inputs.items() if n.startswith("L0_attn_a_")}
    f = {n.removeprefix("L0_ffn_"): np.asarray(v) for n, v in inputs.items() if n.startswith("L0_ffn_")}
    t = {n.removeprefix("L0_attn_b_"): np.asarray(v) for n, v in inputs.items() if n.startswith("L0_attn_b_")}
    by_column = np.arange(P).reshape(H, HD).T.reshape(P)
    lora = np.zeros((P, 5 * P), np.float32)
    for n, term in enumerate(MIX_TERMS):
        row = 32 * n if n < 4 else 0
        lora[row:row + 32, n * P:(n + 1) * P] = a["time_maa_w2"][term]
    decay2 = np.zeros((P, P), np.float32)
    decay2[0:64] = a["time_decay_w2"]
    w_v = a["W_v"][:, by_column]
    lora1 = np.concatenate([a["time_maa_w1"][:, 32 * n:32 * n + 32] for n in MIX_TERMS], axis=1)
    out = {
        "x": a["x"].reshape(NT, P, C).transpose(1, 0, 2).reshape(P, NT * C),
        "rwkv_weights": np.concatenate([
            lora1, lora, a["time_decay_w1"], decay2, a["W_k"],
            w_v[:, 0:64], w_v[:, 0:64], w_v[:, 64:], w_v[:, 64:], a["W_r"], a["W_g"][:, by_column],
            a["W_o"][by_column]], axis=1),
        "columns": np.stack([
            a["time_maa_x"], a["time_maa_w"], a["time_maa_k"], a["time_maa_v"], a["time_maa_r"],
            a["time_maa_g"], a["time_decay"], a["time_faaaa"].reshape(P),
            a["ln_gamma"][by_column], a["ln_beta"][by_column]], axis=1),
        "attn_weights": np.concatenate([t[n] for n in ("Wq", "Wk", "Wqp", "Wkp", "Wv", "Wo")], axis=1),
        "lambda_raw": np.repeat(t["lambda_raw"], HD)[:, None],
        "router": f["router_w"].T,
        "w1": f["w1"].transpose(2, 0, 1).reshape(C, NE * HC * P),
        "w2": f["w2"].reshape(NE, C, HC, P).transpose(3, 0, 2, 1).reshape(P, NE * HC * C),
    }
    return {n: np.ascontiguousarray(v) for n, v in (out | constants()).items()}


def common(nc, ctx, aps):
    def sb(name, shape):
        return ctx.enter_context(nc.sbuf_tensor(name, shape, F32))

    x, ident = sb("x_rows", [P, NT * C]), sb("identity", [P, P])
    minus_half, codes = sb("minus_half", [P, TC]), sb("expert_codes", [P, TC * NE])
    loaded = ctx.enter_context(nc.semaphore("loaded"))
    started = ctx.enter_context(nc.semaphore("started"))
    with nc.Block() as block:
        @block.sync
        def _(sp):
            for dst, src in ((x, aps["x"]), (ident, aps["ident"]), (codes, aps["codes"])):
                sp.dma_start(dst[:], src).then_inc(loaded, 16)

        @block.vector
        def _(v):
            v.wait_ge(loaded, 48)
            nc.vector.memset(minus_half[:], -0.5).then_inc(started, 1)

        @block.gpsimd
        def _(pool):
            pool.wait_ge(started, 1)
    return x, ident, minus_half, codes, started


def wait_apart(engine, semaphore, value, passed):
    engine.wait_ge(semaphore, value)
    engine.sem_inc(passed, 1)


class Steps:

    def __init__(self, engine, order, call, each):
        self.engine, self.order, self.start, self.each, self.n = engine, order, call * each, each, 0

    def __call__(self, instruction):
        self.n += 1
        instruction.then_inc(self.order, 1)
        self.engine.wait_ge(self.order, self.start + self.n)

    def done(self):
        assert self.n == self.each


class Norm:

    def __init__(self, nc, sb, sem, x, minus_half, started):
        self.nc, self.x, self.minus_half, self.started = nc, x, minus_half, started
        self.stats = sb("stats", [P, TC, 6])
        self.sums = sb("sums", [P, TC, 3])
        self.gap = sb("gap", [P, TC])
        self.gap_square = sb("gap_square", [P, TC])
        self.inner = sb("inner", [P, TC])
        self.mean = sb("mean", [P, TC])
        self.var_eps = sb("var_eps", [P, TC])
        self.rstd = sb("rstd", [P, TC])
        self.xn = sb("xn", [P, T])
        self.order = sem("norm_order")
        self.variance_ready = sem("variance_ready")
        self.rstd_ready = sem("rstd_ready")
        self.normed = sem("normed")

    def on_vector(self, v, b, wait_free=None):
        self.statistics(v, b)
        self.scale(v, b, wait_free)

    def statistics(self, v, b):
        nc, step = self.nc, Steps(v, self.order, b, 3)
        for t in range(TC):
            last = nc.vector.bn_stats(self.stats[:, t, :], self.x[:, bass.ds(b * T + t * P, P)])
        step(last)
        even, odd = self.stats[:, :, 0:3], self.stats[:, :, 3:6]
        nc.vector.tensor_tensor(self.sums[:], even, odd, ALU.add)
        step(nc.vector.tensor_tensor(self.gap[:], even[:, :, 1], odd[:, :, 1], ALU.subtract))
        nc.vector.tensor_scalar(self.mean[:], self.sums[:, :, 1], 0.5, None, ALU.mult)
        nc.vector.scalar_tensor_tensor(self.gap_square[:], self.gap[:], 0.25, self.gap[:], ALU.mult, ALU.mult)
        step(nc.vector.tensor_scalar(self.inner[:], self.sums[:, :, 2], 1.0 / C, LN_EPS, ALU.mult, ALU.add))
        nc.vector.tensor_tensor(self.var_eps[:], self.inner[:], self.gap_square[:],
                                ALU.add).then_inc(self.variance_ready, 1)
        step.done()

    def scale(self, v, b, wait_free=None):
        nc = self.nc
        v.wait_ge(self.rstd_ready, b + 1)
        if wait_free is not None:
            v.wait_ge(*wait_free)
        for t in range(TC):
            last = nc.vector.tensor_scalar(self.xn[:, t * P:(t + 1) * P], self.x[:, bass.ds(b * T + t * P, P)],
                                           self.mean[:, t:t + 1], self.rstd[:, t:t + 1], ALU.subtract, ALU.mult)
        last.then_inc(self.normed, 1)

    def on_pool(self, pool, b):
        pool.wait_ge(self.variance_ready, b + 1)
        self.nc.gpsimd.tensor_tensor(self.rstd[:], self.var_eps[:], self.minus_half[:, 0:TC],
                                     ALU.pow).then_inc(self.rstd_ready, 1)


def rwkv_phase(nc, x, ident, minus_half, started, weights, columns, selections):
    J = HD
    HALF = P // 2
    ORDER = [0, 2, 4, 6, 1, 3, 5, 7]
    PROD, BY_ACT, BY_DVE = 9, 6, 3
    STEPS = 6
    with ExitStack() as ctx:
        def sb(name, shape, dt=F32):
            return ctx.enter_context(nc.sbuf_tensor(f"rwkv_{name}", shape, dt))

        def ps(name, shape=(P, T), dt=F32):
            return ctx.enter_context(nc.psum_tensor(f"rwkv_{name}", list(shape), dt))

        def sem(name):
            return ctx.enter_context(nc.semaphore(f"rwkv_{name}"))

        W_LORA1, W_LORA2, W_DECAY1, W_DECAY2 = 0, 160, 800, 864
        W_K, W_VA, W_VB, W_R, W_G, W_O, W_ALL = 992, 1120, 1248, 1376, 1504, 1632, 1760
        w = sb("w", [P, W_ALL])
        col = sb("col", [P, 10])
        MAA_X, MAA, DECAY, U, GAMMA, BETA = 0, 1, 6, 7, 8, 9
        sel = sb("sel", [P, 64 + 3 * P])
        SUM_HEAD, MEAN_HEAD = 64, 64 + P
        spread_f32 = sb("spread_f32", [P, 4 * P])
        spread = sb("spread", [P, 4 * P], F32R)
        eps_col = sb("eps_col", [P, 1])
        norm = Norm(nc, sb, sem, x, minus_half, started)
        xT = sb("xT", [P, T + 1])
        xx = sb("xx", [P, T])
        xxx = sb("xxx", [P, T])
        lora = sb("lora", [P, T])
        lora_g = sb("lora_g", [32, T])
        mixed = sb("mixed", [P, 2, T])
        xf = sb("xf", [P, 2, T])
        decay_hidden = sb("decay_hidden", [64, T])
        exp_w = sb("exp_w", [P, T])
        tanh_g = sb("tanh_g", [P, T])
        decay = sb("decay", [P, 2, T])
        key = sb("key", [P, 2, T])
        recept = sb("recept", [P, 2, T])
        v_rows = sb("v_rows", [P, 2, T])
        v_a = sb("v_a", [P, 2, T], F32R)
        v_b = sb("v_b", [P, 2, T], F32R)
        gate = sb("gate", [P, 2, T])
        ruk = sb("ruk", [P, T])
        kv = sb("kv", [P, 2, T])
        state = sb("state", [P, J, T + 1])
        rs = sb("rs", [P, J, T])
        y = sb("y", [P, T])
        bonus = sb("bonus", [P, T])
        centred = sb("centred", [P, T])
        square = sb("square", [P, T])
        log_var = sb("log_var", [P, T])
        inv_std = sb("inv_std", [P, T])
        z = sb("z", [P, T])

        ps_t, ps_v, ps_y, ps_s = ps("ps_t"), ps("ps_v"), ps("ps_y"), ps("ps_s")
        ps_m = [ps("ps_m0"), ps("ps_m1")]
        ps_p = [ps("ps_p0"), ps("ps_p1")]

        landed, prepared = sem("landed"), sem("prepared")
        turned = sem("turned")
        xT_ready = sem("xT_ready")
        xx_ready = sem("xx_ready")
        mix_done = sem("mix_done")
        mixed_ready = sem("mixed_ready")
        xf_ready = sem("xf_ready")
        prod_done = sem("prod_done")
        act_free = sem("act_free")
        dve_free = sem("dve_free")
        decay_order = sem("decay_order")
        v_high = sem("v_high")
        tanh_g_ready = sem("tanh_g_ready")
        vj_done = sem("vj_done")
        kv_ready = sem("kv_ready")
        state_ready = sem("state_ready")
        rs_ready = sem("rs_ready")
        ruk_ready = sem("ruk_ready")
        sum_done = sem("sum_done")
        s_done = sem("s_done")
        y_order = sem("y_order")
        square_ready = sem("square_ready")
        log_order = sem("log_order")
        inv_ready = sem("inv_ready")
        added = sem("added")

        block = ctx.enter_context(nc.Block())

        @block.sync
        def _(sp):
            for dst, src in ((w, weights), (col, columns), (sel, selections[:, 0:64 + 3 * P]),
                             (spread_f32, selections[:, 64 + 3 * P:64 + 7 * P])):
                sp.dma_start(dst[:], src).then_inc(landed, 16)

        @block.tensor
        def _(pe):
            mm = nc.tensor.matmul
            pe.wait_ge(landed, 64)
            pe.wait_ge(prepared, 1)

            def turn(b):
                pe.wait_ge(norm.normed, b + 1)
                for t in range(TC):
                    last = nc.tensor.transpose(ps_t[:, t * P:(t + 1) * P], norm.xn[:, t * P:(t + 1) * P], ident[:])
                last.then_inc(turned, 1)

            def product(b, s, n, first, start, width, moving):
                out = ps_p[(n + s) % 2]
                if n == 0 and not first:
                    pe.wait_ge(act_free, b * BY_ACT)
                if n == 1 and not first:
                    pe.wait_ge(dve_free, b * BY_DVE)
                if 2 <= n <= 6:
                    pe.wait_ge(act_free, b * BY_ACT + n - 1)
                if n >= 7:
                    pe.wait_ge(dve_free, b * BY_DVE + n - 6)
                mm(out[0:width, :], w[0:moving.shape[0], start:start + width], moving, start=True,
                   stop=True).then_inc(prod_done, 1)

            def mixing(b, s, first):
                pe.wait_ge(xx_ready, (b + 1) * 2)
                product(b, s, 0, first, W_LORA1, P, xxx[:])
                product(b, s, 1, first, W_LORA1 + P, 32, xxx[:])

            def term(b, s, f, first):
                if f == 0:
                    pe.wait_ge(act_free, b * BY_ACT + 2)
                if not (first and f < 2):
                    pe.wait_ge(mixed_ready, b * 5 + f - 1)
                rows = slice(0, 32) if f == 4 else slice(0, P)
                src = lora_g if f == 4 else lora
                mm(ps_m[(f + s) % 2][:], w[rows, W_LORA2 + f * P:W_LORA2 + (f + 1) * P], src[rows, :],
                   start=True, stop=True).then_inc(mix_done, 1)

            def project(b, s, f):
                moving = xf[:, (f + s) % 2, :]
                pe.wait_ge(xf_ready, b * 5 + f + 1)
                if f == 0:
                    product(b, s, 2, False, W_DECAY1, 64, moving)
                if f == 1:
                    product(b, s, 4, False, W_K, P, moving)
                if f == 2:
                    product(b, s, 5, False, W_VA, P, moving)
                    product(b, s, 6, False, W_VB, P, moving)
                if f == 3:
                    product(b, s, 7, False, W_R, P, moving)
                if f == 4:
                    product(b, s, 8, False, W_G, P, moving)

            def decay_second(b, s):
                pe.wait_ge(act_free, b * BY_ACT + 3)
                product(b, s, 3, False, W_DECAY2, P, decay_hidden[:])

            def spread_v(b, s, n, first):
                j = ORDER[n]
                if n == 0:
                    pe.wait_ge(dve_free, b * BY_DVE + 2)
                if not (first and n == 0):
                    pe.wait_ge(kv_ready, b * J + n)
                src = v_a if j < 4 else v_b
                mm(ps_v[:], spread[:, (j % 4) * P:(j % 4 + 1) * P], src[:, s, :], start=True,
                   stop=True).then_inc(vj_done, 1)

            def sum_k(b, half, first):
                pe.wait_ge(rs_ready, b * J + 4 * half + 4)
                if half == 0 and not first:
                    pe.wait_ge(y_order, (b - 1) * STEPS + 2)
                for q in range(4):
                    last = mm(ps_y[32 * q:32 * q + 32, :], sel[:, 32 * half:32 * half + 32],
                              rs[:, 4 * half + q, :], start=(half == 0), stop=(half == 1))
                last.then_inc(sum_done, 1)

            def sum_ruk(b, first):
                pe.wait_ge(ruk_ready, b + 1)
                if not first:
                    pe.wait_ge(added, b)
                mm(ps_s[:], sel[:, SUM_HEAD:SUM_HEAD + P], ruk[:], start=True, stop=True).then_inc(s_done, 1)

            def mean(b):
                pe.wait_ge(y_order, b * STEPS + 2)
                mm(ps_s[:], sel[:, MEAN_HEAD:MEAN_HEAD + P], y[:], start=True, stop=True).then_inc(s_done, 1)

            def variance(b):
                pe.wait_ge(square_ready, b + 1)
                mm(ps_s[:], sel[:, MEAN_HEAD:MEAN_HEAD + P], square[:], start=True, stop=True).then_inc(s_done, 1)

            def output(b):
                pe.wait_ge(y_order, b * STEPS + 6)
                for t in range(TC):
                    last = mm(ps_s[:, t * P:(t + 1) * P], z[:, t * P:(t + 1) * P], w[:, W_O:W_O + P],
                              start=True, stop=True)
                last.then_inc(s_done, 1)

            def front(b, s, slot, first=False):
                if slot == 1:
                    turn(b)
                if slot == 2:
                    mixing(b, s, first)
                if 3 <= slot < 8:
                    term(b, s, slot - 3, first)
                if slot == 5:
                    decay_second(b, s)
                if slot >= 4:
                    project(b, s, slot - 4)

            def tail(b, slot):
                if slot == 1:
                    mean(b)
                if slot == 2:
                    variance(b)
                if slot == 4:
                    output(b)

            def chunk(b, s, first=False, last=False):
                spread_v(b, s, 0, first)
                for n in range(J):
                    if n + 1 < J:
                        spread_v(b, s, n + 1, first)
                    if not first:
                        tail(b - 1, n)
                    if not last:
                        front(b + 1, 1 - s, n)
                    if n == 5:
                        sum_k(b, 0, first)
                        sum_ruk(b, first)
                if not last:
                    front(b + 1, 1 - s, J)
                sum_k(b, 1, first)

            for slot in range(J + 1):
                front(0, 0, slot, first=True)
            chunk(0, 0, first=True)
            with pe.Fori(0, NB // 2 - 1) as i:
                chunk(i * 2 + 1, 1)
                chunk(i * 2 + 2, 0)
            chunk(NB - 1, 1, last=True)
            for slot in range(J):
                tail(NB - 1, slot)

        @block.scalar
        def _(act):
            fn = nc.scalar.activation
            act.wait_ge(landed, 64)

            def wait(semaphore, value):
                act.wait_ge(semaphore, value)

            def front(b, s, slot, first=False):
                p = lambda n: ps_p[(n + s) % 2]
                if slot == 1:
                    if not first:
                        wait(xf_ready, b * 5)
                    wait(turned, b + 1)
                    fn(xT[:, 1:T + 1], ps_t[:], ACT.Copy).then_inc(xT_ready, 1)
                if slot == 2:
                    wait(prod_done, b * PROD + 1)
                    fn(lora[:], p(0)[:], ACT.Tanh).then_inc(act_free, 1)
                    wait(prod_done, b * PROD + 2)
                    fn(lora_g[:], p(1)[0:32, :], ACT.Tanh).then_inc(act_free, 1)
                if slot == 4:
                    wait(prod_done, b * PROD + 3)
                    fn(decay_hidden[:], p(2)[0:64, :], ACT.Tanh).then_inc(act_free, 1)
                if slot == 5:
                    wait(prod_done, b * PROD + 4)
                    fn(exp_w[:], p(3)[:], ACT.Exp, bias=col[:, DECAY:DECAY + 1]).then_inc(act_free, 1)
                    wait(act_free, b * BY_ACT + 4)
                    fn(decay[:, s, :], exp_w[:], ACT.Exp, scale=-1.0).then_inc(decay_order, 1)
                    wait(prod_done, b * PROD + 5)
                    fn(key[:, s, :], p(4)[:], ACT.Copy).then_inc(act_free, 1)
                if slot == 6:
                    wait(prod_done, b * PROD + 6)
                    fn(v_a[:, s, :], p(5)[:], ACT.Copy)
                    fn(v_rows[0:HALF, s, :], p(5)[0:HALF, :], ACT.Copy).then_inc(v_high, 1)
                    wait(prod_done, b * PROD + 7)
                    fn(v_b[:, s, :], p(6)[:], ACT.Copy)
                    fn(v_rows[HALF:P, s, :], p(6)[HALF:P, :], ACT.Copy).then_inc(v_high, 1)
                if slot == 7:
                    wait(prod_done, b * PROD + 8)
                    fn(recept[:, s, :], p(7)[:], ACT.Copy).then_inc(act_free, 1)
                if slot == 8:
                    wait(prod_done, b * PROD + 9)
                    fn(tanh_g[:], p(8)[:], ACT.Tanh, scale=0.5).then_inc(tanh_g_ready, 1)

            def tail(b, slot):
                if slot == 1:
                    wait(y_order, b * STEPS + 3)
                    fn(square[:], centred[:], ACT.Square).then_inc(square_ready, 1)
                if slot == 2:
                    wait(s_done, b * 4 + 3)
                    fn(log_var[:], ps_s[:], ACT.Ln, bias=eps_col[:]).then_inc(log_order, 1)
                    wait(log_order, b + 1)
                    fn(inv_std[:], log_var[:], ACT.Exp, scale=-0.5).then_inc(inv_ready, 1)

            def chunk(b, s, first=False, last=False):
                for n in range(J):
                    if not first:
                        tail(b - 1, n)
                    if not last:
                        front(b + 1, 1 - s, n)
                if not last:
                    front(b + 1, 1 - s, J)

            for slot in range(J + 1):
                front(0, 0, slot, first=True)
            chunk(0, 0, first=True)
            with act.Fori(0, NB // 2 - 1) as i:
                chunk(i * 2 + 1, 1)
                chunk(i * 2 + 2, 0)
            chunk(NB - 1, 1, last=True)
            for slot in range(J):
                tail(NB - 1, slot)

        @block.gpsimd
        def _(pool):
            tt = nc.gpsimd.tensor_tensor

            def front(b, s, slot, first=False):
                if slot == 0:
                    norm.on_pool(pool, b)
                if slot >= 3 and slot < 8:
                    f = slot - 3
                    pool.wait_ge(mixed_ready, b * 5 + f + 1)
                    if not (first and f < 2):
                        done = {0: -1, 1: 0, 2: 3, 3: 5, 4: 7}[f]
                        pool.wait_ge(prod_done, b * PROD + done)
                    tt(xf[:, (f + s) % 2, :], mixed[:, (f + s) % 2, :], xT[:, 1:T + 1], ALU.add).then_inc(xf_ready, 1)

            def weigh(b, s, n, first):
                pool.wait_ge(state_ready, b * J + n + 1)
                if not first:
                    pool.wait_ge(sum_done, b * 2 - 1 if n < 4 else b * 2)
                tt(rs[:, n, :], recept[:, s, :], state[:, n, 0:T], ALU.mult).then_inc(rs_ready, 1)

            def chunk(b, s, first=False, last=False):
                for n in range(J):
                    if n == 0 and not last:
                        front(b + 1, 1 - s, 0)
                    weigh(b, s, n, first)
                    if n and not last:
                        front(b + 1, 1 - s, n)

            for slot in range(J + 1):
                front(0, 0, slot, first=True)
            chunk(0, 0, first=True)
            with pool.Fori(0, NB // 2 - 1) as i:
                chunk(i * 2 + 1, 1)
                chunk(i * 2 + 2, 0)
            chunk(NB - 1, 1, last=True)

        @block.vector
        def _(v):
            tt, ts, stt = nc.vector.tensor_tensor, nc.vector.tensor_scalar, nc.vector.scalar_tensor_tensor
            nc.vector.memset(xT[:, 0:1], 0.0)
            nc.vector.memset(state[:, :, 0:1], 0.0)
            nc.vector.memset(eps_col[:], GN_EPS)
            v.wait_ge(landed, 64)
            nc.vector.tensor_copy(spread[:], spread_f32[:]).then_inc(prepared, 1)

            def front(b, s, slot, first=False):
                p = lambda n: ps_p[(n + s) % 2]
                if slot == 0:
                    norm.statistics(v, b)
                if slot == 1:
                    norm.scale(v, b)
                if slot == 2:
                    v.wait_ge(xT_ready, b + 1)
                    tt(xx[:], xT[:, 0:T], xT[:, 1:T + 1], ALU.subtract).then_inc(xx_ready, 1)
                    v.wait_ge(xx_ready, b * 2 + 1)
                    stt(xxx[:], xx[:], col[:, MAA_X:MAA_X + 1], xT[:, 1:T + 1], ALU.mult, ALU.add).then_inc(xx_ready, 1)
                if 3 <= slot < 8:
                    f = slot - 3
                    v.wait_ge(mix_done, b * 5 + f + 1)
                    if not (first and f < 2):
                        v.wait_ge(xf_ready, b * 5 + f - 1)
                    stt(mixed[:, (f + s) % 2, :], ps_m[(f + s) % 2][:], col[:, MAA + f:MAA + f + 1], xx[:],
                        ALU.add, ALU.mult).then_inc(mixed_ready, 1)
                if slot == 7:
                    for n, part, low in ((0, v_a, slice(HALF, P)), (1, v_b, slice(0, HALF))):
                        v.wait_ge(v_high, b * 2 + n + 1)
                        tt(part[low, s, :], p(5 + n)[low, :], part[low, s, :].bitcast(F32),
                           ALU.subtract).then_inc(dve_free, 1)
                if slot == 8:
                    v.wait_ge(dve_free, b * BY_DVE + 2)
                    v.wait_ge(tanh_g_ready, b + 1)
                    stt(gate[:, s, :], tanh_g[:], 1.0, p(8)[:], ALU.add, ALU.mult).then_inc(dve_free, 1)

            def tail(b, s, slot):
                o = b * STEPS
                if slot == 0:
                    v.wait_ge(s_done, b * 4 + 1)
                    tt(bonus[:], v_rows[:, s, :], ps_s[:], ALU.mult).then_inc(y_order, 1)
                    v.wait_ge(y_order, o + 1)
                    v.wait_ge(sum_done, b * 2 + 2)
                    tt(y[:], ps_y[:], bonus[:], ALU.add).then_inc(y_order, 1)
                if slot == 1:
                    v.wait_ge(s_done, b * 4 + 2)
                    tt(centred[:], y[:], ps_s[:], ALU.subtract).then_inc(y_order, 1)
                if slot == 3:
                    v.wait_ge(inv_ready, b + 1)
                    tt(z[:], centred[:], inv_std[:], ALU.mult).then_inc(y_order, 1)
                    v.wait_ge(y_order, o + 4)
                    ts(z[:], z[:], col[:, GAMMA:GAMMA + 1], col[:, BETA:BETA + 1], ALU.mult, ALU.add).then_inc(y_order, 1)
                    v.wait_ge(y_order, o + 5)
                    stt(z[:], z[:], 0.5, gate[:, s, :], ALU.mult, ALU.mult).then_inc(y_order, 1)
                if slot == 5:
                    v.wait_ge(s_done, b * 4 + 4)
                    v.wait_ge(y_order, o + 6)
                    rows = x[:, bass.ds(b * T, T)]
                    tt(rows, rows, ps_s[:], ALU.add).then_inc(added, 1)

            def advance(b, s, n, first):
                v.wait_ge(vj_done, b * J + n + 1)
                if n == 0:
                    v.wait_ge(act_free, (b + 1) * BY_ACT)
                    v.wait_ge(decay_order, b + 1)
                tt(kv[:, n % 2, :], key[:, s, :], ps_v[:], ALU.mult).then_inc(kv_ready, 1)

            def scan(b, s, n, first):
                v.wait_ge(kv_ready, b * J + n + 1)
                if not first:
                    v.wait_ge(rs_ready, (b - 1) * J + n + 1)
                nc.vector.tensor_tensor_scan(state[:, n, 1:T + 1], decay[:, s, :], kv[:, n % 2, :], 0.0,
                                             ALU.mult, ALU.add).then_inc(state_ready, 1)

            def chunk(b, s, first=False, last=False):
                for n in range(J):
                    advance(b, s, n, first)
                    if n == 1:
                        if not first:
                            v.wait_ge(s_done, b * 4 - 3)
                        stt(ruk[:], recept[:, s, :], col[:, U:U + 1], key[:, s, :], ALU.mult,
                            ALU.mult).then_inc(ruk_ready, 1)
                    scan(b, s, n, first)
                    if not first:
                        tail(b - 1, 1 - s, n)
                    if not last:
                        front(b + 1, 1 - s, n)
                if not last:
                    front(b + 1, 1 - s, J)

            for slot in range(J + 1):
                front(0, 0, slot, first=True)
            chunk(0, 0, first=True)
            with v.Fori(0, NB // 2 - 1) as i:
                chunk(i * 2 + 1, 1)
                chunk(i * 2 + 2, 0)
            chunk(NB - 1, 1, last=True)
            for slot in range(J):
                tail(NB - 1, 1, slot)


def attention_phase(nc, x, ident, minus_half, started, weights, lambda_raw, selections):
    UH = H // 2
    FR = 24
    ROWS = 3 * FR
    PIECES = 12
    SCALE = HD ** -0.5
    WIDTH = [2 * P, 2 * P, 3 * P, 4 * P]
    PLACE = {0: (0, 4 * P), 1: (4 * P, 3 * P), 3: (7 * P, P), 2: (8 * P, 2 * P)}
    PT = 10 * P
    FRONT = ["turn", "v", "q", "k", "qp", "kp", "msq", "msk"]
    MID = ["turn", "v", "E3", "q", "k", "qp", "kp", "FT", "msq", "msk", "FW", "E0", "M1", "E1", "E2", "M0"]
    ORDERS = {
        "start": FRONT + ["M0"],
        "first": [n for n in MID if n not in ("E3", "FT", "FW")],
        "mid": MID,
        "last": [n for n in MID if n not in FRONT + ["M0"]],
        "end": ["E3", "FT", "FW"],
    }
    n_start, n_first, n_last = (len(ORDERS[k]) for k in ("start", "first", "last"))

    def turn_of(kind, b, name):
        place = ORDERS[kind].index(name)
        if kind == "start":
            return place
        if kind == "first":
            return n_start + place
        if kind == "end":
            return n_start + n_first + len(MID) * (NB - 2) + n_last + place
        return (b - 1) * len(MID) + n_start + n_first + place

    with ExitStack() as ctx:
        def sb(name, shape, dt=F32):
            return ctx.enter_context(nc.sbuf_tensor(f"attn_{name}", shape, dt))

        def ps(name, shape, dt=F32):
            return ctx.enter_context(nc.psum_tensor(f"attn_{name}", list(shape), dt))

        def sem(name):
            return ctx.enter_context(nc.semaphore(f"attn_{name}"))

        w = sb("w", [P, 6 * P])
        W_Q, W_K, W_QP, W_KP, W_V, W_O = (n * P for n in range(6))
        mean_head = sb("mean_head", [P, P])
        mask_f32 = sb("mask_f32", [P, P])
        mask = sb("mask", [P, P], BF16)
        ident_b = sb("ident_b", [P, P], BF16)
        col = sb("col", [P, 5])
        norm = Norm(nc, sb, sem, x, minus_half, started)
        xT = sb("xT", [P, T])
        value = [sb(f"value{s}", [P, 3, T]) for s in range(2)]
        parts = [sb(f"parts{s}", [P, 6, T], F32R) for s in range(2)]
        amp = [sb(f"amp{s}", [P, T]) for s in range(2)]
        phase = [sb(f"phase{s}", [P, T]) for s in range(2)]
        cosine_arg = [sb(f"cosine_arg{s}", [P, T]) for s in range(2)]
        tmp = [sb(f"tmp{s}", [P, T]) for s in range(2)]
        stack = [[sb(f"stack{s}{q}", [ROWS + 2, UH, T], F32R) for q in range(2)] for s in range(2)]
        v_ones = sb("v_ones", [P, 2, TC, H, 32])
        probs = sb("probs", [P, 2, 4, PT])
        maxima = sb("maxima", [P, TC, UH])
        neg_max = sb("neg_max", [UH, 2, T], F32R)
        o_rows = sb("o_rows", [P, T])
        inv = sb("inv", [P, TC * 4])
        o_norm = sb("o_norm", [P, TC, C])
        oT = sb("oT", [P, T])

        ps_h = [ps(f"ps_h{s}", [P, 2 * T]) for s in range(2)]
        ps_g = [ps(f"ps_g{s}", [P, T]) for s in range(2)]
        ps_o = ps("ps_o", [P, T])
        ps_f = ps("ps_f", [P, T])

        landed, prepared, lambda_ready = sem("landed"), sem("prepared"), sem("lambda_ready")
        f_done = sem("f_done")
        f_free = sem("f_free")
        act_feature = sem("act_feature")
        dve_feature = sem("dve_feature")
        pool_feature = sem("pool_feature")
        stacked = [sem("stacked0"), sem("stacked1")]
        neg_max_high = sem("neg_max_high")
        neg_max_landed = sem("neg_max_landed")
        g_done = sem("g_done")
        g_free = sem("g_free")
        h_done = sem("h_done")
        exp_done = sem("exp_done")
        masked = sem("masked")
        av_done = sem("av_done")
        o_ready = sem("o_ready")
        inv_ready = sem("inv_ready")
        pool_passed, sp_passed = sem("pool_passed"), sem("sp_passed")
        NA, NV, NP = 12, 10, 6

        block = ctx.enter_context(nc.Block())

        def stack_head(sp, unit_parity, h):
            for side in range(2):
                for a, low in enumerate(((0, 0, 1), (0, 1, 0))[side]):
                    sp.dma_start(stack[side][unit_parity][FR * a:FR * (a + 1), h % UH, :].bitcast(F32),
                                 parts[side][HD * h:HD * (h + 1), 3 * low:3 * low + 3, :].bitcast(F32)).then_inc(
                                     stacked[unit_parity], 16)

        @block.sync
        def _(sp):
            for dst, src in ((w, weights), (mean_head, selections[:, 64 + 2 * P:64 + 3 * P]),
                             (mask_f32, selections[:, 64 + 7 * P:64 + 8 * P]), (col, lambda_raw)):
                sp.dma_start(dst[:] if dst is not col else col[:, 0:1], src).then_inc(landed, 16)
            for h in range(H):
                if h == 0:
                    sp.wait_ge(dve_feature, NV)
                    sp.wait_ge(pool_feature, NP)
                stack_head(sp, h // UH, h)

            def body(b, last=False):
                if last:
                    return
                wait_apart(sp, dve_feature, (b + 2) * NV, sp_passed)
                wait_apart(sp, pool_feature, (b + 2) * NP, sp_passed)
                for q in range(2):
                    for p in range(4):
                        wait_apart(sp, h_done, (b * 2 + q) * PIECES + 3 * p + 3, sp_passed)
                        for h in (2 * p, 2 * p + 1):
                            stack_head(sp, q, q * UH + h)

            body(0)
            with sp.Fori(0, NB - 2) as i:
                body(i + 1)

        @block.tensor
        def _(pe):
            mm = nc.tensor.matmul
            pe.wait_ge(landed, 64)
            pe.wait_ge(prepared, 1)

            def use(kind, b, name):
                n = turn_of(kind, b, name)
                if not isinstance(n, int) or n > 0:
                    pe.wait_ge(f_free, n)

            def front(kind, b, name):
                use(kind, b - 1, name)
                mine = lambda other: turn_of(kind, b - 1, other) + 1
                if name == "turn":
                    pe.wait_ge(norm.normed, b + 1)
                    for t in range(TC):
                        last = nc.tensor.transpose(ps_f[:, t * P:(t + 1) * P], norm.xn[:, t * P:(t + 1) * P], ident[:])
                elif name == "v":
                    for t in range(TC):
                        last = mm(ps_f[:, t * P:(t + 1) * P], xT[:, t * P:(t + 1) * P], w[:, W_V:W_V + P],
                                  start=True, stop=True)
                elif name in ("msq", "msk"):
                    s = name == "msk"
                    pe.wait_ge(act_feature, b * NA + 5 + s)
                    last = mm(ps_f[:], mean_head[:], tmp[s][:], start=True, stop=True)
                else:
                    at = {"q": W_Q, "k": W_K, "qp": W_QP, "kp": W_KP}[name]
                    last = mm(ps_f[:], w[:, at:at + P], xT[:], start=True, stop=True)
                last.then_inc(f_done, 1)

            def scores_for_maximum(b, q, h, first):
                u = b * 2 + q
                if h == 0:
                    pe.wait_ge(stacked[q], (b + 1) * UH * 6 * 16)
                for t in range(TC):
                    n = h * TC + t
                    if not (first and n < 2):
                        pe.wait_ge(g_free, u * UH * TC + n - 1)
                    out, width = ps_g[n % 2], WIDTH[t]
                    mm(out[:, 0:width], stack[0][q][0:ROWS, h, t * P:(t + 1) * P], stack[1][q][0:ROWS, h, 0:width],
                       start=True, stop=False)
                    mm(out[:, t * P:(t + 1) * P], ident_b[:], mask[:], start=False, stop=True).then_inc(g_done, 1)

            def turn_maxima(kind, b, name, u):
                pe.wait_ge(g_free, (u + 1) * UH * TC)
                use(kind, b, name)
                for t in range(TC):
                    last = mm(ps_f[0:UH, t * P:(t + 1) * P], maxima[:, t, :], ident[:], start=True, stop=True)
                last.then_inc(f_done, 1)

            def scores(b, q, p, first):
                u = b * 2 + q
                if p == 0:
                    pe.wait_ge(neg_max_landed, (u + 1) * 32)

                def tile(out, h, j):
                    return mm(out, stack[1][q][0:ROWS + 2, h, j * P:(j + 1) * P],
                              stack[0][q][0:ROWS + 2, h, j * P:T], start=True, stop=True)

                for piece in range(3):
                    n = 3 * p + piece
                    if not (first and n < 2):
                        pe.wait_ge(exp_done, u * PIECES + n - 1)
                    out = ps_h[n % 2]
                    if piece < 2:
                        h = 2 * p + piece
                        for j in (0, 1, 3):
                            at, width = PLACE[j]
                            last = tile(out[:, at:at + width], h, j)
                    else:
                        for h in (2 * p, 2 * p + 1):
                            at = (h % 2) * 2 * P
                            last = tile(out[:, at:at + 2 * P], h, 2)
                    last.then_inc(h_done, 1)

            def weigh_values(b, s, g, first):
                pe.wait_ge(masked, b * 4 + g + 1)
                if not first or g:
                    pe.wait_ge(o_ready, b * 4 + g)
                for j in range(TC):
                    at, width = PLACE[j]
                    for hh in range(4):
                        last = mm(ps_o[32 * hh:32 * hh + 32, j * P:T], v_ones[:, s, j, 4 * g + hh, :],
                                  probs[:, g % 2, hh, at:at + width], start=(j == 0), stop=(j == TC - 1))
                last.then_inc(av_done, 1)

            def turn_output(kind, b, name, of):
                pe.wait_ge(o_ready, of)
                use(kind, b, name)
                for t in range(TC):
                    last = nc.tensor.transpose(ps_f[:, t * P:(t + 1) * P], o_rows[:, t * P:(t + 1) * P], ident[:])
                last.then_inc(f_done, 1)

            def final(kind, b, name):
                use(kind, b, name)
                for t in range(TC):
                    if name == "FT":
                        last = nc.tensor.transpose(ps_f[:, t * P:(t + 1) * P], o_norm[:, t, :], ident[:])
                    else:
                        last = mm(ps_f[:, t * P:(t + 1) * P], oT[:, t * P:(t + 1) * P], w[:, W_O:W_O + P],
                                  start=True, stop=True)
                last.then_inc(f_done, 1)

            def body(kind, b, s):
                first, last = kind == "first", kind == "last"
                for q in range(2):
                    for p in range(4):
                        scores(b, q, p, first and q == 0)
                        if q == 0 and p == 0:
                            if not last:
                                front(kind, b + 1, "turn")
                            if not first:
                                weigh_values(b - 1, 1 - s, 3, False)
                            if not last:
                                front(kind, b + 1, "v")
                        if p == 2:
                            weigh_values(b, s, 2 * q, first)
                        if q == 1 and p == 0:
                            weigh_values(b, s, 1, False)
                        if q == 0 and p == 1 and not first:
                            turn_output(kind, b, "E3", b * 4)
                        if q == 1 and p == 1:
                            turn_output(kind, b, "E1", b * 4 + 2)
                        if q == 0 and not last:
                            for name in {1: ("q", "k", "qp", "kp")}.get(p, ()):
                                front(kind, b + 1, name)
                        if p in (1, 2) and not (last and q == 1):
                            for h in range(4 * (p - 1), 4 * p):
                                scores_for_maximum(b + q, 1 - q, h, False)
                        if q == 0 and p == 2 and not first:
                            final(kind, b, "FT")
                        if q == 0 and p == 2 and not last:
                            front(kind, b + 1, "msq")
                            front(kind, b + 1, "msk")
                        if q == 0 and p == 3 and not first:
                            final(kind, b, "FW")
                        if p == 3:
                            turn_output(kind, b, "E0" if q == 0 else "E2", b * 4 + 2 * q + 1)
                            if q == 0:
                                turn_maxima(kind, b, "M1", b * 2 + 1)
                            elif not last:
                                turn_maxima(kind, b, "M0", b * 2 + 2)

            for name in FRONT:
                front("start", 0, name)
            for h in range(UH):
                scores_for_maximum(0, 0, h, True)
            turn_maxima("start", 0, "M0", 0)
            body("first", 0, 0)
            with pe.Fori(0, NB // 2 - 1) as i:
                body("mid", i * 2 + 1, 1)
                body("mid", i * 2 + 2, 0)
            body("last", NB - 1, 1)
            weigh_values(NB - 1, 1, 3, False)
            turn_output("end", 0, "E3", NB * 4)
            final("end", 0, "FT")
            final("end", 0, "FW")

        @block.scalar
        def _(act):
            fn = nc.scalar.activation
            act.wait_ge(landed, 64)
            fn(col[:, 1:2], col[:, 0:1], ACT.Tanh).then_inc(lambda_ready, 1)

            def front(kind, b, s, name):
                got = lambda other: turn_of(kind, b - 1, other) + 1
                base = b * NA
                if name in ("turn", "v", "q", "k", "qp", "kp"):
                    act.wait_ge(f_done, got(name))
                if name == "turn":
                    fn(xT[:], ps_f[:], ACT.Copy).then_inc(f_free, 1)
                elif name == "v":
                    fn(v_ones[:, s, :, :, 0:HD].rearrange("p t h d -> p (t h) d"),
                       ps_f[:].rearrange("p (n d) -> p n d", d=HD), ACT.Copy).then_inc(f_free, 1)
                elif name in ("q", "k"):
                    fn(value[name == "k"][:, 0, :], ps_f[:], ACT.Copy).then_inc(f_free, 1)
                elif name in ("qp", "kp"):
                    fn(phase[name == "kp"][:], ps_f[:], ACT.Tanh).then_inc(f_free, 1)
                elif name == "softplus":
                    for s2 in range(2):
                        act.wait_ge(dve_feature, b * NV + 1 + s2)
                        fn(tmp[s2][:], tmp[s2][:], ACT.Exp, scale=-1.0).then_inc(act_feature, 1)
                    for s2 in range(2):
                        act.wait_ge(act_feature, base + 1 + s2)
                        fn(tmp[s2][:], tmp[s2][:], ACT.Ln, bias=col[:, 2:3]).then_inc(act_feature, 1)
                    for s2 in range(2):
                        act.wait_ge(dve_feature, b * NV + 5 + s2)
                        fn(tmp[s2][:], amp[s2][:], ACT.Square).then_inc(act_feature, 1)
                elif name == "rms":
                    for s2, other in enumerate(("msq", "msk")):
                        act.wait_ge(f_done, got(other))
                        fn(tmp[s2][:], ps_f[:], ACT.Ln, bias=col[:, 3:4]).then_inc(f_free, 1)
                        act.wait_ge(f_free, got(other))
                        fn(tmp[s2][:], tmp[s2][:], ACT.Exp, scale=-0.5).then_inc(act_feature, 1)
                elif name == "circle":
                    for s2 in range(2):
                        act.wait_ge(dve_feature, b * NV + 3 + s2)
                        fn(value[s2][:, 2, :], phase[s2][:], ACT.Sin, scale=PI).then_inc(act_feature, 1)
                        fn(value[s2][:, 1, :], cosine_arg[s2][:], ACT.Sin, scale=-PI, bias=col[:, 4:5]).then_inc(act_feature, 1)

            def exponentials(b, q, p, first):
                u = b * 2 + q
                for piece in range(3):
                    n = 3 * p + piece
                    g = 2 * q + p // 2
                    if p % 2 == 0 and piece == 0 and not (first and g < 2):
                        act.wait_ge(av_done, b * 4 + g - 1)
                    act.wait_ge(h_done, u * PIECES + n + 1)
                    out = probs[:, g % 2]
                    if piece < 2:
                        fn(out[:, (2 * p + piece) % 4, 0:8 * P], ps_h[n % 2][:], ACT.Exp, scale=SCALE).then_inc(exp_done, 1)
                    else:
                        hh = (2 * p) % 4
                        fn(out[:, hh:hh + 2, 8 * P:10 * P], ps_h[n % 2][:, 0:4 * P].rearrange("p (h n) -> p h n", h=2),
                           ACT.Exp, scale=SCALE).then_inc(exp_done, 1)

            def take_output(kind, b, g, before):
                act.wait_ge(av_done, b * 4 + g + 1)
                if before is not None:
                    act.wait_ge(f_done, before + 1)
                fn(o_rows[:], ps_o[:], ACT.Copy).then_inc(o_ready, 1)

            def high_maxima(kind, b, name, u):
                act.wait_ge(f_done, turn_of(kind, b, name) + 1)
                if not isinstance(u, int) or u > 0:
                    act.wait_ge(neg_max_landed, u * 32)
                fn(neg_max[:, 0, :], ps_f[0:UH, :], ACT.Copy, scale=-1.0).then_inc(neg_max_high, 1)

            def send_maxima(kind, b, name, q):
                act.wait_ge(f_free, turn_of(kind, b, name) + 1)
                for part in range(2):
                    act.dma_start(stack[0][q][ROWS + part:ROWS + part + 1, :, :].bitcast(F32),
                                  neg_max[:, part, :].bitcast(F32)).then_inc(neg_max_landed, 16)

            def turned_copy(kind, b):
                act.wait_ge(f_done, turn_of(kind, b, "FT") + 1)
                fn(oT[:], ps_f[:], ACT.Copy).then_inc(f_free, 1)

            def body(kind, b, s):
                first, last = kind == "first", kind == "last"
                e = lambda name: turn_of(kind, b, name)
                for q in range(2):
                    for p in range(4):
                        exponentials(b, q, p, first)
                        if q == 0 and p == 0 and not last:
                            front(kind, b + 1, 1 - s, "turn")
                        if q == 0 and p == 0 and not first:
                            take_output(kind, b - 1, 3, e(ORDERS[kind][0]) - 2)
                        if q == 0 and p == 0 and not last:
                            front(kind, b + 1, 1 - s, "v")
                        if q == 0 and p == 1 and not last:
                            for name in ("q", "k", "qp", "kp", "softplus"):
                                front(kind, b + 1, 1 - s, name)
                        if q == 0 and p == 2:
                            take_output(kind, b, 0, None if first else e("E3"))
                            if not first:
                                turned_copy(kind, b)
                            if not last:
                                front(kind, b + 1, 1 - s, "rms")
                                front(kind, b + 1, 1 - s, "circle")
                        if q == 0 and p == 3:
                            high_maxima(kind, b, "M1", b * 2 + 1)
                            send_maxima(kind, b, "M1", 1)
                        if q == 1 and p == 0:
                            take_output(kind, b, 1, e("E0"))
                        if q == 1 and p == 2:
                            take_output(kind, b, 2, e("E1"))
                        if q == 1 and p == 3 and not last:
                            high_maxima(kind, b, "M0", b * 2 + 2)
                            send_maxima(kind, b, "M0", 0)

            act.wait_ge(prepared, 1)
            for name in ("turn", "v", "q", "k", "qp", "kp", "softplus", "rms", "circle"):
                front("start", 0, 0, name)
            high_maxima("start", 0, "M0", 0)
            send_maxima("start", 0, "M0", 0)
            body("first", 0, 0)
            with act.Fori(0, NB // 2 - 1) as i:
                body("mid", i * 2 + 1, 1)
                body("mid", i * 2 + 2, 0)
            body("last", NB - 1, 1)
            take_output("end", NB - 1, 3, turn_of("last", NB - 1, "E2"))
            turned_copy("end", 0)

        @block.gpsimd
        def _(pool):
            tt = nc.gpsimd.tensor_tensor

            def zero_above(b, g, q, p):
                wait_apart(pool, exp_done, (b * 2 + q) * PIECES + 3 * p + 3, pool_passed)
                for j in range(TC):
                    at = PLACE[j][0]
                    tile = probs[:, g % 2, :, at:at + P]
                    last = nc.gpsimd.affine_select(out=tile, in_=tile, compare_op=ALU.is_ge, fill=0.0, base=0,
                                                   pattern=[[0, 4], [1, P]], channel_multiplier=-1)
                last.then_inc(masked, 1)

            def features(b):
                for s in range(2):
                    pool.wait_ge(act_feature, b * NA + 10 + 2 * s)
                    pool.wait_ge(dve_feature, b * NV + 7 + s)
                    for n in (1, 2):
                        tt(value[s][:, n, :], value[s][:, n, :], amp[s][:], ALU.mult).then_inc(pool_feature, 1)
                for s in range(2):
                    pool.wait_ge(dve_feature, b * NV + 9 + s)
                    tt(parts[s][:, 3:6, :], value[s][:], parts[s][:, 0:3, :].bitcast(F32), ALU.subtract).then_inc(pool_feature, 1)

            def body(kind, b):
                for q in range(2):
                    for p in range(4):
                        if q == 0 and p == 0 and kind != "last":
                            norm.on_pool(pool, b + 1)
                        if p % 2:
                            zero_above(b, 2 * q + p // 2, q, p)
                        if q == 0 and p == 3 and kind != "last":
                            features(b + 1)

            norm.on_pool(pool, 0)
            features(0)
            body("first", 0)
            with pool.Fori(0, NB - 2) as i:
                body("mid", i + 1)
            body("last", NB - 1)

        @block.vector
        def _(v):
            tt, ts, stt = nc.vector.tensor_tensor, nc.vector.tensor_scalar, nc.vector.scalar_tensor_tensor
            v.wait_ge(landed, 64)
            v.wait_ge(lambda_ready, 1)
            for s in range(2):
                nc.vector.memset(v_ones[:, s, :, :, HD:HD + 1], 1.0)
                nc.vector.memset(v_ones[:, s, :, :, HD + 1:32], 0.0)
                nc.vector.memset(stack[1][s][64:ROWS + 2].bitcast(F32), 1.0)
            nc.vector.memset(col[:, 2:3], 1.0)
            nc.vector.memset(col[:, 3:4], AMP_EPS)
            nc.vector.memset(col[:, 4:5], PI / 2)
            ts(col[:, 0:1], col[:, 1:2], LAMBDA_MAX, None, ALU.mult)
            nc.vector.tensor_copy(mask[:], mask_f32[:])
            nc.vector.tensor_copy(ident_b[:], ident[:]).then_inc(prepared, 1)
            v.wait_ge(prepared, 1)

            def front(kind, b, step, first=False):
                got = lambda other: turn_of(kind, b - 1, other) + 1
                if step == 0:
                    norm.on_vector(v, b)
                if step == 1:
                    for s, name in enumerate(("q", "k")):
                        v.wait_ge(f_free, got(name))
                        stt(tmp[s][:], value[s][:, 0, :], -1.0, value[s][:, 0, :], ALU.mult, ALU.max).then_inc(dve_feature, 1)
                    for s, name in enumerate(("qp", "kp")):
                        v.wait_ge(f_free, got(name))
                        stt(cosine_arg[s][:], phase[s][:], -1.0, phase[s][:], ALU.mult, ALU.max).then_inc(dve_feature, 1)
                if step == 2:
                    for s in range(2):
                        v.wait_ge(act_feature, b * NA + 3 + s)
                        stt(amp[s][:], value[s][:, 0, :], 0.0, tmp[s][:], ALU.max, ALU.add).then_inc(dve_feature, 1)
                if step == 3:
                    for s in range(2):
                        v.wait_ge(act_feature, b * NA + 7 + s)
                        if s == 0:
                            stt(amp[s][:], amp[s][:], col[:, 0:1], tmp[s][:], ALU.mult, ALU.mult).then_inc(dve_feature, 1)
                        else:
                            tt(amp[s][:], amp[s][:], tmp[s][:], ALU.mult).then_inc(dve_feature, 1)
                if step == 4:
                    for s in range(2):
                        v.wait_ge(pool_feature, b * NP + 2 + 2 * s)
                        if not first and s == 0:
                            v.wait_ge(stacked[1], b * UH * 6 * 16)
                            v.wait_ge(stacked[0], b * UH * 6 * 16)
                        nc.vector.tensor_copy(parts[s][:, 0:3, :], value[s][:]).then_inc(dve_feature, 1)

            def take_maxima(b, q, h, first):
                u = b * 2 + q
                for t in range(TC):
                    n = h * TC + t
                    v.wait_ge(g_done, u * UH * TC + n + 1)
                    nc.vector.tensor_reduce(maxima[:, t, h:h + 1], ps_g[n % 2][:, 0:(t + 1) * P], AX_X,
                                            ALU.max).then_inc(g_free, 1)

            def low_maxima(kind, b, name, u):
                v.wait_ge(neg_max_high, u + 1)
                stt(neg_max[:, 1, :], ps_f[0:UH, :], -1.0, neg_max[:, 0, :].bitcast(F32), ALU.mult,
                    ALU.subtract).then_inc(f_free, 1)

            def normalise(kind, b, name, g, count):
                v.wait_ge(f_done, turn_of(kind, b, name) + 1)
                rows = ps_f[:].rearrange("p (n c) -> p n c", c=32)
                nc.vector.reciprocal(inv[:], rows[:, :, HD]).then_inc(inv_ready, 1)
                v.wait_ge(inv_ready, count + 1)
                tt(o_norm[:, :, 4 * g * HD:4 * (g + 1) * HD].rearrange("p t (h d) -> p t h d", d=HD),
                   rows[:, :, 0:HD].rearrange("p (t h) d -> p t h d", t=TC),
                   inv[:].rearrange("p (t h) -> p t h", t=TC).unsqueeze(3).broadcast_to([P, TC, 4, HD]),
                   ALU.mult).then_inc(f_free, 1)

            def add_output(kind, b, of):
                v.wait_ge(f_done, turn_of(kind, b, "FW") + 1)
                rows = x[:, bass.ds(of * T, T)]
                tt(rows, rows, ps_f[:], ALU.add).then_inc(f_free, 1)

            def body(kind, b):
                first, last = kind == "first", kind == "last"
                for q in range(2):
                    for p in range(4):
                        if q == 0 and p == 0 and not last:
                            front(kind, b + 1, 0)
                        if q == 0 and p == 1:
                            if not first:
                                normalise(kind, b, "E3", 3, b * 4 - 1)
                            if not last:
                                front(kind, b + 1, 1)
                        if p in (1, 2) and not (last and q == 1):
                            for h in range(4 * (p - 1), 4 * p):
                                take_maxima(b + q, 1 - q, h, False)
                                if q == 0 and h == 1 and not last:
                                    front(kind, b + 1, 2)
                        if q == 0 and p == 2 and not last:
                            front(kind, b + 1, 3)
                        if q == 0 and p == 3:
                            if not first:
                                add_output(kind, b, b - 1)
                            normalise(kind, b, "E0", 0, b * 4)
                            low_maxima(kind, b, "M1", b * 2 + 1)
                            if not last:
                                front(kind, b + 1, 4)
                        if q == 1 and p == 1:
                            normalise(kind, b, "E1", 1, b * 4 + 1)
                        if q == 1 and p == 3:
                            normalise(kind, b, "E2", 2, b * 4 + 2)
                            if not last:
                                low_maxima(kind, b, "M0", b * 2 + 2)

            for step in range(5):
                front("start", 0, step, first=True)
            for h in range(UH):
                take_maxima(0, 0, h, True)
            low_maxima("start", 0, "M0", 0)
            body("first", 0)
            with v.Fori(0, NB - 2) as i:
                body("mid", i + 1)
            body("last", NB - 1)
            normalise("end", 0, "E3", 3, NB * 4 - 1)
            add_output("end", 0, NB - 1)


def moe_phase(nc, phase, x, ident, minus_half, codes, started, router_w, w1, w2):
    with ExitStack() as ctx:
        def sb(name, shape, dt=F32):
            return ctx.enter_context(nc.sbuf_tensor(f"{phase}_{name}", shape, dt))

        def ps(name, shape=(P, 512), dt=F32):
            return ctx.enter_context(nc.psum_tensor(f"{phase}_{name}", list(shape), dt))

        def sem(name):
            return ctx.enter_context(nc.semaphore(f"{phase}_{name}"))

        w1_cols = sb("w1_cols", [P, NE * HC * P])
        w1_high = sb("w1_high", [P, NE * HC * P], F32R)
        w1_low = sb("w1_low", [P, NE * HC * P], F32R)
        w2_cols = sb("w2_cols", [P, NE * HC * P])
        router = sb("router", [P, NE])
        norm = Norm(nc, sb, sem, x, minus_half, started)
        xT = sb("xT", [P, 2, T])
        x_high = sb("x_high", [P, 2, T], F32R)
        x_low = sb("x_low", [P, 2, T], F32R)
        logits = sb("logits", [P, TC, NE])
        code = sb("code", [P, TC, NE])
        first = sb("first", [P, TC, NE])
        second = sb("second", [P, TC, NE])
        rest = sb("rest", [P, TC, NE])
        top = sb("top", [P, 4, TC])
        share = sb("share", [P, 4, TC])
        gate = sb("gate", [P, 2, TC, NE])
        hidden = sb("hidden", [P, 2, HC, T])

        ps_t = ps("ps_t")
        ps_logits = ps("ps_logits")
        ps_h = [[ps(f"ps_h{s}{k}") for k in range(HC)] for s in range(2)]
        ps_y = [ps(f"ps_y{s}") for s in range(2)]

        weights_landed = sem("weights_landed")
        weights_split = sem("weights_split")
        weight_order = sem("weight_order")
        gate_order = sem("gate_order")
        gate_ready = sem("gate_ready")
        transposed = sem("transposed")
        high_ready = sem("high_ready")
        low_ready = sem("low_ready")
        logits_done = sem("logits_done")
        gap_ready = sem("gap_ready")
        exp_ready = sem("exp_ready")
        hidden_done = sem("hidden_done")
        gelu_done = sem("gelu_done")
        y_done = sem("y_done")
        y_used = sem("y_used")

        block = ctx.enter_context(nc.Block())

        @block.sync
        def _(sp):
            sp.dma_start(w1_cols[:], w1).then_inc(weights_landed, 16)
            sp.dma_start(w2_cols[:], w2).then_inc(weights_landed, 16)
            sp.dma_start(router[:], router_w).then_inc(weights_landed, 16)

        @block.gpsimd
        def _(pool):
            with pool.Fori(0, NB) as b:
                norm.on_pool(pool, b)

        @block.tensor
        def _(pe):
            pe.wait_ge(weights_landed, 48)
            pe.wait_ge(weights_split, 1)

            def turn(b):
                pe.wait_ge(norm.normed, b + 1)
                for t in range(TC):
                    last = nc.tensor.transpose(ps_t[:, t * P:(t + 1) * P], norm.xn[:, t * P:(t + 1) * P], ident[:])
                last.then_inc(transposed, 1)

            def route(b, s):
                pe.wait_ge(high_ready, b + 1)
                for t in range(TC):
                    last = nc.tensor.matmul(ps_logits[:, t * NE:(t + 1) * NE], xT[:, s, t * P:(t + 1) * P],
                                            router[:], start=True, stop=True)
                last.then_inc(logits_done, 1)

            def up(b, s, e, wait_slot=True):
                if e == 0:
                    pe.wait_ge(low_ready, b + 1)
                for k in range(HC):
                    if wait_slot:
                        pe.wait_ge(gelu_done, (b * NE + e - 2) * HC + k + 1)
                    cols = slice((e * HC + k) * P, (e * HC + k + 1) * P)
                    out = ps_h[e % 2][k]
                    nc.tensor.matmul(out[:], w1_high[:, cols], x_high[:, s, :], start=True, stop=False)
                    nc.tensor.matmul(out[:], w1_high[:, cols], x_low[:, s, :], start=False, stop=False)
                    nc.tensor.matmul(out[:], w1_low[:, cols], x_high[:, s, :], start=False,
                                     stop=True).then_inc(hidden_done, 1)

            def down(b, e, wait_slot=True):
                pe.wait_ge(gelu_done, (b * NE + e + 1) * HC)
                if wait_slot:
                    pe.wait_ge(y_used, b * NE + e - 1)
                for t in range(TC):
                    for k in range(HC):
                        cols = slice((e * HC + k) * P, (e * HC + k + 1) * P)
                        last = nc.tensor.matmul(ps_y[e % 2][:, t * P:(t + 1) * P], hidden[:, e % 2, k, t * P:(t + 1) * P],
                                                w2_cols[:, cols], start=(k == 0), stop=(k == HC - 1))
                last.then_inc(y_done, 1)

            def chunk(b, s, first=False, last=False):
                for e in range(NE):
                    if e + 1 < NE:
                        up(b, s, e + 1, wait_slot=not (first and e + 1 < 2))
                    elif not last:
                        up(b + 1, 1 - s, 0)
                    down(b, e, wait_slot=not (first and e < 2))
                    if e == 4 and not last:
                        turn(b + 1)
                    if e == 5 and not last:
                        route(b + 1, 1 - s)

            turn(0)
            route(0, 0)
            up(0, 0, 0, wait_slot=False)
            chunk(0, 0, first=True)
            with pe.Fori(0, NB // 2 - 1) as i:
                chunk(i * 2 + 1, 1)
                chunk(i * 2 + 2, 0)
            chunk(NB - 1, 1, last=True)

        @block.scalar
        def _(act):
            def copies(b, s):
                act.wait_ge(transposed, b + 1)
                nc.scalar.copy(xT[:, s, :], ps_t[:])
                nc.scalar.copy(x_high[:, s, :], ps_t[:]).then_inc(high_ready, 1)

            def gap(b):
                act.wait_ge(gap_ready, b + 1)
                nc.scalar.activation(share[:, 0, :], share[:, 3, :], ACT.Exp).then_inc(exp_ready, 1)

            def gelu(b, e, wait_slot=True):
                for k in range(HC):
                    if wait_slot and k == 0:
                        act.wait_ge(y_done, b * NE + e - 1)
                    act.wait_ge(hidden_done, (b * NE + e) * HC + k + 1)
                    nc.scalar.activation(hidden[:, e % 2, k, :], ps_h[e % 2][k][:], ACT.Gelu).then_inc(gelu_done, 1)

            def chunk(b, s, first=False, last=False):
                for e in range(NE):
                    gelu(b, e, wait_slot=not (first and e < 2))
                    if e == 5 and not last:
                        copies(b + 1, 1 - s)
                    if e == 6 and not last:
                        gap(b + 1)

            copies(0, 0)
            gap(0)
            chunk(0, 0, first=True)
            with act.Fori(0, NB // 2 - 1) as i:
                chunk(i * 2 + 1, 1)
                chunk(i * 2 + 2, 0)
            chunk(NB - 1, 1, last=True)

        @block.vector
        def _(v):
            v.wait_ge(weights_landed, 48)
            nc.vector.tensor_copy(w1_high[:], w1_cols[:]).then_inc(weight_order, 1)
            v.wait_ge(weight_order, 1)
            nc.vector.tensor_tensor(w1_low[:], w1_cols[:], w1_high[:].bitcast(F32),
                                    ALU.subtract).then_inc(weights_split, 1)

            def low(b, s):
                v.wait_ge(high_ready, b + 1)
                nc.vector.tensor_tensor(x_low[:, s, :], ps_t[:], x_high[:, s, :].bitcast(F32),
                                        ALU.subtract).then_inc(low_ready, 1)

            def gates(b, s):
                step = Steps(v, gate_order, b, 16)
                wide = lambda column: column.unsqueeze(2).broadcast_to([P, TC, NE])
                tt, ts, tr = nc.vector.tensor_tensor, nc.vector.tensor_scalar, nc.vector.tensor_reduce
                v.wait_ge(logits_done, b + 1)
                step(nc.vector.tensor_copy(logits[:], ps_logits[:, 0:TC * NE]))
                step(tr(top[:, 0, :], logits[:], AX_X, ALU.max))
                for pick, value, at, left in ((first, 0, 1, logits), (second, 2, 3, rest)):
                    step(tt(pick[:], left[:], wide(top[:, value, :]), ALU.is_equal))
                    step(tt(code[:], pick[:], codes[:].rearrange("p (t e) -> p t e", t=TC), ALU.mult))
                    step(tr(top[:, at, :], code[:], AX_X, ALU.max))
                    step(tt(pick[:], code[:], wide(top[:, at, :]), ALU.is_equal))
                    if pick is first:
                        step(nc.vector.scalar_tensor_tensor(rest[:], first[:], LOWEST, logits[:], ALU.mult, ALU.add))
                        step(tr(top[:, 2, :], rest[:], AX_X, ALU.max))
                tt(share[:, 3, :], top[:, 2, :], top[:, 0, :], ALU.subtract).then_inc(gap_ready, 1)
                v.wait_ge(exp_ready, b + 1)
                step(ts(share[:, 1, :], share[:, 0, :], 1.0, None, ALU.add))
                step(nc.vector.reciprocal(share[:, 1, :], share[:, 1, :]))
                step(tt(share[:, 2, :], share[:, 0, :], share[:, 1, :], ALU.mult))
                tt(first[:], first[:], wide(share[:, 1, :]), ALU.mult)
                step(tt(second[:], second[:], wide(share[:, 2, :]), ALU.mult))
                tt(gate[:, s], first[:], second[:], ALU.add).then_inc(gate_ready, 1)
                step.done()
                v.wait_ge(gate_ready, b + 1)

            def add(b, s, e):
                v.wait_ge(y_done, b * NE + e + 1)
                if e:
                    v.wait_ge(y_used, b * NE + e)
                for t in range(TC):
                    rows = x[:, bass.ds(b * T + t * P, P)]
                    last = nc.vector.scalar_tensor_tensor(rows, ps_y[e % 2][:, t * P:(t + 1) * P],
                                                          gate[:, s, t, e:e + 1], rows, ALU.mult, ALU.add)
                last.then_inc(y_used, 1)

            def chunk(b, s, last=False):
                for e in range(NE):
                    add(b, s, e)
                    if not last:
                        if e == 2:
                            norm.on_vector(v, b + 1, (transposed, b + 1))
                        if e == 4:
                            low(b + 1, 1 - s)
                        if e == 5:
                            gates(b + 1, 1 - s)

            norm.on_vector(v, 0)
            low(0, 0)
            gates(0, 0)
            chunk(0, 0)
            with v.Fori(0, NB // 2 - 1) as i:
                chunk(i * 2 + 1, 1)
                chunk(i * 2 + 2, 0)
            chunk(NB - 1, 1, last=True)


def program(nc, aps, out):
    with ExitStack() as ctx:
        x, ident, minus_half, codes, started = common(nc, ctx, aps)
        experts = (codes, started, aps["router"], aps["w1"], aps["w2"])
        rwkv_phase(nc, x, ident, minus_half, started, aps["rwkv_weights"], aps["columns"], aps["selections"])
        moe_phase(nc, "moe0", x, ident, minus_half, *experts)
        attention_phase(nc, x, ident, minus_half, started, aps["attn_weights"], aps["lambda_raw"], aps["selections"])
        moe_phase(nc, "moe1", x, ident, minus_half, *experts)
        stored = ctx.enter_context(nc.semaphore("stored"))
        with nc.Block() as block:
            @block.sync
            def _(sp):
                sp.dma_start(out, x[:]).then_inc(stored, 16)
                sp.wait_ge(stored, 16)


def kernel(**inputs):
    import concourse.bacc as bacc
    from concourse.bass_utils import run_bass_kernel_spmd

    nc = bacc.Bacc("TRN2", target_bir_lowering=False, num_devices=1)
    arrays = layout(inputs)
    aps = {n: nc.dram_tensor(f"in_{n}", a.shape, F32, kind="ExternalInput").ap() for n, a in arrays.items()}
    out = nc.dram_tensor("out_rows", (P, NT * C), F32, kind="ExternalOutput").ap()
    program(nc, aps, out)
    got = run_bass_kernel_spmd(nc, [{f"in_{n}": a for n, a in arrays.items()}], core_ids=[0])
    rows = got.results[0]["out_rows"]
    return rows.reshape(P, NT, C).transpose(1, 0, 2).reshape(NB, T, C)
```

```python
from contextlib import ExitStack

import numpy as np
import concourse.bass as bass
from concourse import mybir

ALU = mybir.AluOpType
ACT = mybir.ActivationFunctionType
F32 = mybir.dt.float32
F32R = mybir.dt.float32r
BF16 = mybir.dt.bfloat16
AX_X = mybir.AxisListType.X

P = 128
NB = 8
T = 512
TC = T // P
NT = NB * TC
C = 128
H = 16
HD = C // H
NE = 8
PI = float(np.nextafter(np.float32(np.pi), np.float32(0)))
LAMBDA_MAX = 0.5
AMP_EPS = 1e-6
MIX_TERMS = (0, 1, 2, 3, 4)
HC = 2
LN_EPS = 1e-5
GN_EPS = 1e-5 * 8 ** 2
LOWEST = -3e38


def constants():
    rows = np.arange(P)
    head_of_channel, head_of_column = rows // HD, rows % H
    sel = np.zeros((P, 64 + 8 * P), np.float32)
    for half in range(2):
        sel[rows, 32 * half + 16 * half + head_of_channel] = 1.0
    sel[:, 64:64 + P] = head_of_channel[:, None] == head_of_column[None, :]
    sel[:, 64 + P:64 + 2 * P] = (head_of_column[:, None] == head_of_column[None, :]) / HD
    sel[:, 64 + 2 * P:64 + 3 * P] = (head_of_channel[:, None] == head_of_channel[None, :]) / HD
    for j in range(4):
        takes = (rows[:, None] % 64 // H == j) & (head_of_column[:, None] == head_of_channel[None, :])
        sel[:, 64 + (3 + j) * P:64 + (4 + j) * P] = takes
    sel[:, 64 + 7 * P:] = np.where(rows[None, :] > rows[:, None], LOWEST / 300, 0.0)
    return {
        "selections": sel,
        "ident": np.eye(P, dtype=np.float32),
        "codes": np.tile(np.arange(NE, 0, -1, dtype=np.float32), (P, TC)),
    }


def layout(inputs):
    a = {n.removeprefix("L0_attn_a_"): np.asarray(v) for n, v in inputs.items() if n.startswith("L0_attn_a_")}
    f = {n.removeprefix("L0_ffn_"): np.asarray(v) for n, v in inputs.items() if n.startswith("L0_ffn_")}
    t = {n.removeprefix("L0_attn_b_"): np.asarray(v) for n, v in inputs.items() if n.startswith("L0_attn_b_")}
    by_column = np.arange(P).reshape(H, HD).T.reshape(P)
    lora = np.zeros((P, 5 * P), np.float32)
    for n, term in enumerate(MIX_TERMS):
        row = 32 * n if n < 4 else 0
        lora[row:row + 32, n * P:(n + 1) * P] = a["time_maa_w2"][term]
    decay2 = np.zeros((P, P), np.float32)
    decay2[0:64] = a["time_decay_w2"]
    w_v = a["W_v"][:, by_column]
    lora1 = np.concatenate([a["time_maa_w1"][:, 32 * n:32 * n + 32] for n in MIX_TERMS], axis=1)
    out = {
        "x": a["x"].reshape(NT, P, C).transpose(1, 0, 2).reshape(P, NT * C),
        "rwkv_weights": np.concatenate([
            lora1, lora, a["time_decay_w1"], decay2, a["W_k"],
            w_v[:, 0:64], w_v[:, 0:64], w_v[:, 64:], w_v[:, 64:], a["W_r"], a["W_g"][:, by_column],
            a["W_o"][by_column]], axis=1),
        "columns": np.stack([
            a["time_maa_x"], a["time_maa_w"], a["time_maa_k"], a["time_maa_v"], a["time_maa_r"],
            a["time_maa_g"], a["time_decay"], a["time_faaaa"].reshape(P),
            a["ln_gamma"][by_column], a["ln_beta"][by_column]], axis=1),
        "attn_weights": np.concatenate([t[n] for n in ("Wq", "Wk", "Wqp", "Wkp", "Wv", "Wo")], axis=1),
        "lambda_raw": np.repeat(t["lambda_raw"], HD)[:, None],
        "router": f["router_w"].T,
        "w1": f["w1"].transpose(2, 0, 1).reshape(C, NE * HC * P),
        "w2": f["w2"].reshape(NE, C, HC, P).transpose(3, 0, 2, 1).reshape(P, NE * HC * C),
    }
    return {n: np.ascontiguousarray(v) for n, v in (out | constants()).items()}


def common(nc, ctx, aps):
    def sb(name, shape):
        return ctx.enter_context(nc.sbuf_tensor(name, shape, F32))

    x, ident = sb("x_rows", [P, NT * C]), sb("identity", [P, P])
    minus_half, codes = sb("minus_half", [P, TC]), sb("expert_codes", [P, TC * NE])
    loaded = ctx.enter_context(nc.semaphore("loaded"))
    started = ctx.enter_context(nc.semaphore("started"))
    with nc.Block() as block:
        @block.sync
        def _(sp):
            for dst, src in ((x, aps["x"]), (ident, aps["ident"]), (codes, aps["codes"])):
                sp.dma_start(dst[:], src).then_inc(loaded, 16)

        @block.vector
        def _(v):
            v.wait_ge(loaded, 48)
            nc.vector.memset(minus_half[:], -0.5).then_inc(started, 1)

        @block.gpsimd
        def _(pool):
            pool.wait_ge(started, 1)
    return x, ident, minus_half, codes, started


def wait_apart(engine, semaphore, value, passed):
    engine.wait_ge(semaphore, value)
    engine.sem_inc(passed, 1)


class Steps:

    def __init__(self, engine, order, call, each):
        self.engine, self.order, self.start, self.each, self.n = engine, order, call * each, each, 0

    def __call__(self, instruction):
        self.n += 1
        instruction.then_inc(self.order, 1)
        self.engine.wait_ge(self.order, self.start + self.n)

    def done(self):
        assert self.n == self.each


class Norm:

    def __init__(self, nc, sb, sem, x, minus_half, started):
        self.nc, self.x, self.minus_half, self.started = nc, x, minus_half, started
        self.stats = sb("stats", [P, TC, 6])
        self.sums = sb("sums", [P, TC, 3])
        self.gap = sb("gap", [P, TC])
        self.gap_square = sb("gap_square", [P, TC])
        self.inner = sb("inner", [P, TC])
        self.mean = sb("mean", [P, TC])
        self.var_eps = sb("var_eps", [P, TC])
        self.rstd = sb("rstd", [P, TC])
        self.xn = sb("xn", [P, T])
        self.order = sem("norm_order")
        self.variance_ready = sem("variance_ready")
        self.rstd_ready = sem("rstd_ready")
        self.normed = sem("normed")

    def on_vector(self, v, b, wait_free=None):
        self.statistics(v, b)
        self.scale(v, b, wait_free)

    def statistics(self, v, b):
        nc, step = self.nc, Steps(v, self.order, b, 3)
        for t in range(TC):
            last = nc.vector.bn_stats(self.stats[:, t, :], self.x[:, bass.ds(b * T + t * P, P)])
        step(last)
        even, odd = self.stats[:, :, 0:3], self.stats[:, :, 3:6]
        nc.vector.tensor_tensor(self.sums[:], even, odd, ALU.add)
        step(nc.vector.tensor_tensor(self.gap[:], even[:, :, 1], odd[:, :, 1], ALU.subtract))
        nc.vector.tensor_scalar(self.mean[:], self.sums[:, :, 1], 0.5, None, ALU.mult)
        nc.vector.scalar_tensor_tensor(self.gap_square[:], self.gap[:], 0.25, self.gap[:], ALU.mult, ALU.mult)
        step(nc.vector.tensor_scalar(self.inner[:], self.sums[:, :, 2], 1.0 / C, LN_EPS, ALU.mult, ALU.add))
        nc.vector.tensor_tensor(self.var_eps[:], self.inner[:], self.gap_square[:],
                                ALU.add).then_inc(self.variance_ready, 1)
        step.done()

    def scale(self, v, b, wait_free=None):
        nc = self.nc
        v.wait_ge(self.rstd_ready, b + 1)
        if wait_free is not None:
            v.wait_ge(*wait_free)
        for t in range(TC):
            last = nc.vector.tensor_scalar(self.xn[:, t * P:(t + 1) * P], self.x[:, bass.ds(b * T + t * P, P)],
                                           self.mean[:, t:t + 1], self.rstd[:, t:t + 1], ALU.subtract, ALU.mult)
        last.then_inc(self.normed, 1)

    def on_pool(self, pool, b):
        pool.wait_ge(self.variance_ready, b + 1)
        self.nc.gpsimd.tensor_tensor(self.rstd[:], self.var_eps[:], self.minus_half[:, 0:TC],
                                     ALU.pow).then_inc(self.rstd_ready, 1)


def rwkv_phase(nc, x, ident, minus_half, started, weights, columns, selections):
    J = HD
    HALF = P // 2
    ORDER = [0, 2, 4, 6, 1, 3, 5, 7]
    PROD, BY_ACT, BY_DVE = 9, 6, 3
    STEPS = 6
    with ExitStack() as ctx:
        def sb(name, shape, dt=F32):
            return ctx.enter_context(nc.sbuf_tensor(f"rwkv_{name}", shape, dt))

        def ps(name, shape=(P, T), dt=F32):
            return ctx.enter_context(nc.psum_tensor(f"rwkv_{name}", list(shape), dt))

        def sem(name):
            return ctx.enter_context(nc.semaphore(f"rwkv_{name}"))

        W_LORA1, W_LORA2, W_DECAY1, W_DECAY2 = 0, 160, 800, 864
        W_K, W_VA, W_VB, W_R, W_G, W_O, W_ALL = 992, 1120, 1248, 1376, 1504, 1632, 1760
        w = sb("w", [P, W_ALL])
        col = sb("col", [P, 10])
        MAA_X, MAA, DECAY, U, GAMMA, BETA = 0, 1, 6, 7, 8, 9
        sel = sb("sel", [P, 64 + 3 * P])
        SUM_HEAD, MEAN_HEAD = 64, 64 + P
        spread_f32 = sb("spread_f32", [P, 4 * P])
        spread = sb("spread", [P, 4 * P], F32R)
        eps_col = sb("eps_col", [P, 1])
        norm = Norm(nc, sb, sem, x, minus_half, started)
        xT = sb("xT", [P, T + 1])
        xx = sb("xx", [P, T])
        xxx = sb("xxx", [P, T])
        lora = sb("lora", [P, T])
        lora_g = sb("lora_g", [32, T])
        mixed = sb("mixed", [P, 2, T])
        xf = sb("xf", [P, 2, T])
        decay_hidden = sb("decay_hidden", [64, T])
        exp_w = sb("exp_w", [P, T])
        tanh_g = sb("tanh_g", [P, T])
        decay = sb("decay", [P, 2, T])
        key = sb("key", [P, 2, T])
        recept = sb("recept", [P, 2, T])
        v_rows = sb("v_rows", [P, 2, T])
        v_a = sb("v_a", [P, 2, T], F32R)
        v_b = sb("v_b", [P, 2, T], F32R)
        gate = sb("gate", [P, 2, T])
        ruk = sb("ruk", [P, T])
        kv = sb("kv", [P, 2, T])
        state = sb("state", [P, J, T + 1])
        rs = sb("rs", [P, J, T])
        y = sb("y", [P, T])
        bonus = sb("bonus", [P, T])
        centred = sb("centred", [P, T])
        square = sb("square", [P, T])
        log_var = sb("log_var", [P, T])
        inv_std = sb("inv_std", [P, T])
        z = sb("z", [P, T])

        ps_t, ps_v, ps_y, ps_s = ps("ps_t"), ps("ps_v"), ps("ps_y"), ps("ps_s")
        ps_m = [ps("ps_m0"), ps("ps_m1")]
        ps_p = [ps("ps_p0"), ps("ps_p1")]

        landed, prepared = sem("landed"), sem("prepared")
        turned = sem("turned")
        xT_ready = sem("xT_ready")
        xx_ready = sem("xx_ready")
        mix_done = sem("mix_done")
        mixed_ready = sem("mixed_ready")
        xf_ready = sem("xf_ready")
        prod_done = sem("prod_done")
        act_free = sem("act_free")
        dve_free = sem("dve_free")
        decay_order = sem("decay_order")
        v_high = sem("v_high")
        tanh_g_ready = sem("tanh_g_ready")
        vj_done = sem("vj_done")
        kv_ready = sem("kv_ready")
        state_ready = sem("state_ready")
        rs_ready = sem("rs_ready")
        ruk_ready = sem("ruk_ready")
        sum_done = sem("sum_done")
        s_done = sem("s_done")
        y_order = sem("y_order")
        square_ready = sem("square_ready")
        log_order = sem("log_order")
        inv_ready = sem("inv_ready")
        added = sem("added")

        block = ctx.enter_context(nc.Block())

        @block.sync
        def _(sp):
            for dst, src in ((w, weights), (col, columns), (sel, selections[:, 0:64 + 3 * P]),
                             (spread_f32, selections[:, 64 + 3 * P:64 + 7 * P])):
                sp.dma_start(dst[:], src).then_inc(landed, 16)

        @block.tensor
        def _(pe):
            mm = nc.tensor.matmul
            pe.wait_ge(landed, 64)
            pe.wait_ge(prepared, 1)

            def turn(b):
                pe.wait_ge(norm.normed, b + 1)
                for t in range(TC):
                    last = nc.tensor.transpose(ps_t[:, t * P:(t + 1) * P], norm.xn[:, t * P:(t + 1) * P], ident[:])
                last.then_inc(turned, 1)

            def product(b, s, n, first, start, width, moving):
                out = ps_p[(n + s) % 2]
                if n == 0 and not first:
                    pe.wait_ge(act_free, b * BY_ACT)
                if n == 1 and not first:
                    pe.wait_ge(dve_free, b * BY_DVE)
                if 2 <= n <= 6:
                    pe.wait_ge(act_free, b * BY_ACT + n - 1)
                if n >= 7:
                    pe.wait_ge(dve_free, b * BY_DVE + n - 6)
                mm(out[0:width, :], w[0:moving.shape[0], start:start + width], moving, start=True,
                   stop=True).then_inc(prod_done, 1)

            def mixing(b, s, first):
                pe.wait_ge(xx_ready, (b + 1) * 2)
                product(b, s, 0, first, W_LORA1, P, xxx[:])
                product(b, s, 1, first, W_LORA1 + P, 32, xxx[:])

            def term(b, s, f, first):
                if f == 0:
                    pe.wait_ge(act_free, b * BY_ACT + 2)
                if not (first and f < 2):
                    pe.wait_ge(mixed_ready, b * 5 + f - 1)
                rows = slice(0, 32) if f == 4 else slice(0, P)
                src = lora_g if f == 4 else lora
                mm(ps_m[(f + s) % 2][:], w[rows, W_LORA2 + f * P:W_LORA2 + (f + 1) * P], src[rows, :],
                   start=True, stop=True).then_inc(mix_done, 1)

            def project(b, s, f):
                moving = xf[:, (f + s) % 2, :]
                pe.wait_ge(xf_ready, b * 5 + f + 1)
                if f == 0:
                    product(b, s, 2, False, W_DECAY1, 64, moving)
                if f == 1:
                    product(b, s, 4, False, W_K, P, moving)
                if f == 2:
                    product(b, s, 5, False, W_VA, P, moving)
                    product(b, s, 6, False, W_VB, P, moving)
                if f == 3:
                    product(b, s, 7, False, W_R, P, moving)
                if f == 4:
                    product(b, s, 8, False, W_G, P, moving)

            def decay_second(b, s):
                pe.wait_ge(act_free, b * BY_ACT + 3)
                product(b, s, 3, False, W_DECAY2, P, decay_hidden[:])

            def spread_v(b, s, n, first):
                j = ORDER[n]
                if n == 0:
                    pe.wait_ge(dve_free, b * BY_DVE + 2)
                if not (first and n == 0):
                    pe.wait_ge(kv_ready, b * J + n)
                src = v_a if j < 4 else v_b
                mm(ps_v[:], spread[:, (j % 4) * P:(j % 4 + 1) * P], src[:, s, :], start=True,
                   stop=True).then_inc(vj_done, 1)

            def sum_k(b, half, first):
                pe.wait_ge(rs_ready, b * J + 4 * half + 4)
                if half == 0 and not first:
                    pe.wait_ge(y_order, (b - 1) * STEPS + 2)
                for q in range(4):
                    last = mm(ps_y[32 * q:32 * q + 32, :], sel[:, 32 * half:32 * half + 32],
                              rs[:, 4 * half + q, :], start=(half == 0), stop=(half == 1))
                last.then_inc(sum_done, 1)

            def sum_ruk(b, first):
                pe.wait_ge(ruk_ready, b + 1)
                if not first:
                    pe.wait_ge(added, b)
                mm(ps_s[:], sel[:, SUM_HEAD:SUM_HEAD + P], ruk[:], start=True, stop=True).then_inc(s_done, 1)

            def mean(b):
                pe.wait_ge(y_order, b * STEPS + 2)
                mm(ps_s[:], sel[:, MEAN_HEAD:MEAN_HEAD + P], y[:], start=True, stop=True).then_inc(s_done, 1)

            def variance(b):
                pe.wait_ge(square_ready, b + 1)
                mm(ps_s[:], sel[:, MEAN_HEAD:MEAN_HEAD + P], square[:], start=True, stop=True).then_inc(s_done, 1)

            def output(b):
                pe.wait_ge(y_order, b * STEPS + 6)
                for t in range(TC):
                    last = mm(ps_s[:, t * P:(t + 1) * P], z[:, t * P:(t + 1) * P], w[:, W_O:W_O + P],
                              start=True, stop=True)
                last.then_inc(s_done, 1)

            def front(b, s, slot, first=False):
                if slot == 1:
                    turn(b)
                if slot == 2:
                    mixing(b, s, first)
                if 3 <= slot < 8:
                    term(b, s, slot - 3, first)
                if slot == 5:
                    decay_second(b, s)
                if slot >= 4:
                    project(b, s, slot - 4)

            def tail(b, slot):
                if slot == 1:
                    mean(b)
                if slot == 2:
                    variance(b)
                if slot == 4:
                    output(b)

            def chunk(b, s, first=False, last=False):
                spread_v(b, s, 0, first)
                for n in range(J):
                    if n + 1 < J:
                        spread_v(b, s, n + 1, first)
                    if not first:
                        tail(b - 1, n)
                    if not last:
                        front(b + 1, 1 - s, n)
                    if n == 5:
                        sum_k(b, 0, first)
                        sum_ruk(b, first)
                if not last:
                    front(b + 1, 1 - s, J)
                sum_k(b, 1, first)

            for slot in range(J + 1):
                front(0, 0, slot, first=True)
            chunk(0, 0, first=True)
            with pe.Fori(0, NB // 2 - 1) as i:
                chunk(i * 2 + 1, 1)
                chunk(i * 2 + 2, 0)
            chunk(NB - 1, 1, last=True)
            for slot in range(J):
                tail(NB - 1, slot)

        @block.scalar
        def _(act):
            fn = nc.scalar.activation
            act.wait_ge(landed, 64)

            def wait(semaphore, value):
                act.wait_ge(semaphore, value)

            def front(b, s, slot, first=False):
                p = lambda n: ps_p[(n + s) % 2]
                if slot == 1:
                    if not first:
                        wait(xf_ready, b * 5)
                    wait(turned, b + 1)
                    fn(xT[:, 1:T + 1], ps_t[:], ACT.Copy).then_inc(xT_ready, 1)
                if slot == 2:
                    wait(prod_done, b * PROD + 1)
                    fn(lora[:], p(0)[:], ACT.Tanh).then_inc(act_free, 1)
                    wait(prod_done, b * PROD + 2)
                    fn(lora_g[:], p(1)[0:32, :], ACT.Tanh).then_inc(act_free, 1)
                if slot == 4:
                    wait(prod_done, b * PROD + 3)
                    fn(decay_hidden[:], p(2)[0:64, :], ACT.Tanh).then_inc(act_free, 1)
                if slot == 5:
                    wait(prod_done, b * PROD + 4)
                    fn(exp_w[:], p(3)[:], ACT.Exp, bias=col[:, DECAY:DECAY + 1]).then_inc(act_free, 1)
                    wait(act_free, b * BY_ACT + 4)
                    fn(decay[:, s, :], exp_w[:], ACT.Exp, scale=-1.0).then_inc(decay_order, 1)
                    wait(prod_done, b * PROD + 5)
                    fn(key[:, s, :], p(4)[:], ACT.Copy).then_inc(act_free, 1)
                if slot == 6:
                    wait(prod_done, b * PROD + 6)
                    fn(v_a[:, s, :], p(5)[:], ACT.Copy)
                    fn(v_rows[0:HALF, s, :], p(5)[0:HALF, :], ACT.Copy).then_inc(v_high, 1)
                    wait(prod_done, b * PROD + 7)
                    fn(v_b[:, s, :], p(6)[:], ACT.Copy)
                    fn(v_rows[HALF:P, s, :], p(6)[HALF:P, :], ACT.Copy).then_inc(v_high, 1)
                if slot == 7:
                    wait(prod_done, b * PROD + 8)
                    fn(recept[:, s, :], p(7)[:], ACT.Copy).then_inc(act_free, 1)
                if slot == 8:
                    wait(prod_done, b * PROD + 9)
                    fn(tanh_g[:], p(8)[:], ACT.Tanh, scale=0.5).then_inc(tanh_g_ready, 1)

            def tail(b, slot):
                if slot == 1:
                    wait(y_order, b * STEPS + 3)
                    fn(square[:], centred[:], ACT.Square).then_inc(square_ready, 1)
                if slot == 2:
                    wait(s_done, b * 4 + 3)
                    fn(log_var[:], ps_s[:], ACT.Ln, bias=eps_col[:]).then_inc(log_order, 1)
                    wait(log_order, b + 1)
                    fn(inv_std[:], log_var[:], ACT.Exp, scale=-0.5).then_inc(inv_ready, 1)

            def chunk(b, s, first=False, last=False):
                for n in range(J):
                    if not first:
                        tail(b - 1, n)
                    if not last:
                        front(b + 1, 1 - s, n)
                if not last:
                    front(b + 1, 1 - s, J)

            for slot in range(J + 1):
                front(0, 0, slot, first=True)
            chunk(0, 0, first=True)
            with act.Fori(0, NB // 2 - 1) as i:
                chunk(i * 2 + 1, 1)
                chunk(i * 2 + 2, 0)
            chunk(NB - 1, 1, last=True)
            for slot in range(J):
                tail(NB - 1, slot)

        @block.gpsimd
        def _(pool):
            tt = nc.gpsimd.tensor_tensor

            def front(b, s, slot, first=False):
                if slot == 0:
                    norm.on_pool(pool, b)
                if slot >= 3 and slot < 8:
                    f = slot - 3
                    pool.wait_ge(mixed_ready, b * 5 + f + 1)
                    if not (first and f < 2):
                        done = {0: -1, 1: 0, 2: 3, 3: 5, 4: 7}[f]
                        pool.wait_ge(prod_done, b * PROD + done)
                    tt(xf[:, (f + s) % 2, :], mixed[:, (f + s) % 2, :], xT[:, 1:T + 1], ALU.add).then_inc(xf_ready, 1)

            def weigh(b, s, n, first):
                pool.wait_ge(state_ready, b * J + n + 1)
                if not first:
                    pool.wait_ge(sum_done, b * 2 - 1 if n < 4 else b * 2)
                tt(rs[:, n, :], recept[:, s, :], state[:, n, 0:T], ALU.mult).then_inc(rs_ready, 1)

            def chunk(b, s, first=False, last=False):
                for n in range(J):
                    if n == 0 and not last:
                        front(b + 1, 1 - s, 0)
                    weigh(b, s, n, first)
                    if n and not last:
                        front(b + 1, 1 - s, n)

            for slot in range(J + 1):
                front(0, 0, slot, first=True)
            chunk(0, 0, first=True)
            with pool.Fori(0, NB // 2 - 1) as i:
                chunk(i * 2 + 1, 1)
                chunk(i * 2 + 2, 0)
            chunk(NB - 1, 1, last=True)

        @block.vector
        def _(v):
            tt, ts, stt = nc.vector.tensor_tensor, nc.vector.tensor_scalar, nc.vector.scalar_tensor_tensor
            nc.vector.memset(xT[:, 0:1], 0.0)
            nc.vector.memset(state[:, :, 0:1], 0.0)
            nc.vector.memset(eps_col[:], GN_EPS)
            v.wait_ge(landed, 64)
            nc.vector.tensor_copy(spread[:], spread_f32[:]).then_inc(prepared, 1)

            def front(b, s, slot, first=False):
                p = lambda n: ps_p[(n + s) % 2]
                if slot == 0:
                    norm.statistics(v, b)
                if slot == 1:
                    norm.scale(v, b)
                if slot == 2:
                    v.wait_ge(xT_ready, b + 1)
                    tt(xx[:], xT[:, 0:T], xT[:, 1:T + 1], ALU.subtract).then_inc(xx_ready, 1)
                    v.wait_ge(xx_ready, b * 2 + 1)
                    stt(xxx[:], xx[:], col[:, MAA_X:MAA_X + 1], xT[:, 1:T + 1], ALU.mult, ALU.add).then_inc(xx_ready, 1)
                if 3 <= slot < 8:
                    f = slot - 3
                    v.wait_ge(mix_done, b * 5 + f + 1)
                    if not (first and f < 2):
                        v.wait_ge(xf_ready, b * 5 + f - 1)
                    stt(mixed[:, (f + s) % 2, :], ps_m[(f + s) % 2][:], col[:, MAA + f:MAA + f + 1], xx[:],
                        ALU.add, ALU.mult).then_inc(mixed_ready, 1)
                if slot == 7:
                    for n, part, low in ((0, v_a, slice(HALF, P)), (1, v_b, slice(0, HALF))):
                        v.wait_ge(v_high, b * 2 + n + 1)
                        tt(part[low, s, :], p(5 + n)[low, :], part[low, s, :].bitcast(F32),
                           ALU.subtract).then_inc(dve_free, 1)
                if slot == 8:
                    v.wait_ge(dve_free, b * BY_DVE + 2)
                    v.wait_ge(tanh_g_ready, b + 1)
                    stt(gate[:, s, :], tanh_g[:], 1.0, p(8)[:], ALU.add, ALU.mult).then_inc(dve_free, 1)

            def tail(b, s, slot):
                o = b * STEPS
                if slot == 0:
                    v.wait_ge(s_done, b * 4 + 1)
                    tt(bonus[:], v_rows[:, s, :], ps_s[:], ALU.mult).then_inc(y_order, 1)
                    v.wait_ge(y_order, o + 1)
                    v.wait_ge(sum_done, b * 2 + 2)
                    tt(y[:], ps_y[:], bonus[:], ALU.add).then_inc(y_order, 1)
                if slot == 1:
                    v.wait_ge(s_done, b * 4 + 2)
                    tt(centred[:], y[:], ps_s[:], ALU.subtract).then_inc(y_order, 1)
                if slot == 3:
                    v.wait_ge(inv_ready, b + 1)
                    tt(z[:], centred[:], inv_std[:], ALU.mult).then_inc(y_order, 1)
                    v.wait_ge(y_order, o + 4)
                    ts(z[:], z[:], col[:, GAMMA:GAMMA + 1], col[:, BETA:BETA + 1], ALU.mult, ALU.add).then_inc(y_order, 1)
                    v.wait_ge(y_order, o + 5)
                    stt(z[:], z[:], 0.5, gate[:, s, :], ALU.mult, ALU.mult).then_inc(y_order, 1)
                if slot == 5:
                    v.wait_ge(s_done, b * 4 + 4)
                    v.wait_ge(y_order, o + 6)
                    rows = x[:, bass.ds(b * T, T)]
                    tt(rows, rows, ps_s[:], ALU.add).then_inc(added, 1)

            def advance(b, s, n, first):
                v.wait_ge(vj_done, b * J + n + 1)
                if n == 0:
                    v.wait_ge(act_free, (b + 1) * BY_ACT)
                    v.wait_ge(decay_order, b + 1)
                tt(kv[:, n % 2, :], key[:, s, :], ps_v[:], ALU.mult).then_inc(kv_ready, 1)

            def scan(b, s, n, first):
                v.wait_ge(kv_ready, b * J + n + 1)
                if not first:
                    v.wait_ge(rs_ready, (b - 1) * J + n + 1)
                nc.vector.tensor_tensor_scan(state[:, n, 1:T + 1], decay[:, s, :], kv[:, n % 2, :], 0.0,
                                             ALU.mult, ALU.add).then_inc(state_ready, 1)

            def chunk(b, s, first=False, last=False):
                for n in range(J):
                    advance(b, s, n, first)
                    if n == 1:
                        if not first:
                            v.wait_ge(s_done, b * 4 - 3)
                        stt(ruk[:], recept[:, s, :], col[:, U:U + 1], key[:, s, :], ALU.mult,
                            ALU.mult).then_inc(ruk_ready, 1)
                    scan(b, s, n, first)
                    if not first:
                        tail(b - 1, 1 - s, n)
                    if not last:
                        front(b + 1, 1 - s, n)
                if not last:
                    front(b + 1, 1 - s, J)

            for slot in range(J + 1):
                front(0, 0, slot, first=True)
            chunk(0, 0, first=True)
            with v.Fori(0, NB // 2 - 1) as i:
                chunk(i * 2 + 1, 1)
                chunk(i * 2 + 2, 0)
            chunk(NB - 1, 1, last=True)
            for slot in range(J):
                tail(NB - 1, 1, slot)


def attention_phase(nc, x, ident, minus_half, started, weights, lambda_raw, selections):
    UH = H // 2
    FR = 24
    ROWS = 3 * FR
    PIECES = 12
    SCALE = HD ** -0.5
    WIDTH = [2 * P, 2 * P, 3 * P, 4 * P]
    PLACE = {0: (0, 4 * P), 1: (4 * P, 3 * P), 3: (7 * P, P), 2: (8 * P, 2 * P)}
    PT = 10 * P
    FRONT = ["turn", "q", "k", "qp", "kp", "msq", "msk"]
    NEXT = ["v", "M0a"]
    BEFORE = ["E3", "FT", "FW"]
    MID = ["v", "M0b", "E3", "FT", "M1a", "FW", "E0", "turn", "q", "M1b", "k", "qp", "E1", "kp",
           "M0a", "E2", "msq", "msk"]
    ORDERS = {
        "start": FRONT[:5] + ["v"] + FRONT[5:],
        "start1": FRONT,
        "start2": ["M0a"],
        "first": [n for n in MID if n not in BEFORE],
        "mid": MID,
        "late": [n for n in MID if n not in FRONT],
        "last": [n for n in MID if n not in FRONT + NEXT],
        "end": BEFORE,
    }
    n_of = {kind: len(order) for kind, order in ORDERS.items()}
    n_begin = n_of["start"] + n_of["start1"] + n_of["start2"]

    def turn_of(kind, b, name):
        place = ORDERS[kind].index(name)
        if kind in ("start", "start1", "start2"):
            return place + {"start": 0, "start1": n_of["start"], "start2": n_of["start"] + n_of["start1"]}[kind]
        if kind == "first":
            return n_begin + place
        if kind in ("mid", "late"):
            return (b - 1) * len(MID) + n_begin + n_of["first"] + place
        before_last = n_begin + n_of["first"] + (NB - 3) * len(MID) + n_of["late"]
        return before_last + place + (n_of["last"] if kind == "end" else 0)

    with ExitStack() as ctx:
        def sb(name, shape, dt=F32):
            return ctx.enter_context(nc.sbuf_tensor(f"attn_{name}", shape, dt))

        def ps(name, shape, dt=F32):
            return ctx.enter_context(nc.psum_tensor(f"attn_{name}", list(shape), dt))

        def sem(name):
            return ctx.enter_context(nc.semaphore(f"attn_{name}"))

        scratch = [[nc.dram_tensor(f"attn_scratch{s}{side}", (6, HD, H, T), F32, kind="Internal").ap()
                    for side in range(2)] for s in range(2)]
        w = sb("w", [P, 6 * P])
        W_Q, W_K, W_QP, W_KP, W_V, W_O = (n * P for n in range(6))
        mean_head = sb("mean_head", [P, P])
        mask_f32 = sb("mask_f32", [P, P])
        mask = sb("mask", [P, P], BF16)
        ident_b = sb("ident_b", [P, P], BF16)
        col = sb("col", [P, 5])
        norm = Norm(nc, sb, sem, x, minus_half, started)
        xT = sb("xT", [P, T])
        value = [sb(f"value{s}", [P, 3, T]) for s in range(2)]
        parts = [sb(f"parts{s}", [P, 6, T], F32R) for s in range(2)]
        amp = [sb(f"amp{s}", [P, T]) for s in range(2)]
        tmp = [sb(f"tmp{s}", [P, T]) for s in range(2)]
        stack = [[sb(f"stack{s}{q}", [ROWS + 2, UH, T], F32R) for q in range(2)] for s in range(2)]
        v_ones = sb("v_ones", [P, 2, TC, H, 32])
        probs = sb("probs", [P, 2, 4, PT])
        maxima = sb("maxima", [P, TC, UH])
        neg_max = [sb(f"neg_max{half}", [4, 2, T], F32R) for half in range(2)]
        o_rows = sb("o_rows", [P, T])
        inv = sb("inv", [P, TC * 4])
        o_norm = sb("o_norm", [P, TC, C])
        oT = sb("oT", [P, T])

        ps_h = [ps(f"ps_h{s}", [P, 2 * T]) for s in range(2)]
        ps_g = [ps(f"ps_g{s}", [P, T]) for s in range(2)]
        ps_o = ps("ps_o", [P, T])
        ps_f = ps("ps_f", [P, T])

        landed, prepared, lambda_ready = sem("landed"), sem("prepared"), sem("lambda_ready")
        f_done = sem("f_done")
        f_free = sem("f_free")
        act_feature = sem("act_feature")
        dve_feature = sem("dve_feature")
        pool_feature = sem("pool_feature")
        kept = sem("kept")
        stacked = [[sem(f"stacked{q}{half}") for half in range(2)] for q in range(2)]
        neg_max_high = sem("neg_max_high")
        neg_max_landed = [sem("neg_max_landed0"), sem("neg_max_landed1")]
        g_done = sem("g_done")
        g_free = sem("g_free")
        h_done = sem("h_done")
        exp_done = sem("exp_done")
        masked = sem("masked")
        av_done = sem("av_done")
        o_ready = sem("o_ready")
        inv_ready = sem("inv_ready")
        pool_passed, sp_passed = sem("pool_passed"), sem("sp_passed")
        NA, NV, NP = 14, 10, 8
        KEPT = 12 * 16
        STACK = 6 * 16

        block = ctx.enter_context(nc.Block())

        def keep_parts(sp, s):
            for side in range(2):
                for part in range(6):
                    sp.dma_start(scratch[s][side][part].rearrange("d h t -> h d t"),
                                 parts[side][:, part, :].bitcast(F32)).then_inc(kept, 16)

        def stack_heads(sp, s, q, half):
            for side in range(2):
                for a, low in enumerate(((0, 0, 1), (0, 1, 0))[side]):
                    sp.dma_start(stack[side][q][FR * a:FR * (a + 1), 4 * half:4 * half + 4, :].bitcast(F32),
                                 scratch[s][side].rearrange("x d h t -> (x d) h t")[
                                     FR * low:FR * (low + 1), q * UH + 4 * half:q * UH + 4 * half + 4, :]).then_inc(
                                         stacked[q][half], 16)

        @block.sync
        def _(sp):
            for dst, src in ((w, weights), (mean_head, selections[:, 64 + 2 * P:64 + 3 * P]),
                             (mask_f32, selections[:, 64 + 7 * P:64 + 8 * P]), (col, lambda_raw)):
                sp.dma_start(dst[:] if dst is not col else col[:, 0:1], src).then_inc(landed, 16)
            sp.wait_ge(dve_feature, NV)
            sp.wait_ge(pool_feature, NP)
            keep_parts(sp, 0)
            sp.wait_ge(kept, KEPT)
            for q in range(2):
                for half in range(2):
                    stack_heads(sp, 0, q, half)

            def body(b, s):
                wait_apart(sp, dve_feature, (b + 2) * NV, sp_passed)
                wait_apart(sp, pool_feature, (b + 2) * NP, sp_passed)
                for q in range(2):
                    for half in range(2):
                        wait_apart(sp, stacked[q][half], (b + 1) * STACK, sp_passed)
                keep_parts(sp, 1 - s)
                wait_apart(sp, kept, (b + 2) * KEPT, sp_passed)
                for q in range(2):
                    for half in range(2):
                        wait_apart(sp, h_done, (b * 2 + q) * PIECES + 6 * half + 6, sp_passed)
                        stack_heads(sp, 1 - s, q, half)

            body(0, 0)
            with sp.Fori(0, NB // 2 - 1) as i:
                body(i * 2 + 1, 1)
                body(i * 2 + 2, 0)

        @block.tensor
        def _(pe):
            mm = nc.tensor.matmul
            pe.wait_ge(landed, 64)
            pe.wait_ge(prepared, 1)

            def use(kind, b, name):
                n = turn_of(kind, b, name)
                if not isinstance(n, int) or n > 0:
                    pe.wait_ge(f_free, n)

            def front(kind, b, name):
                use(kind, b - 1 if name == "v" else b - 2, name)
                if name == "turn":
                    pe.wait_ge(norm.normed, b + 1)
                    for t in range(TC):
                        last = nc.tensor.transpose(ps_f[:, t * P:(t + 1) * P], norm.xn[:, t * P:(t + 1) * P], ident[:])
                elif name == "v":
                    for t in range(TC):
                        last = mm(ps_f[:, t * P:(t + 1) * P], xT[:, t * P:(t + 1) * P], w[:, W_V:W_V + P],
                                  start=True, stop=True)
                elif name in ("msq", "msk"):
                    s = name == "msk"
                    pe.wait_ge(pool_feature, b * NP + 1 + s)
                    last = mm(ps_f[:], mean_head[:], tmp[s][:], start=True, stop=True)
                else:
                    at = {"q": W_Q, "k": W_K, "qp": W_QP, "kp": W_KP}[name]
                    last = mm(ps_f[:], w[:, at:at + P], xT[:], start=True, stop=True)
                last.then_inc(f_done, 1)

            def scores_for_maximum(b, q, h, tiles, first):
                u = b * 2 + q
                if h % 4 == 0 and tiles[0] == 0:
                    pe.wait_ge(stacked[q][h // 4], (b + 1) * STACK)
                for t in tiles:
                    n = h * TC + t
                    if not (first and n < 2):
                        pe.wait_ge(g_free, u * UH * TC + n - 1)
                    out, width = ps_g[n % 2], WIDTH[t]
                    mm(out[:, 0:width], stack[0][q][0:ROWS, h, t * P:(t + 1) * P], stack[1][q][0:ROWS, h, 0:width],
                       start=True, stop=False)
                    mm(out[:, t * P:(t + 1) * P], ident_b[:], mask[:], start=False, stop=True).then_inc(g_done, 1)

            def turn_maxima(kind, b, name, u):
                half = name.endswith("b")
                pe.wait_ge(g_free, u * UH * TC + (half + 1) * 4 * TC)
                use(kind, b, name)
                for t in range(TC):
                    last = mm(ps_f[0:4, t * P:(t + 1) * P], maxima[:, t, 4 * half:4 * half + 4], ident[:],
                              start=True, stop=True)
                last.then_inc(f_done, 1)

            def scores(b, q, p, piece, first):
                u = b * 2 + q
                if p % 2 == 0 and piece == 0:
                    pe.wait_ge(neg_max_landed[p // 2], (u + 1) * 32)

                def tile(out, h, j):
                    return mm(out, stack[1][q][0:ROWS + 2, h, j * P:(j + 1) * P],
                              stack[0][q][0:ROWS + 2, h, j * P:T], start=True, stop=True)

                n = 3 * p + piece
                if not (first and n < 2):
                    pe.wait_ge(exp_done, u * PIECES + n - 1)
                out = ps_h[n % 2]
                if piece < 2:
                    h = 2 * p + piece
                    for j in (0, 1, 3):
                        at, width = PLACE[j]
                        last = tile(out[:, at:at + width], h, j)
                else:
                    for h in (2 * p, 2 * p + 1):
                        at = (h % 2) * 2 * P
                        last = tile(out[:, at:at + 2 * P], h, 2)
                last.then_inc(h_done, 1)

            def weigh_values(b, s, g, first, tiles):
                if tiles[0] == 0:
                    pe.wait_ge(masked, b * 4 + g + 1)
                    if not first or g:
                        pe.wait_ge(o_ready, b * 4 + g)
                for j in tiles:
                    at, width = PLACE[j]
                    for hh in range(4):
                        last = mm(ps_o[32 * hh:32 * hh + 32, j * P:T], v_ones[:, s, j, 4 * g + hh, :],
                                  probs[:, g % 2, hh, at:at + width], start=(j == 0), stop=(j == TC - 1))
                if tiles[-1] == TC - 1:
                    last.then_inc(av_done, 1)

            def turn_output(kind, b, name, of):
                pe.wait_ge(o_ready, of)
                use(kind, b, name)
                for t in range(TC):
                    last = nc.tensor.transpose(ps_f[:, t * P:(t + 1) * P], o_rows[:, t * P:(t + 1) * P], ident[:])
                last.then_inc(f_done, 1)

            def final(kind, b, name):
                use(kind, b, name)
                for t in range(TC):
                    if name == "FT":
                        last = nc.tensor.transpose(ps_f[:, t * P:(t + 1) * P], o_norm[:, t, :], ident[:])
                    else:
                        last = mm(ps_f[:, t * P:(t + 1) * P], oT[:, t * P:(t + 1) * P], w[:, W_O:W_O + P],
                                  start=True, stop=True)
                last.then_inc(f_done, 1)

            def between(kind, b, s, here):
                first, last = kind == "first", kind == "last"
                ahead = kind not in ("late", "last")
                q, p, piece = here
                if p % 2 == 0 and piece > 0 and not (first and here[:2] == (0, 0)):
                    tiles = (0,) if piece == 1 else (1, 2, 3)
                    if here[:2] == (0, 0):
                        weigh_values(b - 1, 1 - s, 3, False, tiles)
                    else:
                        weigh_values(b, s, 2 * q + p // 2 - 1, first, tiles)
                if here == (0, 0, 2) and not last:
                    front(kind, b + 1, "v")
                if here == (0, 1, 0):
                    turn_maxima(kind, b, "M0b", b * 2)
                if here == (0, 1, 1) and not first:
                    turn_output(kind, b, "E3", b * 4)
                if here == (0, 2, 0) and not first:
                    final(kind, b, "FT")
                if here == (0, 2, 1):
                    turn_maxima(kind, b, "M1a", b * 2 + 1)
                if here == (0, 2, 2) and not first:
                    final(kind, b, "FW")
                if here == (0, 3, 1):
                    turn_output(kind, b, "E0", b * 4 + 1)
                if here == (0, 3, 2) and ahead:
                    front(kind, b + 2, "turn")
                if here == (1, 0, 0) and ahead:
                    front(kind, b + 2, "q")
                if here == (1, 0, 1):
                    turn_maxima(kind, b, "M1b", b * 2 + 1)
                if here == (1, 0, 2) and ahead:
                    front(kind, b + 2, "k")
                if here == (1, 1, 0) and ahead:
                    front(kind, b + 2, "qp")
                if here == (1, 1, 1):
                    turn_output(kind, b, "E1", b * 4 + 2)
                if here == (1, 1, 2) and ahead:
                    front(kind, b + 2, "kp")
                if here == (1, 2, 1) and not last:
                    turn_maxima(kind, b, "M0a", b * 2 + 2)
                if here == (1, 3, 1):
                    turn_output(kind, b, "E2", b * 4 + 3)
                if here == (1, 3, 1) and ahead:
                    front(kind, b + 2, "msq")
                if here == (1, 3, 2) and ahead:
                    front(kind, b + 2, "msk")

            def body(kind, b, s):
                for q in range(2):
                    for p in range(4):
                        for piece in range(3):
                            scores(b, q, p, piece, kind == "first" and q == 0)
                            if not (kind == "last" and q == 1):
                                at = 8 * p + (0, 3, 6)[piece]
                                for n in range(at, at + (3, 3, 2)[piece]):
                                    scores_for_maximum(b + q, 1 - q, n // TC, (n % TC,), False)
                            between(kind, b, s, (q, p, piece))

            for name in ORDERS["start"]:
                front("start", 0, name)
            for name in ORDERS["start1"]:
                front("start1", 1, name)
            for h in range(UH):
                scores_for_maximum(0, 0, h, range(TC), True)
                if h == 4:
                    turn_maxima("start2", 0, "M0a", 0)
            body("first", 0, 0)
            with pe.Fori(0, NB // 2 - 2) as i:
                body("mid", i * 2 + 1, 1)
                body("mid", i * 2 + 2, 0)
            body("mid", NB - 3, 1)
            body("late", NB - 2, 0)
            body("last", NB - 1, 1)
            weigh_values(NB - 1, 1, 3, False, range(TC))
            turn_output("end", 0, "E3", NB * 4)
            final("end", 0, "FT")
            final("end", 0, "FW")

        @block.scalar
        def _(act):
            fn = nc.scalar.activation
            act.wait_ge(landed, 64)
            fn(col[:, 1:2], col[:, 0:1], ACT.Tanh).then_inc(lambda_ready, 1)

            def front(kind, b, s, name):
                got = lambda other: turn_of(kind, b - 1 if other == "v" else b - 2, other) + 1
                base = b * NA
                if name in ("turn", "v", "q", "k", "qp", "kp", "msq", "msk"):
                    act.wait_ge(f_done, got(name))
                if name == "turn":
                    fn(xT[:], ps_f[:], ACT.Copy).then_inc(f_free, 1)
                elif name == "v":
                    fn(v_ones[:, s, :, :, 0:HD].rearrange("p t h d -> p (t h) d"),
                       ps_f[:].rearrange("p (n d) -> p n d", d=HD), ACT.Copy).then_inc(f_free, 1)
                elif name in ("q", "k"):
                    fn(value[name == "k"][:, 0, :], ps_f[:], ACT.Copy).then_inc(f_free, 1)
                elif name in ("qp", "kp"):
                    fn(value[name == "kp"][:, 2, :], ps_f[:], ACT.Copy).then_inc(f_free, 1)
                elif name in ("msq", "msk"):
                    fn(tmp[name == "msk"][:], ps_f[:], ACT.Copy, bias=AMP_EPS).then_inc(f_free, 1)
                elif name == "decay":
                    for s2 in range(2):
                        act.wait_ge(dve_feature, b * NV + 1 + s2)
                        fn(tmp[s2][:], tmp[s2][:], ACT.Exp, scale=-1.0).then_inc(act_feature, 1)
                elif name == "phase":
                    for s2, other in enumerate(("qp", "kp")):
                        act.wait_ge(f_free, got(other))
                        fn(value[s2][:, 2, :], value[s2][:, 2, :], ACT.Tanh).then_inc(act_feature, 1)
                elif name == "softplus":
                    for s2 in range(2):
                        act.wait_ge(act_feature, base + 1 + s2)
                        fn(tmp[s2][:], tmp[s2][:], ACT.Ln, bias=col[:, 2:3]).then_inc(act_feature, 1)
                elif name == "rms":
                    for s2, other in enumerate(("msq", "msk")):
                        act.wait_ge(f_free, got(other))
                        fn(tmp[s2][:], tmp[s2][:], ACT.Ln).then_inc(act_feature, 1)
                elif name == "inverse":
                    for s2 in range(2):
                        act.wait_ge(act_feature, base + 11 + s2)
                        fn(tmp[s2][:], tmp[s2][:], ACT.Exp, scale=-0.5).then_inc(act_feature, 1)
                elif name == "circle":
                    for s2 in range(2):
                        act.wait_ge(dve_feature, b * NV + 3 + s2)
                        fn(value[s2][:, 2, :], value[s2][:, 2, :], ACT.Sin, scale=PI).then_inc(act_feature, 1)
                        fn(value[s2][:, 1, :], value[s2][:, 1, :], ACT.Sin, scale=-PI, bias=col[:, 4:5]).then_inc(act_feature, 1)

            def exponentials(b, q, p, piece, first):
                u = b * 2 + q
                n = 3 * p + piece
                g = 2 * q + p // 2
                if p % 2 == 0 and piece == 0 and not (first and g < 2):
                    act.wait_ge(av_done, b * 4 + g - 1)
                act.wait_ge(h_done, u * PIECES + n + 1)
                out = probs[:, g % 2]
                if piece < 2:
                    fn(out[:, (2 * p + piece) % 4, 0:8 * P], ps_h[n % 2][:], ACT.Exp, scale=SCALE).then_inc(exp_done, 1)
                else:
                    hh = (2 * p) % 4
                    fn(out[:, hh:hh + 2, 8 * P:10 * P], ps_h[n % 2][:, 0:4 * P].rearrange("p (h n) -> p h n", h=2),
                       ACT.Exp, scale=SCALE).then_inc(exp_done, 1)

            def take_output(b, g, before):
                act.wait_ge(av_done, b * 4 + g + 1)
                if before is not None:
                    act.wait_ge(f_done, before + 1)
                fn(o_rows[:], ps_o[:], ACT.Copy).then_inc(o_ready, 1)

            def send_maxima(kind, b, name, u, q):
                half = int(name.endswith("b"))
                act.wait_ge(f_done, turn_of(kind, b, name) + 1)
                if not isinstance(u, int) or u > 0:
                    act.wait_ge(neg_max_landed[half], u * 32)
                fn(neg_max[half][:, 0, :], ps_f[0:4, :], ACT.Copy, scale=-1.0).then_inc(neg_max_high, 1)
                act.wait_ge(f_free, turn_of(kind, b, name) + 1)
                for part in range(2):
                    act.dma_start(stack[0][q][ROWS + part:ROWS + part + 1, 4 * half:4 * half + 4, :].bitcast(F32),
                                  neg_max[half][:, part, :].bitcast(F32)).then_inc(neg_max_landed[half], 16)

            def turned_copy(kind, b):
                act.wait_ge(f_done, turn_of(kind, b, "FT") + 1)
                fn(oT[:], ps_f[:], ACT.Copy).then_inc(f_free, 1)

            def between(kind, b, s, here):
                first, last = kind == "first", kind == "last"
                ahead = kind not in ("late", "last")
                e = lambda name: turn_of(kind, b, name)
                if here == (0, 0, 2) and not last:
                    front(kind, b + 1, 1 - s, "v")
                if here == (0, 1, 0) and not first:
                    take_output(b - 1, 3, e(ORDERS[kind][0]) - (1 if last else 3))
                if here == (0, 1, 0):
                    send_maxima(kind, b, "M0b", b * 2, 0)
                if here == (0, 2, 0) and not first:
                    turned_copy(kind, b)
                if here == (0, 2, 1):
                    send_maxima(kind, b, "M1a", b * 2 + 1, 1)
                if here == (0, 3, 0):
                    take_output(b, 0, None if first else e("E3"))
                if here == (1, 0, 1):
                    send_maxima(kind, b, "M1b", b * 2 + 1, 1)
                if here == (1, 1, 0):
                    take_output(b, 1, e("E0"))
                if here == (1, 2, 1) and not last:
                    send_maxima(kind, b, "M0a", b * 2 + 2, 0)
                if here == (1, 3, 0):
                    take_output(b, 2, e("E1"))
                if ahead:
                    for name in {(0, 3, 2): ("turn",), (1, 0, 0): ("q",), (1, 0, 2): ("k",), (1, 1, 0): ("qp",),
                                 (1, 1, 1): ("decay",), (1, 1, 2): ("kp",), (1, 2, 0): ("phase",),
                                 (1, 2, 1): ("softplus",), (1, 3, 0): ("circle",), (1, 3, 1): ("msq",),
                                 (1, 3, 2): ("msk", "rms", "inverse")}.get(here, ()):
                        front(kind, b + 2, s, name)

            def body(kind, b, s):
                for q in range(2):
                    for p in range(4):
                        for piece in range(3):
                            exponentials(b, q, p, piece, kind == "first")
                            between(kind, b, s, (q, p, piece))

            act.wait_ge(prepared, 1)
            for name in ("turn", "q", "k", "qp", "kp", "v", "decay", "phase", "softplus", "circle", "msq", "msk", "rms",
                         "inverse"):
                front("start", 0, 0, name)
            for name in ("turn", "q", "k", "qp", "kp", "decay", "phase", "softplus", "circle", "msq", "msk", "rms",
                         "inverse"):
                front("start1", 1, 1, name)
            send_maxima("start2", 0, "M0a", 0, 0)
            body("first", 0, 0)
            with act.Fori(0, NB // 2 - 2) as i:
                body("mid", i * 2 + 1, 1)
                body("mid", i * 2 + 2, 0)
            body("mid", NB - 3, 1)
            body("late", NB - 2, 0)
            body("last", NB - 1, 1)
            take_output(NB - 1, 3, turn_of("last", NB - 1, "E2"))
            turned_copy("end", 0)

        @block.gpsimd
        def _(pool):
            tt = nc.gpsimd.tensor_tensor

            def zero_above(b, g, q, p):
                wait_apart(pool, exp_done, (b * 2 + q) * PIECES + 3 * p + 3, pool_passed)
                for j in range(TC):
                    at = PLACE[j][0]
                    tile = probs[:, g % 2, :, at:at + P]
                    last = nc.gpsimd.affine_select(out=tile, in_=tile, compare_op=ALU.is_ge, fill=0.0, base=0,
                                                   pattern=[[0, 4], [1, P]], channel_multiplier=-1)
                last.then_inc(masked, 1)

            def squares(b):
                for s in range(2):
                    pool.wait_ge(dve_feature, b * NV + 5 + s)
                    tt(tmp[s][:], amp[s][:], amp[s][:], ALU.mult).then_inc(pool_feature, 1)

            def products(b):
                for s in range(2):
                    pool.wait_ge(act_feature, b * NA + 8 + 2 * s)
                    pool.wait_ge(dve_feature, b * NV + 7 + s)
                    for n in (1, 2):
                        tt(value[s][:, n, :], value[s][:, n, :], amp[s][:], ALU.mult).then_inc(pool_feature, 1)

            def lows(b):
                for s in range(2):
                    pool.wait_ge(dve_feature, b * NV + 9 + s)
                    tt(parts[s][:, 3:6, :], value[s][:], parts[s][:, 0:3, :].bitcast(F32), ALU.subtract).then_inc(pool_feature, 1)

            def body(kind, b):
                ahead = kind not in ("late", "last")
                for q in range(2):
                    for p in range(4):
                        if q == 0 and p == 0 and kind != "last":
                            products(b + 1)
                            lows(b + 1)
                        if p % 2:
                            zero_above(b, 2 * q + p // 2, q, p)
                        if q == 0 and p == 2 and ahead:
                            norm.on_pool(pool, b + 2)
                        if q == 1 and p == 2 and ahead:
                            squares(b + 2)

            norm.on_pool(pool, 0)
            squares(0)
            products(0)
            lows(0)
            norm.on_pool(pool, 1)
            squares(1)
            body("first", 0)
            with pool.Fori(0, NB - 3) as i:
                body("mid", i + 1)
            body("late", NB - 2)
            body("last", NB - 1)

        @block.vector
        def _(v):
            tt, ts, stt = nc.vector.tensor_tensor, nc.vector.tensor_scalar, nc.vector.scalar_tensor_tensor
            v.wait_ge(landed, 64)
            v.wait_ge(lambda_ready, 1)
            for s in range(2):
                nc.vector.memset(v_ones[:, s, :, :, HD:HD + 1], 1.0)
                nc.vector.memset(v_ones[:, s, :, :, HD + 1:32], 0.0)
                nc.vector.memset(stack[1][s][64:ROWS + 2].bitcast(F32), 1.0)
            nc.vector.memset(col[:, 2:3], 1.0)
            nc.vector.memset(col[:, 3:4], AMP_EPS)
            nc.vector.memset(col[:, 4:5], PI / 2)
            ts(col[:, 0:1], col[:, 1:2], LAMBDA_MAX, None, ALU.mult)
            nc.vector.tensor_copy(mask[:], mask_f32[:])
            nc.vector.tensor_copy(ident_b[:], ident[:]).then_inc(prepared, 1)
            v.wait_ge(prepared, 1)

            def front(kind, b, step, first=False):
                got = lambda other: turn_of(kind, b - 2, other) + 1
                if step == "norm":
                    norm.on_vector(v, b)
                if step == "size":
                    for s, name in enumerate(("q", "k")):
                        v.wait_ge(f_free, got(name))
                        stt(tmp[s][:], value[s][:, 0, :], -1.0, value[s][:, 0, :], ALU.mult, ALU.max).then_inc(dve_feature, 1)
                if step == "phase":
                    for s in range(2):
                        v.wait_ge(act_feature, b * NA + 3 + s)
                        stt(value[s][:, 1, :], value[s][:, 2, :], -1.0, value[s][:, 2, :], ALU.mult, ALU.max).then_inc(dve_feature, 1)
                if step == "softplus":
                    for s in range(2):
                        v.wait_ge(act_feature, b * NA + 5 + s)
                        stt(amp[s][:], value[s][:, 0, :], 0.0, tmp[s][:], ALU.max, ALU.add).then_inc(dve_feature, 1)
                if step == "amplitude":
                    for s in range(2):
                        v.wait_ge(act_feature, b * NA + 13 + s)
                        if s == 0:
                            stt(amp[s][:], amp[s][:], col[:, 0:1], tmp[s][:], ALU.mult, ALU.mult).then_inc(dve_feature, 1)
                        else:
                            tt(amp[s][:], amp[s][:], tmp[s][:], ALU.mult).then_inc(dve_feature, 1)
                if step == "high":
                    for s in range(2):
                        v.wait_ge(pool_feature, b * NP + 4 + 2 * s)
                        if not first and s == 0:
                            v.wait_ge(kept, b * KEPT)
                        nc.vector.tensor_copy(parts[s][:, 0:3, :], value[s][:]).then_inc(dve_feature, 1)

            def take_maxima(b, q, h, t):
                u = b * 2 + q
                n = h * TC + t
                v.wait_ge(g_done, u * UH * TC + n + 1)
                nc.vector.tensor_reduce(maxima[:, t, h:h + 1], ps_g[n % 2][:, 0:(t + 1) * P], AX_X,
                                        ALU.max).then_inc(g_free, 1)

            def low_maxima(name, u):
                half = int(name.endswith("b"))
                v.wait_ge(neg_max_high, u * 2 + half + 1)
                stt(neg_max[half][:, 1, :], ps_f[0:4, :], -1.0, neg_max[half][:, 0, :].bitcast(F32), ALU.mult,
                    ALU.subtract).then_inc(f_free, 1)

            def normalise(kind, b, name, g, count):
                v.wait_ge(f_done, turn_of(kind, b, name) + 1)
                rows = ps_f[:].rearrange("p (n c) -> p n c", c=32)
                nc.vector.reciprocal(inv[:], rows[:, :, HD]).then_inc(inv_ready, 1)
                v.wait_ge(inv_ready, count + 1)
                tt(o_norm[:, :, 4 * g * HD:4 * (g + 1) * HD].rearrange("p t (h d) -> p t h d", d=HD),
                   rows[:, :, 0:HD].rearrange("p (t h) d -> p t h d", t=TC),
                   inv[:].rearrange("p (t h) -> p t h", t=TC).unsqueeze(3).broadcast_to([P, TC, 4, HD]),
                   ALU.mult).then_inc(f_free, 1)

            def add_output(kind, b, of):
                v.wait_ge(f_done, turn_of(kind, b, "FW") + 1)
                rows = x[:, bass.ds(of * T, T)]
                tt(rows, rows, ps_f[:], ALU.add).then_inc(f_free, 1)

            def between(kind, b, here):
                first, last = kind == "first", kind == "last"
                ahead = kind not in ("late", "last")
                if here == (0, 0, 2) and not last:
                    front(kind, b + 1, "amplitude")
                if here == (0, 1, 0):
                    low_maxima("M0b", b * 2)
                if here == (0, 1, 1) and not last:
                    front(kind, b + 1, "high")
                if here == (0, 1, 1) and not first:
                    normalise(kind, b, "E3", 3, b * 4 - 1)
                if here == (0, 1, 2) and ahead:
                    norm.statistics(v, b + 2)
                if here == (0, 2, 1):
                    low_maxima("M1a", b * 2 + 1)
                if here == (0, 2, 2) and not first:
                    add_output(kind, b, b - 1)
                if here == (0, 3, 0) and ahead:
                    norm.scale(v, b + 2)
                if here == (0, 3, 1):
                    normalise(kind, b, "E0", 0, b * 4)
                if here == (1, 0, 1):
                    low_maxima("M1b", b * 2 + 1)
                if here == (1, 1, 0) and ahead:
                    front(kind, b + 2, "size")
                if here == (1, 1, 1):
                    normalise(kind, b, "E1", 1, b * 4 + 1)
                if here == (1, 2, 1) and not last:
                    low_maxima("M0a", b * 2 + 2)
                if here == (1, 2, 1) and ahead:
                    front(kind, b + 2, "phase")
                if here == (1, 3, 0) and ahead:
                    front(kind, b + 2, "softplus")
                if here == (1, 3, 1):
                    normalise(kind, b, "E2", 2, b * 4 + 2)

            def body(kind, b):
                for q in range(2):
                    for p in range(4):
                        for piece in range(3):
                            if not (kind == "last" and q == 1):
                                at = 8 * p + (0, 3, 6)[piece]
                                for n in range(at, at + (3, 3, 2)[piece]):
                                    take_maxima(b + q, 1 - q, n // TC, n % TC)
                            between(kind, b, (q, p, piece))

            for step in ("norm", "size", "phase", "softplus", "amplitude", "high"):
                front("start", 0, step, first=True)
            for step in ("norm", "size", "phase", "softplus"):
                front("start1", 1, step)
            for h in range(UH):
                for t in range(TC):
                    take_maxima(0, 0, h, t)
                if h == 4:
                    low_maxima("M0a", 0)
            body("first", 0)
            with v.Fori(0, NB - 3) as i:
                body("mid", i + 1)
            body("late", NB - 2)
            body("last", NB - 1)
            normalise("end", 0, "E3", 3, NB * 4 - 1)
            add_output("end", 0, NB - 1)


def moe_phase(nc, phase, x, ident, minus_half, codes, started, router_w, w1, w2):
    with ExitStack() as ctx:
        def sb(name, shape, dt=F32):
            return ctx.enter_context(nc.sbuf_tensor(f"{phase}_{name}", shape, dt))

        def ps(name, shape=(P, 512), dt=F32):
            return ctx.enter_context(nc.psum_tensor(f"{phase}_{name}", list(shape), dt))

        def sem(name):
            return ctx.enter_context(nc.semaphore(f"{phase}_{name}"))

        w1_cols = sb("w1_cols", [P, NE * HC * P])
        w1_high = sb("w1_high", [P, NE * HC * P], F32R)
        w1_low = sb("w1_low", [P, NE * HC * P], F32R)
        w2_cols = sb("w2_cols", [P, NE * HC * P])
        router = sb("router", [P, NE])
        norm = Norm(nc, sb, sem, x, minus_half, started)
        xT = sb("xT", [P, 2, T])
        x_high = sb("x_high", [P, 2, T], F32R)
        x_low = sb("x_low", [P, 2, T], F32R)
        logits = sb("logits", [P, TC, NE])
        code = sb("code", [P, TC, NE])
        first = sb("first", [P, TC, NE])
        second = sb("second", [P, TC, NE])
        rest = sb("rest", [P, TC, NE])
        top = sb("top", [P, 4, TC])
        share = sb("share", [P, 4, TC])
        gate = sb("gate", [P, 2, TC, NE])
        hidden = sb("hidden", [P, 2, HC, T])

        ps_t = ps("ps_t")
        ps_logits = ps("ps_logits")
        ps_h = [[ps(f"ps_h{s}{k}") for k in range(HC)] for s in range(2)]
        ps_y = [ps(f"ps_y{s}") for s in range(2)]

        weights_landed = sem("weights_landed")
        weights_split = sem("weights_split")
        weight_order = sem("weight_order")
        gate_order = sem("gate_order")
        gate_ready = sem("gate_ready")
        transposed = sem("transposed")
        high_ready = sem("high_ready")
        low_ready = sem("low_ready")
        logits_done = sem("logits_done")
        gap_ready = sem("gap_ready")
        exp_ready = sem("exp_ready")
        hidden_done = sem("hidden_done")
        gelu_done = sem("gelu_done")
        y_done = sem("y_done")
        y_used = sem("y_used")

        block = ctx.enter_context(nc.Block())

        @block.sync
        def _(sp):
            sp.dma_start(w1_cols[:], w1).then_inc(weights_landed, 16)
            sp.dma_start(w2_cols[:], w2).then_inc(weights_landed, 16)
            sp.dma_start(router[:], router_w).then_inc(weights_landed, 16)

        @block.gpsimd
        def _(pool):
            with pool.Fori(0, NB) as b:
                norm.on_pool(pool, b)

        @block.tensor
        def _(pe):
            pe.wait_ge(weights_landed, 48)
            pe.wait_ge(weights_split, 1)

            def turn(b):
                pe.wait_ge(norm.normed, b + 1)
                for t in range(TC):
                    last = nc.tensor.transpose(ps_t[:, t * P:(t + 1) * P], norm.xn[:, t * P:(t + 1) * P], ident[:])
                last.then_inc(transposed, 1)

            def route(b, s):
                pe.wait_ge(high_ready, b + 1)
                for t in range(TC):
                    last = nc.tensor.matmul(ps_logits[:, t * NE:(t + 1) * NE], xT[:, s, t * P:(t + 1) * P],
                                            router[:], start=True, stop=True)
                last.then_inc(logits_done, 1)

            def up(b, s, e, wait_slot=True):
                if e == 0:
                    pe.wait_ge(low_ready, b + 1)
                for k in range(HC):
                    if wait_slot:
                        pe.wait_ge(gelu_done, (b * NE + e - 2) * HC + k + 1)
                    cols = slice((e * HC + k) * P, (e * HC + k + 1) * P)
                    out = ps_h[e % 2][k]
                    nc.tensor.matmul(out[:], w1_high[:, cols], x_high[:, s, :], start=True, stop=False)
                    nc.tensor.matmul(out[:], w1_high[:, cols], x_low[:, s, :], start=False, stop=False)
                    nc.tensor.matmul(out[:], w1_low[:, cols], x_high[:, s, :], start=False,
                                     stop=True).then_inc(hidden_done, 1)

            def down(b, e, wait_slot=True):
                pe.wait_ge(gelu_done, (b * NE + e + 1) * HC)
                if wait_slot:
                    pe.wait_ge(y_used, b * NE + e - 1)
                for t in range(TC):
                    for k in range(HC):
                        cols = slice((e * HC + k) * P, (e * HC + k + 1) * P)
                        last = nc.tensor.matmul(ps_y[e % 2][:, t * P:(t + 1) * P], hidden[:, e % 2, k, t * P:(t + 1) * P],
                                                w2_cols[:, cols], start=(k == 0), stop=(k == HC - 1))
                last.then_inc(y_done, 1)

            def chunk(b, s, first=False, last=False):
                for e in range(NE):
                    if e + 1 < NE:
                        up(b, s, e + 1, wait_slot=not (first and e + 1 < 2))
                    elif not last:
                        up(b + 1, 1 - s, 0)
                    down(b, e, wait_slot=not (first and e < 2))
                    if e == 4 and not last:
                        turn(b + 1)
                    if e == 5 and not last:
                        route(b + 1, 1 - s)

            turn(0)
            route(0, 0)
            up(0, 0, 0, wait_slot=False)
            chunk(0, 0, first=True)
            with pe.Fori(0, NB // 2 - 1) as i:
                chunk(i * 2 + 1, 1)
                chunk(i * 2 + 2, 0)
            chunk(NB - 1, 1, last=True)

        @block.scalar
        def _(act):
            def copies(b, s):
                act.wait_ge(transposed, b + 1)
                nc.scalar.copy(xT[:, s, :], ps_t[:])
                nc.scalar.copy(x_high[:, s, :], ps_t[:]).then_inc(high_ready, 1)

            def gap(b):
                act.wait_ge(gap_ready, b + 1)
                nc.scalar.activation(share[:, 0, :], share[:, 3, :], ACT.Exp).then_inc(exp_ready, 1)

            def gelu(b, e, wait_slot=True):
                for k in range(HC):
                    if wait_slot and k == 0:
                        act.wait_ge(y_done, b * NE + e - 1)
                    act.wait_ge(hidden_done, (b * NE + e) * HC + k + 1)
                    nc.scalar.activation(hidden[:, e % 2, k, :], ps_h[e % 2][k][:], ACT.Gelu).then_inc(gelu_done, 1)

            def chunk(b, s, first=False, last=False):
                for e in range(NE):
                    gelu(b, e, wait_slot=not (first and e < 2))
                    if e == 5 and not last:
                        copies(b + 1, 1 - s)
                    if e == 6 and not last:
                        gap(b + 1)

            copies(0, 0)
            gap(0)
            chunk(0, 0, first=True)
            with act.Fori(0, NB // 2 - 1) as i:
                chunk(i * 2 + 1, 1)
                chunk(i * 2 + 2, 0)
            chunk(NB - 1, 1, last=True)

        @block.vector
        def _(v):
            v.wait_ge(weights_landed, 48)
            nc.vector.tensor_copy(w1_high[:], w1_cols[:]).then_inc(weight_order, 1)
            v.wait_ge(weight_order, 1)
            nc.vector.tensor_tensor(w1_low[:], w1_cols[:], w1_high[:].bitcast(F32),
                                    ALU.subtract).then_inc(weights_split, 1)

            def low(b, s):
                v.wait_ge(high_ready, b + 1)
                nc.vector.tensor_tensor(x_low[:, s, :], ps_t[:], x_high[:, s, :].bitcast(F32),
                                        ALU.subtract).then_inc(low_ready, 1)

            def gates(b, s):
                step = Steps(v, gate_order, b, 16)
                wide = lambda column: column.unsqueeze(2).broadcast_to([P, TC, NE])
                tt, ts, tr = nc.vector.tensor_tensor, nc.vector.tensor_scalar, nc.vector.tensor_reduce
                v.wait_ge(logits_done, b + 1)
                step(nc.vector.tensor_copy(logits[:], ps_logits[:, 0:TC * NE]))
                step(tr(top[:, 0, :], logits[:], AX_X, ALU.max))
                for pick, value, at, left in ((first, 0, 1, logits), (second, 2, 3, rest)):
                    step(tt(pick[:], left[:], wide(top[:, value, :]), ALU.is_equal))
                    step(tt(code[:], pick[:], codes[:].rearrange("p (t e) -> p t e", t=TC), ALU.mult))
                    step(tr(top[:, at, :], code[:], AX_X, ALU.max))
                    step(tt(pick[:], code[:], wide(top[:, at, :]), ALU.is_equal))
                    if pick is first:
                        step(nc.vector.scalar_tensor_tensor(rest[:], first[:], LOWEST, logits[:], ALU.mult, ALU.add))
                        step(tr(top[:, 2, :], rest[:], AX_X, ALU.max))
                tt(share[:, 3, :], top[:, 2, :], top[:, 0, :], ALU.subtract).then_inc(gap_ready, 1)
                v.wait_ge(exp_ready, b + 1)
                step(ts(share[:, 1, :], share[:, 0, :], 1.0, None, ALU.add))
                step(nc.vector.reciprocal(share[:, 1, :], share[:, 1, :]))
                step(tt(share[:, 2, :], share[:, 0, :], share[:, 1, :], ALU.mult))
                tt(first[:], first[:], wide(share[:, 1, :]), ALU.mult)
                step(tt(second[:], second[:], wide(share[:, 2, :]), ALU.mult))
                tt(gate[:, s], first[:], second[:], ALU.add).then_inc(gate_ready, 1)
                step.done()
                v.wait_ge(gate_ready, b + 1)

            def add(b, s, e):
                v.wait_ge(y_done, b * NE + e + 1)
                if e:
                    v.wait_ge(y_used, b * NE + e)
                for t in range(TC):
                    rows = x[:, bass.ds(b * T + t * P, P)]
                    last = nc.vector.scalar_tensor_tensor(rows, ps_y[e % 2][:, t * P:(t + 1) * P],
                                                          gate[:, s, t, e:e + 1], rows, ALU.mult, ALU.add)
                last.then_inc(y_used, 1)

            def chunk(b, s, last=False):
                for e in range(NE):
                    add(b, s, e)
                    if not last:
                        if e == 2:
                            norm.on_vector(v, b + 1, (transposed, b + 1))
                        if e == 4:
                            low(b + 1, 1 - s)
                        if e == 5:
                            gates(b + 1, 1 - s)

            norm.on_vector(v, 0)
            low(0, 0)
            gates(0, 0)
            chunk(0, 0)
            with v.Fori(0, NB // 2 - 1) as i:
                chunk(i * 2 + 1, 1)
                chunk(i * 2 + 2, 0)
            chunk(NB - 1, 1, last=True)


def program(nc, aps, out):
    with ExitStack() as ctx:
        x, ident, minus_half, codes, started = common(nc, ctx, aps)
        experts = (codes, started, aps["router"], aps["w1"], aps["w2"])
        rwkv_phase(nc, x, ident, minus_half, started, aps["rwkv_weights"], aps["columns"], aps["selections"])
        moe_phase(nc, "moe0", x, ident, minus_half, *experts)
        attention_phase(nc, x, ident, minus_half, started, aps["attn_weights"], aps["lambda_raw"], aps["selections"])
        moe_phase(nc, "moe1", x, ident, minus_half, *experts)
        stored = ctx.enter_context(nc.semaphore("stored"))
        with nc.Block() as block:
            @block.sync
            def _(sp):
                sp.dma_start(out, x[:]).then_inc(stored, 16)
                sp.wait_ge(stored, 16)


def kernel(**inputs):
    import concourse.bacc as bacc
    from concourse.bass_utils import run_bass_kernel_spmd

    nc = bacc.Bacc("TRN2", target_bir_lowering=False, num_devices=1)
    arrays = layout(inputs)
    aps = {n: nc.dram_tensor(f"in_{n}", a.shape, F32, kind="ExternalInput").ap() for n, a in arrays.items()}
    out = nc.dram_tensor("out_rows", (P, NT * C), F32, kind="ExternalOutput").ap()
    program(nc, aps, out)
    got = run_bass_kernel_spmd(nc, [{f"in_{n}": a for n, a in arrays.items()}], core_ids=[0])
    rows = got.results[0]["out_rows"]
    return rows.reshape(P, NT, C).transpose(1, 0, 2).reshape(NB, T, C)
```

```python
from contextlib import ExitStack

import numpy as np
import concourse.bass as bass
from concourse import mybir

ALU = mybir.AluOpType
ACT = mybir.ActivationFunctionType
F32 = mybir.dt.float32
F32R = mybir.dt.float32r
BF16 = mybir.dt.bfloat16
AX_X = mybir.AxisListType.X

P = 128
NB = 8
T = 512
TC = T // P
NT = NB * TC
C = 128
H = 16
HD = C // H
NE = 8
PI = float(np.nextafter(np.float32(np.pi), np.float32(0)))
LAMBDA_MAX = 0.5
AMP_EPS = 1e-6
MIX_TERMS = (0, 1, 2, 3, 4)
HC = 2
LN_EPS = 1e-5
GN_EPS = 1e-5 * 8 ** 2
LOWEST = -3e38
EXPERT_SHAPES = dict(router=[P, NE], w1=[P, NE * HC * P], w2=[P, NE * HC * C])


def constants():
    rows = np.arange(P)
    head_of_channel, head_of_column = rows // HD, rows % H
    sel = np.zeros((P, 64 + 8 * P), np.float32)
    for half in range(2):
        sel[rows, 32 * half + 16 * half + head_of_channel] = 1.0
    sel[:, 64:64 + P] = head_of_channel[:, None] == head_of_column[None, :]
    sel[:, 64 + P:64 + 2 * P] = (head_of_column[:, None] == head_of_column[None, :]) / HD
    sel[:, 64 + 2 * P:64 + 3 * P] = (head_of_channel[:, None] == head_of_channel[None, :]) / HD
    for j in range(4):
        takes = (rows[:, None] % 64 // H == j) & (head_of_column[:, None] == head_of_channel[None, :])
        sel[:, 64 + (3 + j) * P:64 + (4 + j) * P] = takes
    sel[:, 64 + 7 * P:] = np.where(rows[None, :] > rows[:, None], LOWEST / 300, 0.0)
    return {
        "selections": sel,
        "ident": np.eye(P, dtype=np.float32),
        "codes": np.tile(np.arange(NE, 0, -1, dtype=np.float32), (P, TC)),
    }


def layout(inputs):
    a = {n.removeprefix("L0_attn_a_"): np.asarray(v) for n, v in inputs.items() if n.startswith("L0_attn_a_")}
    f = {n.removeprefix("L0_ffn_"): np.asarray(v) for n, v in inputs.items() if n.startswith("L0_ffn_")}
    t = {n.removeprefix("L0_attn_b_"): np.asarray(v) for n, v in inputs.items() if n.startswith("L0_attn_b_")}
    by_column = np.arange(P).reshape(H, HD).T.reshape(P)
    lora = np.zeros((P, 5 * P), np.float32)
    for n, term in enumerate(MIX_TERMS):
        row = 32 * n if n < 4 else 0
        lora[row:row + 32, n * P:(n + 1) * P] = a["time_maa_w2"][term]
    decay2 = np.zeros((P, P), np.float32)
    decay2[0:64] = a["time_decay_w2"]
    w_v = a["W_v"][:, by_column]
    lora1 = np.concatenate([a["time_maa_w1"][:, 32 * n:32 * n + 32] for n in MIX_TERMS], axis=1)
    out = {
        "x": a["x"].reshape(NT, P, C).transpose(1, 0, 2).reshape(P, NT * C),
        "rwkv_weights": np.concatenate([
            lora1, lora, a["time_decay_w1"], decay2, a["W_k"],
            w_v[:, 0:64], w_v[:, 0:64], w_v[:, 64:], w_v[:, 64:], a["W_r"], a["W_g"][:, by_column],
            a["W_o"][by_column]], axis=1),
        "columns": np.stack([
            a["time_maa_x"], a["time_maa_w"], a["time_maa_k"], a["time_maa_v"], a["time_maa_r"],
            a["time_maa_g"], a["time_decay"], a["time_faaaa"].reshape(P),
            a["ln_gamma"][by_column], a["ln_beta"][by_column]], axis=1),
        "attn_weights": np.concatenate([t[n] for n in ("Wq", "Wk", "Wqp", "Wkp", "Wv", "Wo")], axis=1),
        "lambda_raw": np.repeat(t["lambda_raw"], HD)[:, None],
        "router": f["router_w"].T,
        "w1": f["w1"].transpose(2, 0, 1).reshape(C, NE * HC * P),
        "w2": f["w2"].reshape(NE, C, HC, P).transpose(3, 0, 2, 1).reshape(P, NE * HC * C),
    }
    return {n: np.ascontiguousarray(v) for n, v in (out | constants()).items()}


class Loaded:

    def __init__(self, nc, ctx, name, **shapes):
        self.landed = ctx.enter_context(nc.semaphore(f"{name}_landed"))
        self.full = 16 * len(shapes)
        self.tiles = [ctx.enter_context(nc.sbuf_tensor(f"{name}_{n}", shape, F32)) for n, shape in shapes.items()]

    def load(self, sp, *sources):
        for tile, source in zip(self.tiles, sources):
            sp.dma_start(tile[:, 0:source.shape[1]], source).then_inc(self.landed, 16)

    def wait(self, engine):
        engine.wait_ge(self.landed, self.full)


class Rows:

    def __init__(self, nc, ctx):
        def sb(name, shape):
            return ctx.enter_context(nc.sbuf_tensor(name, shape, F32))

        self.x, self.ident = sb("x_rows", [P, NT * C]), sb("identity", [P, P])
        self.minus_half, self.codes = sb("minus_half", [P, TC]), sb("expert_codes", [P, TC * NE])
        self.loaded = ctx.enter_context(nc.semaphore("loaded"))
        self.rest_loaded = ctx.enter_context(nc.semaphore("rest_loaded"))
        self.started = ctx.enter_context(nc.semaphore("started"))


def load(nc, aps, rows, mixing, experts, attention):
    EARLY = 2 * T
    x, ident, codes, sel = rows.x, rows.ident, rows.codes, aps["selections"]
    with nc.Block() as block:
        @block.sync
        def _(sp):
            sp.dma_start(x[:, 0:EARLY], aps["x"][:, 0:EARLY]).then_inc(rows.loaded, 16)
            sp.dma_start(ident[:], aps["ident"]).then_inc(rows.loaded, 16)
            mixing.load(sp, aps["rwkv_weights"], aps["columns"], sel[:, 0:64 + 3 * P], sel[:, 64 + 3 * P:64 + 7 * P])
            sp.dma_start(x[:, EARLY:], aps["x"][:, EARLY:]).then_inc(rows.rest_loaded, 16)
            sp.dma_start(codes[:], aps["codes"]).then_inc(rows.rest_loaded, 16)
            experts.load(sp, aps["router"], aps["w1"], aps["w2"])
            attention.load(sp, aps["attn_weights"], sel[:, 64 + 2 * P:64 + 3 * P], sel[:, 64 + 7 * P:64 + 8 * P],
                           aps["lambda_raw"])

        @block.vector
        def _(v):
            v.wait_ge(rows.loaded, 32)
            nc.vector.memset(rows.minus_half[:], -0.5).then_inc(rows.started, 1)

        @block.gpsimd
        def _(pool):
            pool.wait_ge(rows.started, 1)


def wait_apart(engine, semaphore, value, passed):
    engine.wait_ge(semaphore, value)
    engine.sem_inc(passed, 1)


class Steps:

    def __init__(self, engine, order, call, each):
        self.engine, self.order, self.start, self.each, self.n = engine, order, call * each, each, 0

    def __call__(self, instruction):
        self.n += 1
        instruction.then_inc(self.order, 1)
        self.engine.wait_ge(self.order, self.start + self.n)

    def done(self):
        assert self.n == self.each


class Norm:

    def __init__(self, nc, sb, sem, x, minus_half, started):
        self.nc, self.x, self.minus_half, self.started = nc, x, minus_half, started
        self.stats = sb("stats", [P, TC, 6])
        self.sums = sb("sums", [P, TC, 3])
        self.gap = sb("gap", [P, TC])
        self.gap_square = sb("gap_square", [P, TC])
        self.inner = sb("inner", [P, TC])
        self.mean = sb("mean", [P, TC])
        self.var_eps = sb("var_eps", [P, TC])
        self.rstd = sb("rstd", [P, TC])
        self.xn = sb("xn", [P, T])
        self.order = sem("norm_order")
        self.variance_ready = sem("variance_ready")
        self.rstd_ready = sem("rstd_ready")
        self.normed = sem("normed")

    def on_vector(self, v, b, wait_free=None):
        self.statistics(v, b)
        self.scale(v, b, wait_free)

    def statistics(self, v, b):
        nc, step = self.nc, Steps(v, self.order, b, 3)
        for t in range(TC):
            last = nc.vector.bn_stats(self.stats[:, t, :], self.x[:, bass.ds(b * T + t * P, P)])
        step(last)
        even, odd = self.stats[:, :, 0:3], self.stats[:, :, 3:6]
        nc.vector.tensor_tensor(self.sums[:], even, odd, ALU.add)
        step(nc.vector.tensor_tensor(self.gap[:], even[:, :, 1], odd[:, :, 1], ALU.subtract))
        nc.vector.tensor_scalar(self.mean[:], self.sums[:, :, 1], 0.5, None, ALU.mult)
        nc.vector.scalar_tensor_tensor(self.gap_square[:], self.gap[:], 0.25, self.gap[:], ALU.mult, ALU.mult)
        step(nc.vector.tensor_scalar(self.inner[:], self.sums[:, :, 2], 1.0 / C, LN_EPS, ALU.mult, ALU.add))
        nc.vector.tensor_tensor(self.var_eps[:], self.inner[:], self.gap_square[:],
                                ALU.add).then_inc(self.variance_ready, 1)
        step.done()

    def scale(self, v, b, wait_free=None):
        nc = self.nc
        v.wait_ge(self.rstd_ready, b + 1)
        if wait_free is not None:
            v.wait_ge(*wait_free)
        for t in range(TC):
            last = nc.vector.tensor_scalar(self.xn[:, t * P:(t + 1) * P], self.x[:, bass.ds(b * T + t * P, P)],
                                           self.mean[:, t:t + 1], self.rstd[:, t:t + 1], ALU.subtract, ALU.mult)
        last.then_inc(self.normed, 1)

    def on_pool(self, pool, b):
        pool.wait_ge(self.variance_ready, b + 1)
        self.nc.gpsimd.tensor_tensor(self.rstd[:], self.var_eps[:], self.minus_half[:, 0:TC],
                                     ALU.pow).then_inc(self.rstd_ready, 1)


def rwkv_phase(nc, x, ident, minus_half, rest_loaded, started, loads):
    J = HD
    HALF = P // 2
    ORDER = [0, 2, 4, 6, 1, 3, 5, 7]
    PROD, BY_ACT, BY_DVE = 9, 6, 3
    STEPS = 6
    with ExitStack() as ctx:
        def sb(name, shape, dt=F32):
            return ctx.enter_context(nc.sbuf_tensor(f"rwkv_{name}", shape, dt))

        def ps(name, shape=(P, T), dt=F32):
            return ctx.enter_context(nc.psum_tensor(f"rwkv_{name}", list(shape), dt))

        def sem(name):
            return ctx.enter_context(nc.semaphore(f"rwkv_{name}"))

        W_LORA1, W_LORA2, W_DECAY1, W_DECAY2 = 0, 160, 800, 864
        W_K, W_VA, W_VB, W_R, W_G, W_O, W_ALL = 992, 1120, 1248, 1376, 1504, 1632, 1760
        w, col, sel, spread_f32 = loads.tiles
        MAA_X, MAA, DECAY, U, GAMMA, BETA = 0, 1, 6, 7, 8, 9
        SUM_HEAD, MEAN_HEAD = 64, 64 + P
        spread = sb("spread", [P, 4 * P], F32R)
        eps_col = sb("eps_col", [P, 1])
        norm = Norm(nc, sb, sem, x, minus_half, started)
        xT = sb("xT", [P, T + 1])
        xx = sb("xx", [P, T])
        xxx = sb("xxx", [P, T])
        lora = sb("lora", [P, T])
        lora_g = sb("lora_g", [32, T])
        mixed = sb("mixed", [P, 2, T])
        xf = sb("xf", [P, 2, T])
        decay_hidden = sb("decay_hidden", [64, T])
        exp_w = sb("exp_w", [P, T])
        tanh_g = sb("tanh_g", [P, T])
        decay = sb("decay", [P, 2, T])
        key = sb("key", [P, 2, T])
        recept = sb("recept", [P, 2, T])
        v_rows = sb("v_rows", [P, 2, T])
        v_a = sb("v_a", [P, 2, T], F32R)
        v_b = sb("v_b", [P, 2, T], F32R)
        gate = sb("gate", [P, 2, T])
        ruk = sb("ruk", [P, T])
        kv = sb("kv", [P, 2, T])
        state = sb("state", [P, J, T + 1])
        rs = sb("rs", [P, J, T])
        y = sb("y", [P, T])
        bonus = sb("bonus", [P, T])
        centred = sb("centred", [P, T])
        square = sb("square", [P, T])
        log_var = sb("log_var", [P, T])
        inv_std = sb("inv_std", [P, T])
        z = sb("z", [P, T])

        ps_t, ps_v, ps_y, ps_s = ps("ps_t"), ps("ps_v"), ps("ps_y"), ps("ps_s")
        ps_m = [ps("ps_m0"), ps("ps_m1")]
        ps_p = [ps("ps_p0"), ps("ps_p1")]

        prepared = sem("prepared")
        turned = sem("turned")
        xT_ready = sem("xT_ready")
        xx_ready = sem("xx_ready")
        mix_done = sem("mix_done")
        mixed_ready = sem("mixed_ready")
        xf_ready = sem("xf_ready")
        prod_done = sem("prod_done")
        act_free = sem("act_free")
        dve_free = sem("dve_free")
        decay_order = sem("decay_order")
        v_high = sem("v_high")
        tanh_g_ready = sem("tanh_g_ready")
        vj_done = sem("vj_done")
        kv_ready = sem("kv_ready")
        state_ready = sem("state_ready")
        rs_ready = sem("rs_ready")
        ruk_ready = sem("ruk_ready")
        sum_done = sem("sum_done")
        s_done = sem("s_done")
        y_order = sem("y_order")
        square_ready = sem("square_ready")
        log_order = sem("log_order")
        inv_ready = sem("inv_ready")
        added = sem("added")

        block = ctx.enter_context(nc.Block())

        @block.tensor
        def _(pe):
            mm = nc.tensor.matmul
            loads.wait(pe)
            pe.wait_ge(prepared, 1)

            def turn(b):
                pe.wait_ge(norm.normed, b + 1)
                for t in range(TC):
                    last = nc.tensor.transpose(ps_t[:, t * P:(t + 1) * P], norm.xn[:, t * P:(t + 1) * P], ident[:])
                last.then_inc(turned, 1)

            def product(b, s, n, first, start, width, moving):
                out = ps_p[(n + s) % 2]
                if n == 0 and not first:
                    pe.wait_ge(act_free, b * BY_ACT)
                if n == 1 and not first:
                    pe.wait_ge(dve_free, b * BY_DVE)
                if 2 <= n <= 6:
                    pe.wait_ge(act_free, b * BY_ACT + n - 1)
                if n >= 7:
                    pe.wait_ge(dve_free, b * BY_DVE + n - 6)
                mm(out[0:width, :], w[0:moving.shape[0], start:start + width], moving, start=True,
                   stop=True).then_inc(prod_done, 1)

            def mixing(b, s, first):
                pe.wait_ge(xx_ready, (b + 1) * 2)
                product(b, s, 0, first, W_LORA1, P, xxx[:])
                product(b, s, 1, first, W_LORA1 + P, 32, xxx[:])

            def term(b, s, f, first):
                if f == 0:
                    pe.wait_ge(act_free, b * BY_ACT + 2)
                if not (first and f < 2):
                    pe.wait_ge(mixed_ready, b * 5 + f - 1)
                rows = slice(0, 32) if f == 4 else slice(0, P)
                src = lora_g if f == 4 else lora
                mm(ps_m[(f + s) % 2][:], w[rows, W_LORA2 + f * P:W_LORA2 + (f + 1) * P], src[rows, :],
                   start=True, stop=True).then_inc(mix_done, 1)

            def project(b, s, f):
                moving = xf[:, (f + s) % 2, :]
                pe.wait_ge(xf_ready, b * 5 + f + 1)
                if f == 0:
                    product(b, s, 2, False, W_DECAY1, 64, moving)
                if f == 1:
                    product(b, s, 4, False, W_K, P, moving)
                if f == 2:
                    product(b, s, 5, False, W_VA, P, moving)
                    product(b, s, 6, False, W_VB, P, moving)
                if f == 3:
                    product(b, s, 7, False, W_R, P, moving)
                if f == 4:
                    product(b, s, 8, False, W_G, P, moving)

            def decay_second(b, s):
                pe.wait_ge(act_free, b * BY_ACT + 3)
                product(b, s, 3, False, W_DECAY2, P, decay_hidden[:])

            def spread_v(b, s, n, first):
                j = ORDER[n]
                if n == 0:
                    pe.wait_ge(dve_free, b * BY_DVE + 2)
                if not (first and n == 0):
                    pe.wait_ge(kv_ready, b * J + n)
                src = v_a if j < 4 else v_b
                mm(ps_v[:], spread[:, (j % 4) * P:(j % 4 + 1) * P], src[:, s, :], start=True,
                   stop=True).then_inc(vj_done, 1)

            def sum_k(b, half, first):
                pe.wait_ge(rs_ready, b * J + 4 * half + 4)
                if half == 0 and not first:
                    pe.wait_ge(y_order, (b - 1) * STEPS + 2)
                for q in range(4):
                    last = mm(ps_y[32 * q:32 * q + 32, :], sel[:, 32 * half:32 * half + 32],
                              rs[:, 4 * half + q, :], start=(half == 0), stop=(half == 1))
                last.then_inc(sum_done, 1)

            def sum_ruk(b, first):
                pe.wait_ge(ruk_ready, b + 1)
                if not first:
                    pe.wait_ge(added, b)
                mm(ps_s[:], sel[:, SUM_HEAD:SUM_HEAD + P], ruk[:], start=True, stop=True).then_inc(s_done, 1)

            def mean(b):
                pe.wait_ge(y_order, b * STEPS + 2)
                mm(ps_s[:], sel[:, MEAN_HEAD:MEAN_HEAD + P], y[:], start=True, stop=True).then_inc(s_done, 1)

            def variance(b):
                pe.wait_ge(square_ready, b + 1)
                mm(ps_s[:], sel[:, MEAN_HEAD:MEAN_HEAD + P], square[:], start=True, stop=True).then_inc(s_done, 1)

            def output(b):
                pe.wait_ge(y_order, b * STEPS + 6)
                for t in range(TC):
                    last = mm(ps_s[:, t * P:(t + 1) * P], z[:, t * P:(t + 1) * P], w[:, W_O:W_O + P],
                              start=True, stop=True)
                last.then_inc(s_done, 1)

            def front(b, s, slot, first=False):
                if slot == 0:
                    turn(b)
                if slot == 1:
                    mixing(b, s, first)
                if 2 <= slot < 7:
                    term(b, s, slot - 2, first)
                if slot == 4:
                    decay_second(b, s)
                if slot >= 3:
                    project(b, s, slot - 3)

            def tail(b, slot):
                if slot == 1:
                    mean(b)
                if slot == 2:
                    variance(b)
                if slot == 4:
                    output(b)

            def chunk(b, s, first=False, late=False, last=False):
                spread_v(b, s, 0, first)
                for n in range(J):
                    if not first and n < 2:
                        tail(b - 1, n)
                    if not last:
                        front(b + 1, 1 - s, n)
                    if not first and n == 0:
                        sum_k(b - 1, 1, False)
                    if not first and n >= 2:
                        tail(b - 1, n)
                    if n + 1 < J:
                        spread_v(b, s, n + 1, first)
                    if n == 5:
                        sum_k(b, 0, first)
                        sum_ruk(b, first)

            for slot in range(J):
                front(0, 0, slot, first=True)
            chunk(0, 0, first=True)
            with pe.Fori(0, NB // 2 - 2) as i:
                chunk(i * 2 + 1, 1)
                chunk(i * 2 + 2, 0)
            chunk(NB - 3, 1)
            chunk(NB - 2, 0, late=True)
            chunk(NB - 1, 1, last=True)
            sum_k(NB - 1, 1, False)
            for slot in range(J):
                tail(NB - 1, slot)

        @block.scalar
        def _(act):
            fn = nc.scalar.activation
            loads.wait(act)

            def wait(semaphore, value):
                act.wait_ge(semaphore, value)

            def front(b, s, slot, first=False):
                p = lambda n: ps_p[(n + s) % 2]
                if slot == 0:
                    if not first:
                        wait(xf_ready, b * 5)
                    wait(turned, b + 1)
                    fn(xT[:, 1:T + 1], ps_t[:], ACT.Copy).then_inc(xT_ready, 1)
                if slot == 1:
                    wait(prod_done, b * PROD + 1)
                    fn(lora[:], p(0)[:], ACT.Tanh).then_inc(act_free, 1)
                    wait(prod_done, b * PROD + 2)
                    fn(lora_g[:], p(1)[0:32, :], ACT.Tanh).then_inc(act_free, 1)
                if slot == 3:
                    wait(prod_done, b * PROD + 3)
                    fn(decay_hidden[:], p(2)[0:64, :], ACT.Tanh).then_inc(act_free, 1)
                if slot == 4:
                    wait(prod_done, b * PROD + 4)
                    fn(exp_w[:], p(3)[:], ACT.Exp, bias=col[:, DECAY:DECAY + 1]).then_inc(act_free, 1)
                    wait(act_free, b * BY_ACT + 4)
                    fn(decay[:, s, :], exp_w[:], ACT.Exp, scale=-1.0).then_inc(decay_order, 1)
                    wait(prod_done, b * PROD + 5)
                    fn(key[:, s, :], p(4)[:], ACT.Copy).then_inc(act_free, 1)
                if slot == 5:
                    wait(prod_done, b * PROD + 6)
                    fn(v_a[:, s, :], p(5)[:], ACT.Copy)
                    fn(v_rows[0:HALF, s, :], p(5)[0:HALF, :], ACT.Copy).then_inc(v_high, 1)
                    wait(prod_done, b * PROD + 7)
                    fn(v_b[:, s, :], p(6)[:], ACT.Copy)
                    fn(v_rows[HALF:P, s, :], p(6)[HALF:P, :], ACT.Copy).then_inc(v_high, 1)
                if slot == 6:
                    wait(prod_done, b * PROD + 8)
                    fn(recept[:, s, :], p(7)[:], ACT.Copy).then_inc(act_free, 1)
                if slot == 7:
                    wait(prod_done, b * PROD + 9)
                    fn(tanh_g[:], p(8)[:], ACT.Tanh, scale=0.5).then_inc(tanh_g_ready, 1)

            def tail(b, slot):
                if slot == 1:
                    wait(y_order, b * STEPS + 3)
                    fn(square[:], centred[:], ACT.Square).then_inc(square_ready, 1)
                if slot == 2:
                    wait(s_done, b * 4 + 3)
                    fn(log_var[:], ps_s[:], ACT.Ln, bias=eps_col[:]).then_inc(log_order, 1)
                    wait(log_order, b + 1)
                    fn(inv_std[:], log_var[:], ACT.Exp, scale=-0.5).then_inc(inv_ready, 1)

            def chunk(b, s, first=False, late=False, last=False):
                for n in range(J):
                    if not last:
                        front(b + 1, 1 - s, n)
                    if not first:
                        tail(b - 1, n)

            for slot in range(J):
                front(0, 0, slot, first=True)
            chunk(0, 0, first=True)
            with act.Fori(0, NB // 2 - 2) as i:
                chunk(i * 2 + 1, 1)
                chunk(i * 2 + 2, 0)
            chunk(NB - 3, 1)
            chunk(NB - 2, 0, late=True)
            chunk(NB - 1, 1, last=True)
            for slot in range(J):
                tail(NB - 1, slot)

        @block.gpsimd
        def _(pool):
            tt = nc.gpsimd.tensor_tensor

            def front(b, s, slot, first=False):
                if 2 <= slot < 7:
                    f = slot - 2
                    pool.wait_ge(mixed_ready, b * 5 + f + 1)
                    if not (first and f < 2):
                        done = {0: -1, 1: 0, 2: 3, 3: 5, 4: 7}[f]
                        pool.wait_ge(prod_done, b * PROD + done)
                    tt(xf[:, (f + s) % 2, :], mixed[:, (f + s) % 2, :], xT[:, 1:T + 1], ALU.add).then_inc(xf_ready, 1)

            def weigh(b, s, n, first):
                pool.wait_ge(state_ready, b * J + n + 1)
                if not first:
                    pool.wait_ge(sum_done, b * 2 - 1 if n < 4 else b * 2)
                tt(rs[:, n, :], recept[:, s, :], state[:, n, 0:T], ALU.mult).then_inc(rs_ready, 1)

            def chunk(b, s, first=False, late=False, last=False):
                for n in range(J):
                    weigh(b, s, n, first)
                    if not last:
                        front(b + 1, 1 - s, n)
                    if n == 5 and not (late or last):
                        norm.on_pool(pool, b + 2)

            norm.on_pool(pool, 0)
            norm.on_pool(pool, 1)
            for slot in range(J):
                front(0, 0, slot, first=True)
            chunk(0, 0, first=True)
            with pool.Fori(0, NB // 2 - 2) as i:
                chunk(i * 2 + 1, 1)
                chunk(i * 2 + 2, 0)
            chunk(NB - 3, 1)
            chunk(NB - 2, 0, late=True)
            chunk(NB - 1, 1, last=True)

        @block.vector
        def _(v):
            tt, ts, stt = nc.vector.tensor_tensor, nc.vector.tensor_scalar, nc.vector.scalar_tensor_tensor
            nc.vector.memset(xT[:, 0:1], 0.0)
            nc.vector.memset(state[:, :, 0:1], 0.0)
            nc.vector.memset(eps_col[:], GN_EPS)
            norm.on_vector(v, 0)
            loads.wait(v)
            nc.vector.tensor_copy(spread[:], spread_f32[:]).then_inc(prepared, 1)

            def front(b, s, slot, first=False):
                p = lambda n: ps_p[(n + s) % 2]
                if slot == 0:
                    v.wait_ge(xT_ready, b + 1)
                    tt(xx[:], xT[:, 0:T], xT[:, 1:T + 1], ALU.subtract).then_inc(xx_ready, 1)
                    v.wait_ge(xx_ready, b * 2 + 1)
                    stt(xxx[:], xx[:], col[:, MAA_X:MAA_X + 1], xT[:, 1:T + 1], ALU.mult, ALU.add).then_inc(xx_ready, 1)
                if 2 <= slot < 7:
                    f = slot - 2
                    v.wait_ge(mix_done, b * 5 + f + 1)
                    if not (first and f < 2):
                        v.wait_ge(xf_ready, b * 5 + f - 1)
                    stt(mixed[:, (f + s) % 2, :], ps_m[(f + s) % 2][:], col[:, MAA + f:MAA + f + 1], xx[:],
                        ALU.add, ALU.mult).then_inc(mixed_ready, 1)
                if slot == 6:
                    for n, part, low in ((0, v_a, slice(HALF, P)), (1, v_b, slice(0, HALF))):
                        v.wait_ge(v_high, b * 2 + n + 1)
                        tt(part[low, s, :], p(5 + n)[low, :], part[low, s, :].bitcast(F32),
                           ALU.subtract).then_inc(dve_free, 1)
                if slot == 7:
                    v.wait_ge(dve_free, b * BY_DVE + 2)
                    v.wait_ge(tanh_g_ready, b + 1)
                    stt(gate[:, s, :], tanh_g[:], 1.0, p(8)[:], ALU.add, ALU.mult).then_inc(dve_free, 1)

            def tail(b, s, slot):
                o = b * STEPS
                if slot == 0:
                    v.wait_ge(s_done, b * 4 + 1)
                    tt(bonus[:], v_rows[:, s, :], ps_s[:], ALU.mult).then_inc(y_order, 1)
                    v.wait_ge(y_order, o + 1)
                    v.wait_ge(sum_done, b * 2 + 2)
                    tt(y[:], ps_y[:], bonus[:], ALU.add).then_inc(y_order, 1)
                if slot == 1:
                    v.wait_ge(s_done, b * 4 + 2)
                    tt(centred[:], y[:], ps_s[:], ALU.subtract).then_inc(y_order, 1)
                if slot == 3:
                    v.wait_ge(inv_ready, b + 1)
                    tt(z[:], centred[:], inv_std[:], ALU.mult).then_inc(y_order, 1)
                    v.wait_ge(y_order, o + 4)
                    ts(z[:], z[:], col[:, GAMMA:GAMMA + 1], col[:, BETA:BETA + 1], ALU.mult, ALU.add).then_inc(y_order, 1)
                    v.wait_ge(y_order, o + 5)
                    stt(z[:], z[:], 0.5, gate[:, s, :], ALU.mult, ALU.mult).then_inc(y_order, 1)
                if slot == 5:
                    v.wait_ge(s_done, b * 4 + 4)
                    v.wait_ge(y_order, o + 6)
                    rows = x[:, bass.ds(b * T, T)]
                    tt(rows, rows, ps_s[:], ALU.add).then_inc(added, 1)

            def advance(b, s, n, first):
                v.wait_ge(vj_done, b * J + n + 1)
                if n == 0:
                    v.wait_ge(act_free, (b + 1) * BY_ACT)
                    v.wait_ge(decay_order, b + 1)
                tt(kv[:, n % 2, :], key[:, s, :], ps_v[:], ALU.mult).then_inc(kv_ready, 1)

            def scan(b, s, n, first):
                v.wait_ge(kv_ready, b * J + n + 1)
                if not first:
                    v.wait_ge(rs_ready, (b - 1) * J + n + 1)
                nc.vector.tensor_tensor_scan(state[:, n, 1:T + 1], decay[:, s, :], kv[:, n % 2, :], 0.0,
                                             ALU.mult, ALU.add).then_inc(state_ready, 1)

            def chunk(b, s, first=False, late=False, last=False):
                for n in range(J):
                    advance(b, s, n, first)
                    if n == 1:
                        if not first:
                            v.wait_ge(s_done, b * 4 - 3)
                        stt(ruk[:], recept[:, s, :], col[:, U:U + 1], key[:, s, :], ALU.mult,
                            ALU.mult).then_inc(ruk_ready, 1)
                    scan(b, s, n, first)
                    if not first and n < 2:
                        tail(b - 1, 1 - s, n)
                    if not last:
                        front(b + 1, 1 - s, n)
                    if not first and n >= 2:
                        tail(b - 1, 1 - s, n)
                    if n == 4 and not (late or last):
                        norm.statistics(v, b + 2)
                    if n == 7 and not (late or last):
                        norm.scale(v, b + 2)

            norm.on_vector(v, 1, (turned, 1))
            for slot in range(J):
                front(0, 0, slot, first=True)
            v.wait_ge(rest_loaded, 32)
            chunk(0, 0, first=True)
            with v.Fori(0, NB // 2 - 2) as i:
                chunk(i * 2 + 1, 1)
                chunk(i * 2 + 2, 0)
            chunk(NB - 3, 1)
            chunk(NB - 2, 0, late=True)
            chunk(NB - 1, 1, last=True)
            for slot in range(J):
                tail(NB - 1, 1, slot)


def attention_phase(nc, x, ident, minus_half, started, loads):
    UH = H // 2
    FR = 24
    ROWS = 3 * FR
    PIECES = 12
    SCALE = HD ** -0.5
    WIDTH = [2 * P, 2 * P, 3 * P, 4 * P]
    GROUPS = ((0, 1), (2,), (3,))
    NG = len(GROUPS)
    PLACE = {0: (0, 4 * P), 1: (4 * P, 3 * P), 3: (7 * P, P), 2: (8 * P, 2 * P)}
    PT = 10 * P
    FRONT = ["turn", "q", "k", "qp", "kp", "msq", "msk"]
    NEXT = ["v", "M0a"]
    BEFORE = ["E3", "FT", "FW"]
    MID = ["v", "M0b", "E3", "FT", "M1a", "FW", "E0", "turn", "q", "M1b", "k", "qp", "E1", "kp",
           "M0a", "E2", "msq", "msk"]
    ORDERS = {
        "start": FRONT[:5] + ["v"] + FRONT[5:],
        "start1": FRONT,
        "start2": ["M0a"],
        "first": [n for n in MID if n not in BEFORE],
        "mid": MID,
        "late": [n for n in MID if n not in FRONT],
        "last": [n for n in MID if n not in FRONT + NEXT],
        "end": BEFORE,
    }
    n_of = {kind: len(order) for kind, order in ORDERS.items()}
    n_begin = n_of["start"] + n_of["start1"] + n_of["start2"]

    def turn_of(kind, b, name):
        place = ORDERS[kind].index(name)
        if kind in ("start", "start1", "start2"):
            return place + {"start": 0, "start1": n_of["start"], "start2": n_of["start"] + n_of["start1"]}[kind]
        if kind == "first":
            return n_begin + place
        if kind in ("mid", "late"):
            return (b - 1) * len(MID) + n_begin + n_of["first"] + place
        before_last = n_begin + n_of["first"] + (NB - 3) * len(MID) + n_of["late"]
        return before_last + place + (n_of["last"] if kind == "end" else 0)

    with ExitStack() as ctx:
        def sb(name, shape, dt=F32):
            return ctx.enter_context(nc.sbuf_tensor(f"attn_{name}", shape, dt))

        def ps(name, shape, dt=F32):
            return ctx.enter_context(nc.psum_tensor(f"attn_{name}", list(shape), dt))

        def sem(name):
            return ctx.enter_context(nc.semaphore(f"attn_{name}"))

        scratch = [[nc.dram_tensor(f"attn_scratch{s}{side}", (6, HD, H, T), F32, kind="Internal").ap()
                    for side in range(2)] for s in range(2)]
        w, mean_head, mask_f32, col = loads.tiles
        W_Q, W_K, W_QP, W_KP, W_V, W_O = (n * P for n in range(6))
        mask = sb("mask", [P, P], BF16)
        ident_b = sb("ident_b", [P, P], BF16)
        norm = Norm(nc, sb, sem, x, minus_half, started)
        xT = sb("xT", [P, T])
        value = [sb(f"value{s}", [P, 3, T]) for s in range(2)]
        parts = [sb(f"parts{s}", [P, 6, T], F32R) for s in range(2)]
        amp = [sb(f"amp{s}", [P, T]) for s in range(2)]
        tmp = [sb(f"tmp{s}", [P, T]) for s in range(2)]
        stack = [[sb(f"stack{s}{q}", [ROWS + 2, UH, T], F32R) for q in range(2)] for s in range(2)]
        v_ones = sb("v_ones", [P, 2, TC, H, 32])
        probs = sb("probs", [P, 2, 4, PT])
        maxima = sb("maxima", [P, TC, UH])
        neg_max = [sb(f"neg_max{half}", [4, 2, T], F32R) for half in range(2)]
        o_rows = sb("o_rows", [P, T])
        inv = sb("inv", [P, TC * 4])
        o_norm = sb("o_norm", [P, TC, C])
        oT = sb("oT", [P, T])

        ps_h = [ps(f"ps_h{s}", [P, 2 * T]) for s in range(2)]
        ps_g = [ps(f"ps_g{s}", [P, T]) for s in range(2)]
        ps_o = ps("ps_o", [P, T])
        ps_f = ps("ps_f", [P, T])

        prepared, lambda_ready = sem("prepared"), sem("lambda_ready")
        filled = sem("filled")
        f_done = sem("f_done")
        f_free = sem("f_free")
        act_feature = sem("act_feature")
        dve_feature = sem("dve_feature")
        pool_feature = sem("pool_feature")
        kept = sem("kept")
        stacked = [[sem(f"stacked{q}{half}") for half in range(2)] for q in range(2)]
        neg_max_high = sem("neg_max_high")
        neg_max_landed = [sem("neg_max_landed0"), sem("neg_max_landed1")]
        g_done = sem("g_done")
        g_free = sem("g_free")
        h_done = sem("h_done")
        exp_done = sem("exp_done")
        masked = sem("masked")
        av_done = sem("av_done")
        o_ready = sem("o_ready")
        inv_ready = sem("inv_ready")
        pool_passed, sp_passed = sem("pool_passed"), sem("sp_passed")
        NA, NV, NP = 14, 10, 8
        KEPT = 12 * 16
        STACK = 6 * 16

        block = ctx.enter_context(nc.Block())

        def keep_parts(sp, s):
            for side in range(2):
                for part in range(6):
                    sp.dma_start(scratch[s][side][part].rearrange("d h t -> h d t"),
                                 parts[side][:, part, :].bitcast(F32)).then_inc(kept, 16)

        def stack_heads(sp, s, q, half):
            for side in range(2):
                for a, low in enumerate(((0, 0, 1), (0, 1, 0))[side]):
                    sp.dma_start(stack[side][q][FR * a:FR * (a + 1), 4 * half:4 * half + 4, :].bitcast(F32),
                                 scratch[s][side].rearrange("x d h t -> (x d) h t")[
                                     FR * low:FR * (low + 1), q * UH + 4 * half:q * UH + 4 * half + 4, :]).then_inc(
                                         stacked[q][half], 16)

        @block.sync
        def _(sp):
            sp.wait_ge(dve_feature, NV)
            sp.wait_ge(pool_feature, NP)
            keep_parts(sp, 0)
            sp.wait_ge(kept, KEPT)
            sp.wait_ge(filled, 4)
            for q in range(2):
                for half in range(2):
                    stack_heads(sp, 0, q, half)

            def body(b, s):
                wait_apart(sp, dve_feature, (b + 2) * NV, sp_passed)
                wait_apart(sp, pool_feature, (b + 2) * NP, sp_passed)
                for q in range(2):
                    for half in range(2):
                        wait_apart(sp, stacked[q][half], (b + 1) * STACK, sp_passed)
                keep_parts(sp, 1 - s)
                wait_apart(sp, kept, (b + 2) * KEPT, sp_passed)
                for q in range(2):
                    for half in range(2):
                        wait_apart(sp, h_done, (b * 2 + q) * PIECES + 6 * half + 6, sp_passed)
                        stack_heads(sp, 1 - s, q, half)

            body(0, 0)
            with sp.Fori(0, NB // 2 - 1) as i:
                body(i * 2 + 1, 1)
                body(i * 2 + 2, 0)

        @block.tensor
        def _(pe):
            mm = nc.tensor.matmul
            loads.wait(pe)
            pe.wait_ge(prepared, 1)

            def use(kind, b, name):
                n = turn_of(kind, b, name)
                if not isinstance(n, int) or n > 0:
                    pe.wait_ge(f_free, n)

            def front(kind, b, name):
                use(kind, b - 1 if name == "v" else b - 2, name)
                if name == "turn":
                    pe.wait_ge(norm.normed, b + 1)
                    for t in range(TC):
                        last = nc.tensor.transpose(ps_f[:, t * P:(t + 1) * P], norm.xn[:, t * P:(t + 1) * P], ident[:])
                elif name == "v":
                    for t in range(TC):
                        last = mm(ps_f[:, t * P:(t + 1) * P], xT[:, t * P:(t + 1) * P], w[:, W_V:W_V + P],
                                  start=True, stop=True)
                elif name in ("msq", "msk"):
                    s = name == "msk"
                    pe.wait_ge(pool_feature, b * NP + 1 + s)
                    last = mm(ps_f[:], mean_head[:], tmp[s][:], start=True, stop=True)
                else:
                    at = {"q": W_Q, "k": W_K, "qp": W_QP, "kp": W_KP}[name]
                    last = mm(ps_f[:], w[:, at:at + P], xT[:], start=True, stop=True)
                last.then_inc(f_done, 1)

            def scores_for_maximum(b, q, n, first):
                u, h = b * 2 + q, n // NG
                if n % (4 * NG) == 0:
                    pe.wait_ge(stacked[q][h // 4], (b + 1) * STACK)
                if not (first and n < 2):
                    pe.wait_ge(g_free, u * UH * NG + n - 1)
                for place, t in enumerate(GROUPS[n % NG]):
                    at, width = place * 2 * P, WIDTH[t]
                    out = ps_g[n % 2]
                    mm(out[:, at:at + width], stack[0][q][0:ROWS, h, t * P:(t + 1) * P],
                       stack[1][q][0:ROWS, h, 0:width], start=True, stop=False)
                    last = mm(out[:, at + t * P:at + (t + 1) * P], ident_b[:], mask[:], start=False, stop=True)
                last.then_inc(g_done, 1)

            def turn_maxima(kind, b, name, u):
                half = name.endswith("b")
                pe.wait_ge(g_free, u * UH * NG + (half + 1) * 4 * NG)
                use(kind, b, name)
                for t in range(TC):
                    last = mm(ps_f[0:4, t * P:(t + 1) * P], maxima[:, t, 4 * half:4 * half + 4], ident[:],
                              start=True, stop=True)
                last.then_inc(f_done, 1)

            def scores(b, q, p, piece, first):
                u = b * 2 + q
                if p % 2 == 0 and piece == 0:
                    pe.wait_ge(neg_max_landed[p // 2], (u + 1) * 32)

                def tile(out, h, j):
                    return mm(out, stack[1][q][0:ROWS + 2, h, j * P:(j + 1) * P],
                              stack[0][q][0:ROWS + 2, h, j * P:T], start=True, stop=True)

                n = 3 * p + piece
                if not (first and n < 2):
                    pe.wait_ge(exp_done, u * PIECES + n - 1)
                out = ps_h[n % 2]
                if piece < 2:
                    h = 2 * p + piece
                    for j in (0, 1, 3):
                        at, width = PLACE[j]
                        last = tile(out[:, at:at + width], h, j)
                else:
                    for h in (2 * p, 2 * p + 1):
                        at = (h % 2) * 2 * P
                        last = tile(out[:, at:at + 2 * P], h, 2)
                last.then_inc(h_done, 1)

            def weigh_values(b, s, g, first, tiles):
                if tiles[0] == 0:
                    pe.wait_ge(masked, b * 4 + g + 1)
                    if not first or g:
                        pe.wait_ge(o_ready, b * 4 + g)
                for j in tiles:
                    at, width = PLACE[j]
                    for hh in range(4):
                        last = mm(ps_o[32 * hh:32 * hh + 32, j * P:T], v_ones[:, s, j, 4 * g + hh, :],
                                  probs[:, g % 2, hh, at:at + width], start=(j == 0), stop=(j == TC - 1))
                if tiles[-1] == TC - 1:
                    last.then_inc(av_done, 1)

            def turn_output(kind, b, name, of):
                pe.wait_ge(o_ready, of)
                use(kind, b, name)
                for t in range(TC):
                    last = nc.tensor.transpose(ps_f[:, t * P:(t + 1) * P], o_rows[:, t * P:(t + 1) * P], ident[:])
                last.then_inc(f_done, 1)

            def final(kind, b, name):
                use(kind, b, name)
                for t in range(TC):
                    if name == "FT":
                        last = nc.tensor.transpose(ps_f[:, t * P:(t + 1) * P], o_norm[:, t, :], ident[:])
                    else:
                        last = mm(ps_f[:, t * P:(t + 1) * P], oT[:, t * P:(t + 1) * P], w[:, W_O:W_O + P],
                                  start=True, stop=True)
                last.then_inc(f_done, 1)

            def between(kind, b, s, here):
                first, last = kind == "first", kind == "last"
                ahead = kind not in ("late", "last")
                q, p, piece = here
                if p % 2 == 0 and piece > 0 and not (first and here[:2] == (0, 0)):
                    tiles = (0,) if piece == 1 else (1, 2, 3)
                    if here[:2] == (0, 0):
                        weigh_values(b - 1, 1 - s, 3, False, tiles)
                    else:
                        weigh_values(b, s, 2 * q + p // 2 - 1, first, tiles)
                if here == (0, 0, 2) and not last:
                    front(kind, b + 1, "v")
                if here == (0, 1, 0):
                    turn_maxima(kind, b, "M0b", b * 2)
                if here == (0, 1, 1) and not first:
                    turn_output(kind, b, "E3", b * 4)
                if here == (0, 2, 0) and not first:
                    final(kind, b, "FT")
                if here == (0, 2, 1):
                    turn_maxima(kind, b, "M1a", b * 2 + 1)
                if here == (0, 2, 2) and not first:
                    final(kind, b, "FW")
                if here == (0, 3, 1):
                    turn_output(kind, b, "E0", b * 4 + 1)
                if here == (0, 3, 2) and ahead:
                    front(kind, b + 2, "turn")
                if here == (1, 0, 0) and ahead:
                    front(kind, b + 2, "q")
                if here == (1, 0, 1):
                    turn_maxima(kind, b, "M1b", b * 2 + 1)
                if here == (1, 0, 2) and ahead:
                    front(kind, b + 2, "k")
                if here == (1, 1, 0) and ahead:
                    front(kind, b + 2, "qp")
                if here == (1, 1, 1):
                    turn_output(kind, b, "E1", b * 4 + 2)
                if here == (1, 1, 2) and ahead:
                    front(kind, b + 2, "kp")
                if here == (1, 2, 1) and not last:
                    turn_maxima(kind, b, "M0a", b * 2 + 2)
                if here == (1, 3, 1):
                    turn_output(kind, b, "E2", b * 4 + 3)
                if here == (1, 3, 1) and ahead:
                    front(kind, b + 2, "msq")
                if here == (1, 3, 2) and ahead:
                    front(kind, b + 2, "msk")

            def body(kind, b, s):
                for q in range(2):
                    for p in range(4):
                        for piece in range(3):
                            scores(b, q, p, piece, kind == "first" and q == 0)
                            if not (kind == "last" and q == 1):
                                at = 2 * (3 * p + piece)
                                for n in (at, at + 1):
                                    scores_for_maximum(b + q, 1 - q, n, False)
                            between(kind, b, s, (q, p, piece))

            for name in ORDERS["start"]:
                front("start", 0, name)
            for name in ORDERS["start1"]:
                front("start1", 1, name)
            for n in range(UH * NG):
                scores_for_maximum(0, 0, n, True)
                if n == 5 * NG - 1:
                    turn_maxima("start2", 0, "M0a", 0)
            body("first", 0, 0)
            with pe.Fori(0, NB // 2 - 2) as i:
                body("mid", i * 2 + 1, 1)
                body("mid", i * 2 + 2, 0)
            body("mid", NB - 3, 1)
            body("late", NB - 2, 0)
            body("last", NB - 1, 1)
            weigh_values(NB - 1, 1, 3, False, range(TC))
            turn_output("end", 0, "E3", NB * 4)
            final("end", 0, "FT")
            final("end", 0, "FW")

        @block.scalar
        def _(act):
            fn = nc.scalar.activation
            loads.wait(act)
            fn(col[:, 1:2], col[:, 0:1], ACT.Tanh).then_inc(lambda_ready, 1)

            def front(kind, b, s, name):
                got = lambda other: turn_of(kind, b - 1 if other == "v" else b - 2, other) + 1
                base = b * NA
                if name in ("turn", "v", "q", "k", "qp", "kp", "msq", "msk"):
                    act.wait_ge(f_done, got(name))
                if name == "turn":
                    fn(xT[:], ps_f[:], ACT.Copy).then_inc(f_free, 1)
                elif name == "v":
                    fn(v_ones[:, s, :, :, 0:HD].rearrange("p t h d -> p (t h) d"),
                       ps_f[:].rearrange("p (n d) -> p n d", d=HD), ACT.Copy).then_inc(f_free, 1)
                elif name in ("q", "k"):
                    fn(value[name == "k"][:, 0, :], ps_f[:], ACT.Copy).then_inc(f_free, 1)
                elif name in ("qp", "kp"):
                    fn(value[name == "kp"][:, 2, :], ps_f[:], ACT.Copy).then_inc(f_free, 1)
                elif name in ("msq", "msk"):
                    fn(tmp[name == "msk"][:], ps_f[:], ACT.Copy, bias=AMP_EPS).then_inc(f_free, 1)
                elif name == "decay":
                    for s2 in range(2):
                        act.wait_ge(dve_feature, b * NV + 1 + s2)
                        fn(tmp[s2][:], tmp[s2][:], ACT.Exp, scale=-1.0).then_inc(act_feature, 1)
                elif name == "phase":
                    for s2, other in enumerate(("qp", "kp")):
                        act.wait_ge(f_free, got(other))
                        fn(value[s2][:, 2, :], value[s2][:, 2, :], ACT.Tanh).then_inc(act_feature, 1)
                elif name == "softplus":
                    for s2 in range(2):
                        act.wait_ge(act_feature, base + 1 + s2)
                        fn(tmp[s2][:], tmp[s2][:], ACT.Ln, bias=col[:, 2:3]).then_inc(act_feature, 1)
                elif name == "rms":
                    for s2, other in enumerate(("msq", "msk")):
                        act.wait_ge(f_free, got(other))
                        fn(tmp[s2][:], tmp[s2][:], ACT.Ln).then_inc(act_feature, 1)
                elif name == "inverse":
                    for s2 in range(2):
                        act.wait_ge(act_feature, base + 11 + s2)
                        fn(tmp[s2][:], tmp[s2][:], ACT.Exp, scale=-0.5).then_inc(act_feature, 1)
                elif name == "circle":
                    for s2 in range(2):
                        act.wait_ge(dve_feature, b * NV + 3 + s2)
                        fn(value[s2][:, 2, :], value[s2][:, 2, :], ACT.Sin, scale=PI).then_inc(act_feature, 1)
                        fn(value[s2][:, 1, :], value[s2][:, 1, :], ACT.Sin, scale=-PI, bias=col[:, 4:5]).then_inc(act_feature, 1)

            def exponentials(b, q, p, piece, first):
                u = b * 2 + q
                n = 3 * p + piece
                g = 2 * q + p // 2
                if p % 2 == 0 and piece == 0 and not (first and g < 2):
                    act.wait_ge(av_done, b * 4 + g - 1)
                act.wait_ge(h_done, u * PIECES + n + 1)
                out = probs[:, g % 2]
                if piece < 2:
                    fn(out[:, (2 * p + piece) % 4, 0:8 * P], ps_h[n % 2][:], ACT.Exp, scale=SCALE).then_inc(exp_done, 1)
                else:
                    hh = (2 * p) % 4
                    fn(out[:, hh:hh + 2, 8 * P:10 * P], ps_h[n % 2][:, 0:4 * P].rearrange("p (h n) -> p h n", h=2),
                       ACT.Exp, scale=SCALE).then_inc(exp_done, 1)

            def take_output(b, g, before):
                act.wait_ge(av_done, b * 4 + g + 1)
                if before is not None:
                    act.wait_ge(f_done, before + 1)
                fn(o_rows[:], ps_o[:], ACT.Copy).then_inc(o_ready, 1)

            def send_maxima(kind, b, name, u, q):
                half = int(name.endswith("b"))
                act.wait_ge(f_done, turn_of(kind, b, name) + 1)
                if not isinstance(u, int) or u > 0:
                    act.wait_ge(neg_max_landed[half], u * 32)
                fn(neg_max[half][:, 0, :], ps_f[0:4, :], ACT.Copy, scale=-1.0).then_inc(neg_max_high, 1)
                act.wait_ge(f_free, turn_of(kind, b, name) + 1)
                for part in range(2):
                    act.dma_start(stack[0][q][ROWS + part:ROWS + part + 1, 4 * half:4 * half + 4, :].bitcast(F32),
                                  neg_max[half][:, part, :].bitcast(F32)).then_inc(neg_max_landed[half], 16)

            def turned_copy(kind, b):
                act.wait_ge(f_done, turn_of(kind, b, "FT") + 1)
                fn(oT[:], ps_f[:], ACT.Copy).then_inc(f_free, 1)

            def between(kind, b, s, here):
                first, last = kind == "first", kind == "last"
                ahead = kind not in ("late", "last")
                e = lambda name: turn_of(kind, b, name)
                if here == (0, 0, 2) and not last:
                    front(kind, b + 1, 1 - s, "v")
                if here == (0, 1, 0) and not first:
                    take_output(b - 1, 3, e(ORDERS[kind][0]) - (1 if last else 3))
                if here == (0, 1, 0):
                    send_maxima(kind, b, "M0b", b * 2, 0)
                if here == (0, 2, 0) and not first:
                    turned_copy(kind, b)
                if here == (0, 2, 1):
                    send_maxima(kind, b, "M1a", b * 2 + 1, 1)
                if here == (0, 3, 0):
                    take_output(b, 0, None if first else e("E3"))
                if here == (1, 0, 1):
                    send_maxima(kind, b, "M1b", b * 2 + 1, 1)
                if here == (1, 1, 0):
                    take_output(b, 1, e("E0"))
                if here == (1, 2, 1) and not last:
                    send_maxima(kind, b, "M0a", b * 2 + 2, 0)
                if here == (1, 3, 0):
                    take_output(b, 2, e("E1"))
                if ahead:
                    for name in {(0, 3, 2): ("turn",), (1, 0, 0): ("q",), (1, 0, 2): ("k",), (1, 1, 0): ("qp",),
                                 (1, 1, 1): ("decay",), (1, 1, 2): ("kp",), (1, 2, 0): ("phase",),
                                 (1, 2, 1): ("softplus",), (1, 3, 0): ("circle",), (1, 3, 1): ("msq",),
                                 (1, 3, 2): ("msk", "rms", "inverse")}.get(here, ()):
                        front(kind, b + 2, s, name)

            def body(kind, b, s):
                for q in range(2):
                    for p in range(4):
                        for piece in range(3):
                            exponentials(b, q, p, piece, kind == "first")
                            between(kind, b, s, (q, p, piece))

            act.wait_ge(prepared, 1)
            for name in ("turn", "q", "k", "qp", "kp", "v", "decay", "phase", "softplus", "circle", "msq", "msk", "rms",
                         "inverse"):
                front("start", 0, 0, name)
            for name in ("turn", "q", "k", "qp", "kp", "decay", "phase", "softplus", "circle", "msq", "msk", "rms",
                         "inverse"):
                front("start1", 1, 1, name)
            send_maxima("start2", 0, "M0a", 0, 0)
            body("first", 0, 0)
            with act.Fori(0, NB // 2 - 2) as i:
                body("mid", i * 2 + 1, 1)
                body("mid", i * 2 + 2, 0)
            body("mid", NB - 3, 1)
            body("late", NB - 2, 0)
            body("last", NB - 1, 1)
            take_output(NB - 1, 3, turn_of("last", NB - 1, "E2"))
            turned_copy("end", 0)

        @block.gpsimd
        def _(pool):
            tt = nc.gpsimd.tensor_tensor

            def zero_above(b, g, q, p):
                wait_apart(pool, exp_done, (b * 2 + q) * PIECES + 3 * p + 3, pool_passed)
                for j in range(TC):
                    at = PLACE[j][0]
                    tile = probs[:, g % 2, :, at:at + P]
                    last = nc.gpsimd.affine_select(out=tile, in_=tile, compare_op=ALU.is_ge, fill=0.0, base=0,
                                                   pattern=[[0, 4], [1, P]], channel_multiplier=-1)
                last.then_inc(masked, 1)

            def squares(b):
                for s in range(2):
                    pool.wait_ge(dve_feature, b * NV + 5 + s)
                    tt(tmp[s][:], amp[s][:], amp[s][:], ALU.mult).then_inc(pool_feature, 1)

            def products(b):
                for s in range(2):
                    pool.wait_ge(act_feature, b * NA + 8 + 2 * s)
                    pool.wait_ge(dve_feature, b * NV + 7 + s)
                    for n in (1, 2):
                        tt(value[s][:, n, :], value[s][:, n, :], amp[s][:], ALU.mult).then_inc(pool_feature, 1)

            def lows(b):
                for s in range(2):
                    pool.wait_ge(dve_feature, b * NV + 9 + s)
                    tt(parts[s][:, 3:6, :], value[s][:], parts[s][:, 0:3, :].bitcast(F32), ALU.subtract).then_inc(pool_feature, 1)

            def body(kind, b):
                ahead = kind not in ("late", "last")
                for q in range(2):
                    for p in range(4):
                        if q == 0 and p == 0 and kind != "last":
                            products(b + 1)
                            lows(b + 1)
                        if p % 2:
                            zero_above(b, 2 * q + p // 2, q, p)
                        if q == 0 and p == 2 and ahead:
                            norm.on_pool(pool, b + 2)
                        if q == 1 and p == 2 and ahead:
                            squares(b + 2)

            norm.on_pool(pool, 0)
            for s in range(2):
                nc.gpsimd.memset(v_ones[:, s, :, :, HD:HD + 1], 1.0)
                nc.gpsimd.memset(v_ones[:, s, :, :, HD + 1:32], 0.0).then_inc(filled, 1)
                pool.wait_ge(filled, 2 * s + 1)
                nc.gpsimd.memset(stack[1][s][64:ROWS + 2].bitcast(F32), 1.0).then_inc(filled, 1)
                pool.wait_ge(filled, 2 * s + 2)
            squares(0)
            products(0)
            lows(0)
            norm.on_pool(pool, 1)
            squares(1)
            body("first", 0)
            with pool.Fori(0, NB - 3) as i:
                body("mid", i + 1)
            body("late", NB - 2)
            body("last", NB - 1)

        @block.vector
        def _(v):
            tt, ts, stt = nc.vector.tensor_tensor, nc.vector.tensor_scalar, nc.vector.scalar_tensor_tensor
            norm.on_vector(v, 0)
            loads.wait(v)
            v.wait_ge(lambda_ready, 1)
            nc.vector.memset(col[:, 2:3], 1.0)
            nc.vector.memset(col[:, 3:4], AMP_EPS)
            nc.vector.memset(col[:, 4:5], PI / 2)
            ts(col[:, 0:1], col[:, 1:2], LAMBDA_MAX, None, ALU.mult)
            nc.vector.tensor_copy(mask[:], mask_f32[:])
            nc.vector.tensor_copy(ident_b[:], ident[:]).then_inc(prepared, 1)
            v.wait_ge(prepared, 1)

            def front(kind, b, step, first=False):
                got = lambda other: turn_of(kind, b - 2, other) + 1
                if step == "norm":
                    norm.on_vector(v, b)
                if step == "size":
                    for s, name in enumerate(("q", "k")):
                        v.wait_ge(f_free, got(name))
                        stt(tmp[s][:], value[s][:, 0, :], -1.0, value[s][:, 0, :], ALU.mult, ALU.max).then_inc(dve_feature, 1)
                if step == "phase":
                    for s in range(2):
                        v.wait_ge(act_feature, b * NA + 3 + s)
                        stt(value[s][:, 1, :], value[s][:, 2, :], -1.0, value[s][:, 2, :], ALU.mult, ALU.max).then_inc(dve_feature, 1)
                if step == "softplus":
                    for s in range(2):
                        v.wait_ge(act_feature, b * NA + 5 + s)
                        stt(amp[s][:], value[s][:, 0, :], 0.0, tmp[s][:], ALU.max, ALU.add).then_inc(dve_feature, 1)
                if step == "amplitude":
                    for s in range(2):
                        v.wait_ge(act_feature, b * NA + 13 + s)
                        if s == 0:
                            stt(amp[s][:], amp[s][:], col[:, 0:1], tmp[s][:], ALU.mult, ALU.mult).then_inc(dve_feature, 1)
                        else:
                            tt(amp[s][:], amp[s][:], tmp[s][:], ALU.mult).then_inc(dve_feature, 1)
                if step == "high":
                    for s in range(2):
                        v.wait_ge(pool_feature, b * NP + 4 + 2 * s)
                        if not first and s == 0:
                            v.wait_ge(kept, b * KEPT)
                        nc.vector.tensor_copy(parts[s][:, 0:3, :], value[s][:]).then_inc(dve_feature, 1)

            def take_maxima(b, q, n):
                u, h = b * 2 + q, n // NG
                v.wait_ge(g_done, u * UH * NG + n + 1)
                for place, t in enumerate(GROUPS[n % NG]):
                    at = place * 2 * P
                    last = nc.vector.tensor_reduce(maxima[:, t, h:h + 1], ps_g[n % 2][:, at:at + (t + 1) * P], AX_X,
                                                   ALU.max)
                last.then_inc(g_free, 1)

            def low_maxima(name, u):
                half = int(name.endswith("b"))
                v.wait_ge(neg_max_high, u * 2 + half + 1)
                stt(neg_max[half][:, 1, :], ps_f[0:4, :], -1.0, neg_max[half][:, 0, :].bitcast(F32), ALU.mult,
                    ALU.subtract).then_inc(f_free, 1)

            def normalise(kind, b, name, g, count):
                v.wait_ge(f_done, turn_of(kind, b, name) + 1)
                rows = ps_f[:].rearrange("p (n c) -> p n c", c=32)
                nc.vector.reciprocal(inv[:], rows[:, :, HD]).then_inc(inv_ready, 1)
                v.wait_ge(inv_ready, count + 1)
                tt(o_norm[:, :, 4 * g * HD:4 * (g + 1) * HD].rearrange("p t (h d) -> p t h d", d=HD),
                   rows[:, :, 0:HD].rearrange("p (t h) d -> p t h d", t=TC),
                   inv[:].rearrange("p (t h) -> p t h", t=TC).unsqueeze(3).broadcast_to([P, TC, 4, HD]),
                   ALU.mult).then_inc(f_free, 1)

            def add_output(kind, b, of):
                v.wait_ge(f_done, turn_of(kind, b, "FW") + 1)
                rows = x[:, bass.ds(of * T, T)]
                tt(rows, rows, ps_f[:], ALU.add).then_inc(f_free, 1)

            def between(kind, b, here):
                first, last = kind == "first", kind == "last"
                ahead = kind not in ("late", "last")
                if here == (0, 0, 2) and not last:
                    front(kind, b + 1, "amplitude")
                if here == (0, 1, 0):
                    low_maxima("M0b", b * 2)
                if here == (0, 1, 1) and not last:
                    front(kind, b + 1, "high")
                if here == (0, 1, 1) and not first:
                    normalise(kind, b, "E3", 3, b * 4 - 1)
                if here == (0, 1, 2) and ahead:
                    norm.statistics(v, b + 2)
                if here == (0, 2, 1):
                    low_maxima("M1a", b * 2 + 1)
                if here == (0, 2, 2) and not first:
                    add_output(kind, b, b - 1)
                if here == (0, 3, 0) and ahead:
                    norm.scale(v, b + 2)
                if here == (0, 3, 1):
                    normalise(kind, b, "E0", 0, b * 4)
                if here == (1, 0, 1):
                    low_maxima("M1b", b * 2 + 1)
                if here == (1, 1, 0) and ahead:
                    front(kind, b + 2, "size")
                if here == (1, 1, 1):
                    normalise(kind, b, "E1", 1, b * 4 + 1)
                if here == (1, 2, 1) and not last:
                    low_maxima("M0a", b * 2 + 2)
                if here == (1, 2, 1) and ahead:
                    front(kind, b + 2, "phase")
                if here == (1, 3, 0) and ahead:
                    front(kind, b + 2, "softplus")
                if here == (1, 3, 1):
                    normalise(kind, b, "E2", 2, b * 4 + 2)

            def body(kind, b):
                for q in range(2):
                    for p in range(4):
                        for piece in range(3):
                            if not (kind == "last" and q == 1):
                                at = 2 * (3 * p + piece)
                                for n in (at, at + 1):
                                    take_maxima(b + q, 1 - q, n)
                            between(kind, b, (q, p, piece))

            for step in ("size", "phase", "softplus", "amplitude", "high"):
                front("start", 0, step, first=True)
            for step in ("norm", "size", "phase", "softplus"):
                front("start1", 1, step)
            for n in range(UH * NG):
                take_maxima(0, 0, n)
                if n == 5 * NG - 1:
                    low_maxima("M0a", 0)
            body("first", 0)
            with v.Fori(0, NB - 3) as i:
                body("mid", i + 1)
            body("late", NB - 2)
            body("last", NB - 1)
            normalise("end", 0, "E3", 3, NB * 4 - 1)
            add_output("end", 0, NB - 1)


def moe_phase(nc, phase, rows, loads, sources=None):
    x, ident, minus_half, codes, started = rows.x, rows.ident, rows.minus_half, rows.codes, rows.started
    with ExitStack() as ctx:
        def sb(name, shape, dt=F32):
            return ctx.enter_context(nc.sbuf_tensor(f"{phase}_{name}", shape, dt))

        def ps(name, shape=(P, 512), dt=F32):
            return ctx.enter_context(nc.psum_tensor(f"{phase}_{name}", list(shape), dt))

        def sem(name):
            return ctx.enter_context(nc.semaphore(f"{phase}_{name}"))

        router, w1_cols, w2_cols = loads.tiles
        w1_high = sb("w1_high", [P, NE * HC * P], F32R)
        w1_low = sb("w1_low", [P, NE * HC * P], F32R)
        norm = Norm(nc, sb, sem, x, minus_half, started)
        xT = sb("xT", [P, 2, T])
        x_high = sb("x_high", [P, 2, T], F32R)
        x_low = sb("x_low", [P, 2, T], F32R)
        logits = sb("logits", [P, TC, NE])
        code = sb("code", [P, TC, NE])
        first = sb("first", [P, TC, NE])
        second = sb("second", [P, TC, NE])
        rest = sb("rest", [P, TC, NE])
        top = sb("top", [P, 4, TC])
        share = sb("share", [P, 4, TC])
        gate = sb("gate", [P, 2, TC, NE])
        hidden = sb("hidden", [P, 2, HC, T])

        ps_t = ps("ps_t")
        ps_logits = ps("ps_logits")
        ps_h = [[ps(f"ps_h{s}{k}") for k in range(HC)] for s in range(2)]
        ps_y = [ps(f"ps_y{s}") for s in range(2)]

        weights_split = sem("weights_split")
        weight_high = sem("weight_high")
        gate_order = sem("gate_order")
        gate_ready = sem("gate_ready")
        transposed = sem("transposed")
        high_ready = sem("high_ready")
        low_ready = sem("low_ready")
        logits_done = sem("logits_done")
        gap_ready = sem("gap_ready")
        exp_ready = sem("exp_ready")
        hidden_done = sem("hidden_done")
        gelu_done = sem("gelu_done")
        y_done = sem("y_done")
        y_used = sem("y_used")

        block = ctx.enter_context(nc.Block())

        @block.sync
        def _(sp):
            if sources is not None:
                loads.load(sp, *sources)

        @block.gpsimd
        def _(pool):
            with pool.Fori(0, NB) as b:
                norm.on_pool(pool, b)

        @block.tensor
        def _(pe):
            loads.wait(pe)

            def turn(b):
                pe.wait_ge(norm.normed, b + 1)
                for t in range(TC):
                    last = nc.tensor.transpose(ps_t[:, t * P:(t + 1) * P], norm.xn[:, t * P:(t + 1) * P], ident[:])
                last.then_inc(transposed, 1)

            def route(b, s):
                pe.wait_ge(high_ready, b + 1)
                for t in range(TC):
                    last = nc.tensor.matmul(ps_logits[:, t * NE:(t + 1) * NE], xT[:, s, t * P:(t + 1) * P],
                                            router[:], start=True, stop=True)
                last.then_inc(logits_done, 1)

            def up(b, s, e, wait_slot=True):
                if e == 0:
                    pe.wait_ge(low_ready, b + 1)
                for k in range(HC):
                    if wait_slot:
                        pe.wait_ge(gelu_done, (b * NE + e - 2) * HC + k + 1)
                    cols = slice((e * HC + k) * P, (e * HC + k + 1) * P)
                    out = ps_h[e % 2][k]
                    nc.tensor.matmul(out[:], w1_high[:, cols], x_high[:, s, :], start=True, stop=False)
                    nc.tensor.matmul(out[:], w1_high[:, cols], x_low[:, s, :], start=False, stop=False)
                    nc.tensor.matmul(out[:], w1_low[:, cols], x_high[:, s, :], start=False,
                                     stop=True).then_inc(hidden_done, 1)

            def down(b, e, wait_slot=True):
                pe.wait_ge(gelu_done, (b * NE + e + 1) * HC)
                if wait_slot:
                    pe.wait_ge(y_used, b * NE + e - 1)
                for t in range(TC):
                    for k in range(HC):
                        cols = slice((e * HC + k) * P, (e * HC + k + 1) * P)
                        last = nc.tensor.matmul(ps_y[e % 2][:, t * P:(t + 1) * P], hidden[:, e % 2, k, t * P:(t + 1) * P],
                                                w2_cols[:, cols], start=(k == 0), stop=(k == HC - 1))
                last.then_inc(y_done, 1)

            def chunk(b, s, first=False, last=False):
                for e in range(NE):
                    if e + 1 < NE:
                        up(b, s, e + 1, wait_slot=not (first and e + 1 < 2))
                    elif not last:
                        up(b + 1, 1 - s, 0)
                    down(b, e, wait_slot=not (first and e < 2))
                    if e == 4 and not last:
                        turn(b + 1)
                    if e == 5 and not last:
                        route(b + 1, 1 - s)

            turn(0)
            route(0, 0)
            pe.wait_ge(weights_split, 1)
            up(0, 0, 0, wait_slot=False)
            chunk(0, 0, first=True)
            with pe.Fori(0, NB // 2 - 1) as i:
                chunk(i * 2 + 1, 1)
                chunk(i * 2 + 2, 0)
            chunk(NB - 1, 1, last=True)

        @block.scalar
        def _(act):
            def copies(b, s):
                act.wait_ge(transposed, b + 1)
                nc.scalar.copy(xT[:, s, :], ps_t[:])
                nc.scalar.copy(x_high[:, s, :], ps_t[:]).then_inc(high_ready, 1)

            def gap(b):
                act.wait_ge(gap_ready, b + 1)
                nc.scalar.activation(share[:, 0, :], share[:, 3, :], ACT.Exp).then_inc(exp_ready, 1)

            def gelu(b, e, wait_slot=True):
                for k in range(HC):
                    if wait_slot and k == 0:
                        act.wait_ge(y_done, b * NE + e - 1)
                    act.wait_ge(hidden_done, (b * NE + e) * HC + k + 1)
                    nc.scalar.activation(hidden[:, e % 2, k, :], ps_h[e % 2][k][:], ACT.Gelu).then_inc(gelu_done, 1)

            def chunk(b, s, first=False, last=False):
                for e in range(NE):
                    gelu(b, e, wait_slot=not (first and e < 2))
                    if e == 5 and not last:
                        copies(b + 1, 1 - s)
                    if e == 6 and not last:
                        gap(b + 1)

            loads.wait(act)
            nc.scalar.copy(w1_high[:], w1_cols[:]).then_inc(weight_high, 1)
            copies(0, 0)
            gap(0)
            chunk(0, 0, first=True)
            with act.Fori(0, NB // 2 - 1) as i:
                chunk(i * 2 + 1, 1)
                chunk(i * 2 + 2, 0)
            chunk(NB - 1, 1, last=True)

        @block.vector
        def _(v):
            def low(b, s):
                v.wait_ge(high_ready, b + 1)
                nc.vector.tensor_tensor(x_low[:, s, :], ps_t[:], x_high[:, s, :].bitcast(F32),
                                        ALU.subtract).then_inc(low_ready, 1)

            def gates(b, s):
                step = Steps(v, gate_order, b, 16)
                wide = lambda column: column.unsqueeze(2).broadcast_to([P, TC, NE])
                tt, ts, tr = nc.vector.tensor_tensor, nc.vector.tensor_scalar, nc.vector.tensor_reduce
                v.wait_ge(logits_done, b + 1)
                step(nc.vector.tensor_copy(logits[:], ps_logits[:, 0:TC * NE]))
                step(tr(top[:, 0, :], logits[:], AX_X, ALU.max))
                for pick, value, at, left in ((first, 0, 1, logits), (second, 2, 3, rest)):
                    step(tt(pick[:], left[:], wide(top[:, value, :]), ALU.is_equal))
                    step(tt(code[:], pick[:], codes[:].rearrange("p (t e) -> p t e", t=TC), ALU.mult))
                    step(tr(top[:, at, :], code[:], AX_X, ALU.max))
                    step(tt(pick[:], code[:], wide(top[:, at, :]), ALU.is_equal))
                    if pick is first:
                        step(nc.vector.scalar_tensor_tensor(rest[:], first[:], LOWEST, logits[:], ALU.mult, ALU.add))
                        step(tr(top[:, 2, :], rest[:], AX_X, ALU.max))
                tt(share[:, 3, :], top[:, 2, :], top[:, 0, :], ALU.subtract).then_inc(gap_ready, 1)
                v.wait_ge(exp_ready, b + 1)
                step(ts(share[:, 1, :], share[:, 0, :], 1.0, None, ALU.add))
                step(nc.vector.reciprocal(share[:, 1, :], share[:, 1, :]))
                step(tt(share[:, 2, :], share[:, 0, :], share[:, 1, :], ALU.mult))
                tt(first[:], first[:], wide(share[:, 1, :]), ALU.mult)
                step(tt(second[:], second[:], wide(share[:, 2, :]), ALU.mult))
                tt(gate[:, s], first[:], second[:], ALU.add).then_inc(gate_ready, 1)
                step.done()
                v.wait_ge(gate_ready, b + 1)

            def add(b, s, e):
                v.wait_ge(y_done, b * NE + e + 1)
                if e:
                    v.wait_ge(y_used, b * NE + e)
                for t in range(TC):
                    rows = x[:, bass.ds(b * T + t * P, P)]
                    last = nc.vector.scalar_tensor_tensor(rows, ps_y[e % 2][:, t * P:(t + 1) * P],
                                                          gate[:, s, t, e:e + 1], rows, ALU.mult, ALU.add)
                last.then_inc(y_used, 1)

            def chunk(b, s, last=False):
                for e in range(NE):
                    add(b, s, e)
                    if not last:
                        if e == 2:
                            norm.on_vector(v, b + 1, (transposed, b + 1))
                        if e == 4:
                            low(b + 1, 1 - s)
                        if e == 5:
                            gates(b + 1, 1 - s)

            norm.on_vector(v, 0)
            loads.wait(v)
            v.wait_ge(weight_high, 1)
            nc.vector.tensor_tensor(w1_low[:], w1_cols[:], w1_high[:].bitcast(F32),
                                    ALU.subtract).then_inc(weights_split, 1)
            low(0, 0)
            gates(0, 0)
            chunk(0, 0)
            with v.Fori(0, NB // 2 - 1) as i:
                chunk(i * 2 + 1, 1)
                chunk(i * 2 + 2, 0)
            chunk(NB - 1, 1, last=True)


def program(nc, aps, out):
    with ExitStack() as ctx:
        attention = Loaded(nc, ctx, "attention_in", w=[P, 6 * P], mean_head=[P, P], mask=[P, P], columns=[P, 5])
        rows = Rows(nc, ctx)
        with ExitStack() as until_experts:
            experts = Loaded(nc, until_experts, "experts_in", **EXPERT_SHAPES)
            with ExitStack() as until_mixing:
                mixing = Loaded(nc, until_mixing, "mixing_in", w=[P, 1760], columns=[P, 10], sums=[P, 64 + 3 * P],
                                spread=[P, 4 * P])
                load(nc, aps, rows, mixing, experts, attention)
                rwkv_phase(nc, rows.x, rows.ident, rows.minus_half, rows.rest_loaded, rows.started, mixing)
            moe_phase(nc, "moe0", rows, experts)
        attention_phase(nc, rows.x, rows.ident, rows.minus_half, rows.started, attention)
        experts = Loaded(nc, ctx, "experts_again", **EXPERT_SHAPES)
        moe_phase(nc, "moe1", rows, experts, (aps["router"], aps["w1"], aps["w2"]))
        stored = ctx.enter_context(nc.semaphore("stored"))
        with nc.Block() as block:
            @block.sync
            def _(sp):
                sp.dma_start(out, rows.x[:]).then_inc(stored, 16)
                sp.wait_ge(stored, 16)


def kernel(**inputs):
    import concourse.bacc as bacc
    from concourse.bass_utils import run_bass_kernel_spmd

    nc = bacc.Bacc("TRN2", target_bir_lowering=False, num_devices=1)
    arrays = layout(inputs)
    aps = {n: nc.dram_tensor(f"in_{n}", a.shape, F32, kind="ExternalInput").ap() for n, a in arrays.items()}
    out = nc.dram_tensor("out_rows", (P, NT * C), F32, kind="ExternalOutput").ap()
    program(nc, aps, out)
    got = run_bass_kernel_spmd(nc, [{f"in_{n}": a for n, a in arrays.items()}], core_ids=[0])
    rows = got.results[0]["out_rows"]
    return rows.reshape(P, NT, C).transpose(1, 0, 2).reshape(NB, T, C)
```
